# Optimizing a Trainium2 kernel written in Bass

```python
import numpy as np
import jax
import jax.numpy as jnp

def _softmax(x, axis=-1):
    return jax.nn.softmax(x, axis=axis)

def _gelu(x):
    return jax.nn.gelu(x, approximate=True)

def _silu(x):
    return jax.nn.silu(x)

def _sigmoid(x):
    return jax.nn.sigmoid(x)

def _layernorm(x, axis=-1, eps=1e-05):
    m = jnp.mean(x, axis=axis, keepdims=True)
    v = jnp.var(x, axis=axis, keepdims=True)
    return (x - m) / jnp.sqrt(v + eps)

def _scatter_add(tgt, idx, src, axis=0):
    return tgt.at[idx].add(src)

def _segment_sum(src, seg, n):
    return jax.ops.segment_sum(src, seg, n)
kernel_name = 'mk_vit_tower_d1_tok_img1024_r4_b313bd'

def setup_inputs(seed: int=0):
    np.random.seed(seed)
    _w = jnp.asarray

    def _rec_inputs():
        import jax
        import jax.numpy as jnp
        _rk = jax.random.key(seed)
        x = -0.000392918 + 0.999932 * jax.random.normal(jax.random.fold_in(_rk, 1), (16, 256, 256, 1), jnp.float32)
        return x
    x = _rec_inputs()

    def _L0_tok_setup():
        import jax, jax.numpy as jnp
        import numpy as np
        INV_SQRT2 = 0.7071067811865476
        LEVEL = 3

        def _split(x, axis):
            ax = axis % x.ndim
            sl0 = [slice(None)] * x.ndim
            sl0[ax] = slice(0, None, 2)
            sl1 = [slice(None)] * x.ndim
            sl1[ax] = slice(1, None, 2)
            x0, x1 = (x[tuple(sl0)], x[tuple(sl1)])
            return ((x0 + x1) * INV_SQRT2, (x0 - x1) * INV_SQRT2)

        def _merge(lo, hi, axis):
            ax = axis % lo.ndim
            e = (lo + hi) * INV_SQRT2
            o = (lo - hi) * INV_SQRT2
            s = jnp.stack([e, o], axis=ax + 1)
            shape = list(lo.shape)
            shape[ax] *= 2
            return s.reshape(shape)

        def _dwt2(x):
            lo, hi = _split(x, -1)
            a, h = _split(lo, -2)
            v, d = _split(hi, -2)
            return (a, h, v, d)

        def _idwt2(a, h, v, d):
            lo = _merge(a, h, -2)
            hi = _merge(v, d, -2)
            return _merge(lo, hi, -1)
        key = jax.random.key(seed)
        ks = jax.random.split(key, 8)
        B, H, W = (16, 256, 256)
        x = jax.random.normal(ks[0], (B, H, W, 1), dtype=jnp.float32)
        na = H // 8 * (W // 8)
        n2 = H // 4 * (W // 4)
        n1 = H // 2 * (W // 2)
        scale = 0.02
        Wa = jax.random.normal(ks[1], (na, 1), dtype=jnp.float32) * scale
        ba = jnp.zeros((1,), jnp.float32)
        Wd1 = jax.random.normal(ks[2], (3 * na, 3), dtype=jnp.float32) * scale
        bd1 = jnp.zeros((3,), jnp.float32)
        Wd2 = jax.random.normal(ks[3], (3 * n2, 3), dtype=jnp.float32) * scale
        bd2 = jnp.zeros((3,), jnp.float32)
        Wd3 = jax.random.normal(ks[4], (3 * n1, 3), dtype=jnp.float32) * scale
        bd3 = jnp.zeros((3,), jnp.float32)
        return {'x': x, 'Wa': Wa, 'ba': ba, 'Wd1': Wd1, 'bd1': bd1, 'Wd2': Wd2, 'bd2': bd2, 'Wd3': Wd3, 'bd3': bd3}
    _L0_tok_all = _L0_tok_setup()
    _L0_tok_in = {k: v for k, v in _L0_tok_all.items() if k in ('Wa', 'ba', 'Wd1', 'bd1', 'Wd2', 'bd2', 'Wd3', 'bd3')}
    del _L0_tok_all

    def _L0_attn_setup():
        import math
        import jax, jax.numpy as jnp
        import numpy as np
        B, S, E, H = (4, 512, 256, 16)
        HD = E // H
        key = jax.random.key(seed)
        ks = jax.random.split(key, 7)
        scale = 1.0 / math.sqrt(E)
        return {'x': jax.random.normal(ks[0], (B, S, E), dtype=jnp.float32), 'Wq': jax.random.normal(ks[1], (H, HD, E), dtype=jnp.float32) * scale, 'bq': jax.random.normal(ks[2], (H, HD), dtype=jnp.float32) * 0.01, 'Wk': jax.random.normal(ks[3], (H, HD, E), dtype=jnp.float32) * scale, 'bk': jax.random.normal(ks[4], (H, HD), dtype=jnp.float32) * 0.01, 'Wv': jax.random.normal(ks[5], (H, HD, E), dtype=jnp.float32) * scale, 'bv': jax.random.normal(ks[6], (H, HD), dtype=jnp.float32) * 0.01}
    _L0_attn_all = _L0_attn_setup()
    _L0_attn_in = {k: v for k, v in _L0_attn_all.items() if k in ('Wq', 'bq', 'Wk', 'bk', 'Wv', 'bv')}
    del _L0_attn_all

    def _L0_ffn_setup():
        import jax, jax.numpy as jnp
        import numpy as np
        import math
        B, S, D = (4, 512, 256)
        E, DFF = (16, 512)
        CAP_FACTOR = 2.0
        ROUTER_HIDDEN = 128
        CAPACITY = int(math.ceil(S * CAP_FACTOR / E))
        key = jax.random.key(seed)
        ks = jax.random.split(key, 6)

        def uinit(k, shape, fan_in):
            bound = math.sqrt(3.0) * math.sqrt(1.0 / 3.0) / math.sqrt(fan_in)
            return jax.random.uniform(k, shape, jnp.float32, -bound, bound)
        return {'hidden_states': jax.random.normal(ks[0], (B, S, D), jnp.float32), 'router_w1': jax.random.normal(ks[1], (D, ROUTER_HIDDEN), jnp.float32) / math.sqrt(D), 'router_w2': jax.random.normal(ks[2], (ROUTER_HIDDEN, E), jnp.float32) / math.sqrt(ROUTER_HIDDEN), 'w1': uinit(ks[3], (E, D, DFF), D), 'w2': uinit(ks[4], (E, D, DFF), D), 'w3': uinit(ks[5], (E, DFF, D), DFF)}
    _L0_ffn_all = _L0_ffn_setup()
    _L0_ffn_in = {k: v for k, v in _L0_ffn_all.items() if k in ('router_w1', 'router_w2', 'w1', 'w2', 'w3')}
    del _L0_ffn_all
    return {'x': x, 'L0_tok_Wa': _L0_tok_in['Wa'], 'L0_tok_ba': _L0_tok_in['ba'], 'L0_tok_Wd1': _L0_tok_in['Wd1'], 'L0_tok_bd1': _L0_tok_in['bd1'], 'L0_tok_Wd2': _L0_tok_in['Wd2'], 'L0_tok_bd2': _L0_tok_in['bd2'], 'L0_tok_Wd3': _L0_tok_in['Wd3'], 'L0_tok_bd3': _L0_tok_in['bd3'], 'L0_attn_Wq': _L0_attn_in['Wq'], 'L0_attn_bq': _L0_attn_in['bq'], 'L0_attn_Wk': _L0_attn_in['Wk'], 'L0_attn_bk': _L0_attn_in['bk'], 'L0_attn_Wv': _L0_attn_in['Wv'], 'L0_attn_bv': _L0_attn_in['bv'], 'L0_ffn_router_w1': _L0_ffn_in['router_w1'], 'L0_ffn_router_w2': _L0_ffn_in['router_w2'], 'L0_ffn_w1': _L0_ffn_in['w1'], 'L0_ffn_w2': _L0_ffn_in['w2'], 'L0_ffn_w3': _L0_ffn_in['w3']}

def reference(x, L0_tok_Wa, L0_tok_ba, L0_tok_Wd1, L0_tok_bd1, L0_tok_Wd2, L0_tok_bd2, L0_tok_Wd3, L0_tok_bd3, L0_attn_Wq, L0_attn_bq, L0_attn_Wk, L0_attn_bk, L0_attn_Wv, L0_attn_bv, L0_ffn_router_w1, L0_ffn_router_w2, L0_ffn_w1, L0_ffn_w2, L0_ffn_w3):
    import jax
    import jax.numpy as jnp

    def _L0_tok_ref(x, Wa, ba, Wd1, bd1, Wd2, bd2, Wd3, bd3):
        import jax, jax.numpy as jnp
        import numpy as np
        INV_SQRT2 = 0.7071067811865476
        LEVEL = 3

        def _split(x, axis):
            ax = axis % x.ndim
            sl0 = [slice(None)] * x.ndim
            sl0[ax] = slice(0, None, 2)
            sl1 = [slice(None)] * x.ndim
            sl1[ax] = slice(1, None, 2)
            x0, x1 = (x[tuple(sl0)], x[tuple(sl1)])
            return ((x0 + x1) * INV_SQRT2, (x0 - x1) * INV_SQRT2)

        def _merge(lo, hi, axis):
            ax = axis % lo.ndim
            e = (lo + hi) * INV_SQRT2
            o = (lo - hi) * INV_SQRT2
            s = jnp.stack([e, o], axis=ax + 1)
            shape = list(lo.shape)
            shape[ax] *= 2
            return s.reshape(shape)

        def _dwt2(x):
            lo, hi = _split(x, -1)
            a, h = _split(lo, -2)
            v, d = _split(hi, -2)
            return (a, h, v, d)

        def _idwt2(a, h, v, d):
            lo = _merge(a, h, -2)
            hi = _merge(v, d, -2)
            return _merge(lo, hi, -1)
        img = x[..., 0]
        B = img.shape[0]
        details = []
        cur = img
        for _ in range(LEVEL):
            cur, h, v, d = _dwt2(cur)
            details.append((h, v, d))
        aw = jax.nn.sigmoid(cur.reshape(B, -1) @ Wa + ba)
        rec = cur * aw[:, :, None]
        det_params = [(Wd1, bd1), (Wd2, bd2), (Wd3, bd3)]
        for (h, v, d), (Wd, bd) in zip(reversed(details), det_params):
            flat = jnp.stack([h, v, d], axis=1).reshape(B, -1)
            w = jax.nn.softmax(flat @ Wd + bd, axis=-1)
            rec = _idwt2(rec, h * w[:, 0, None, None], v * w[:, 1, None, None], d * w[:, 2, None, None])
        return rec

    def _L0_attn_ref(x, Wq, bq, Wk, bk, Wv, bv):
        import math
        import jax, jax.numpy as jnp
        import numpy as np
        B, S, E, H = (4, 512, 256, 16)
        HD = E // H
        b, s, e = x.shape
        h, hd, _ = Wq.shape
        inv_scale = 1.0 / math.sqrt(hd)
        q = jnp.einsum('bse,hde->bshd', x, Wq) + bq
        k = jnp.einsum('bse,hde->bshd', x, Wk) + bk
        v = jnp.einsum('bse,hde->bshd', x, Wv) + bv
        mask = jnp.triu(jnp.full((s, s), -jnp.inf, dtype=x.dtype), k=1)
        scores = (jnp.einsum('bqhd,bkhd->bhqk', q, k) + mask) * inv_scale
        attn = jax.nn.softmax(scores, axis=-1)
        out = jnp.einsum('bhqk,bkhd->bqhd', attn, v)
        return out.reshape(b, s, h * hd)

    def _L0_ffn_ref(hidden_states, router_w1, router_w2, w1, w2, w3):
        import jax, jax.numpy as jnp
        import numpy as np
        import math
        B, S, D = (4, 512, 256)
        E, DFF = (16, 512)
        CAP_FACTOR = 2.0
        ROUTER_HIDDEN = 128
        CAPACITY = int(math.ceil(S * CAP_FACTOR / E))
        b, s, d = hidden_states.shape
        e = w1.shape[0]
        cap = CAPACITY
        router_logits = jax.nn.silu(hidden_states @ router_w1) @ router_w2
        expert_probs = jax.nn.softmax(router_logits.transpose(0, 2, 1), axis=-1)
        expert_weights, token_indices = jax.lax.top_k(expert_probs, cap)
        expert_weights = expert_weights / (expert_weights.sum(-1, keepdims=True) + 1e-09)
        expert_inputs = jax.vmap(lambda h, i: h[i])(hidden_states, token_indices)
        gate = jax.nn.silu(jnp.einsum('becd,edf->becf', expert_inputs, w1))
        value = jnp.einsum('becd,edf->becf', expert_inputs, w2)
        expert_out = jnp.einsum('becf,efd->becd', gate * value, w3)
        weighted = expert_out * expert_weights[..., None]

        def combine(idx, vals):
            return jnp.zeros((s, d), vals.dtype).at[idx.reshape(-1)].add(vals.reshape(-1, d))
        output = jax.vmap(combine)(token_indices, weighted)
        return output
    h = _L0_tok_ref(x, L0_tok_Wa, L0_tok_ba, L0_tok_Wd1, L0_tok_bd1, L0_tok_Wd2, L0_tok_bd2, L0_tok_Wd3, L0_tok_bd3)
    h = h + _L0_attn_ref(_layernorm(h, axis=-1), L0_attn_Wq, L0_attn_bq, L0_attn_Wk, L0_attn_bk, L0_attn_Wv, L0_attn_bv)
    h = h + _L0_ffn_ref(_layernorm(h, axis=-1), L0_ffn_router_w1, L0_ffn_router_w2, L0_ffn_w1, L0_ffn_w2, L0_ffn_w3)
    return h

_drawn_inputs = setup_inputs


def setup_inputs(seed=0):
    import zlib

    import numpy as np

    out = dict(_drawn_inputs(seed))
    spreads = {'L0_tok_bd1': (0.0, 0.515), 'L0_tok_bd2': (0.0, 0.716), 'L0_tok_bd3': (0.0, 0.8)}
    factors = {'L0_attn_bq': 8.0,
     'L0_attn_bk': 8.0,
     'L0_attn_bv': 3.163,
     'L0_ffn_router_w1': 8.0,
     'L0_ffn_router_w2': 8.0,
     'L0_ffn_w1': 8.0,
     'L0_ffn_w2': 8.0,
     'L0_ffn_w3': 8.0}
    for name, (base, spread) in spreads.items():
        noise = np.random.default_rng([zlib.crc32(name.encode()), seed]).standard_normal(out[name].shape)
        drawn = base * np.exp(spread * noise) if base else spread * noise
        out[name] = jnp.asarray(drawn.astype(out[name].dtype))
    for name, factor in factors.items():
        out[name] = (out[name] * factor).astype(out[name].dtype)
    return out
```

```python
from contextlib import ExitStack

import concourse.bass as bass
from concourse import mybir

ALU = mybir.AluOpType
ACT = mybir.ActivationFunctionType
AX = mybir.AxisListType
F32 = mybir.dt.float32
F32R = mybir.dt.float32r
F16 = mybir.dt.float16
BF16 = mybir.dt.bfloat16
I32 = mybir.dt.int32

P = 128
BIG = -3.0e38
EPS = 1e-5


class Chain:

    def __init__(self, eng, sem, per, run):
        self.eng, self.sem, self.per, self.base, self.n = eng, sem, per, run * per, 0

    def step(self, ins):
        ins.then_inc(self.sem, 1)
        self.n += 1

    def wait(self):
        self.eng.wait_ge(self.sem, self.base + self.n)

    def end(self):
        assert self.n == self.per, (self.n, self.per)


def build_program(nc, x, Wa, ba, Wd1, bd1, Wd2, bd2, Wd3, bd3, Wq, bq, Wk, bk, Wv, bv, rw1, rw2, w1, w2, w3, out):
    B, S, D, _ = x.shape
    H, HD, _ = Wq.shape
    E, _, F = w1.shape
    RH = rw1.shape[1]
    TT = S // P
    KT = D // P
    NT = B * TT
    J = H // 2
    IT = 4
    G = S // 8
    assert (P, KT, TT, H * HD, RH, IT * G) == (128, 2, 2, D, 128, P)

    h_dram = nc.dram_tensor("h_scratch", [B * S, D], F32, kind="Internal").ap()
    q_dram = nc.dram_tensor("q_scratch", [2, 2, KT * P, S], F32, kind="Internal").ap()
    k_dram = nc.dram_tensor("k_scratch", [2, 2, KT * P, S], F32, kind="Internal").ap()
    logit_dram = nc.dram_tensor("logit_scratch", [B * E, S], F32, kind="Internal").ap()

    with ExitStack() as ctx:
        sb = lambda n, s, d=F32: ctx.enter_context(nc.sbuf_tensor(n, s, d))
        hacc = sb("hacc", [P, NT, D])
        lnA = sb("lnA", [P, NT, D], F16)
        lnB = sb("lnB", [P, NT, D], F16)
        ident = sb("ident", [P, P])
        ident16 = sb("ident16", [P, P], F16)
        identb = sb("identb", [P, P], BF16)

        with ExitStack() as mid:
            sbm = lambda n, s, d=F32: mid.enter_context(nc.sbuf_tensor(n, s, d))
            WT = {}
            for m in "qkv":
                WT[m] = [sbm(f"W{m}T_hi", [P, KT, D], F32R), sbm(f"W{m}T_lo", [P, KT, D], F32R)]
            maskS = sbm("maskS", [P, 4, P], BF16)
            maskT = sbm("maskT", [P, 4, P], BF16)
            tokenizer(nc, x, Wa, ba, [Wd1, Wd2, Wd3], [bd1, bd2, bd3], Wq, Wk, Wv, WT, hacc, h_dram,
                      ident, ident16, identb, maskS, maskT)
            attention(nc, bq, bk, bv, rw1, rw2, WT, hacc, lnA, lnB, q_dram, k_dram, logit_dram, ident, identb,
                      maskS, maskT, (B, S, D, H, HD, E))
        ffn(nc, ctx, w1, w2, w3, hacc, lnA, lnB, logit_dram, ident, ident16, out, (B, S, D, E, F))


def tokenizer(nc, x, Wa, ba, Wd, bd, Wq, Wk, Wv, WT, hacc, h_dram, ident, ident16, identb, maskS, maskT):
    B, S, D, _ = x.shape
    IT, G = 4, S // 8
    NTL = B // IT
    with ExitStack() as ctx:
        sb = lambda n, s, d=F32: ctx.enter_context(nc.sbuf_tensor(n, s, d))
        sem = lambda n: ctx.enter_context(nc.semaphore(n))
        X = [sb(f"x_tile{i}", [P, 8, D]) for i in range(2)]
        Y = [sb(f"rec_tile{i}", [P, 8, D]) for i in range(2)]
        su = sb("col_sum", [P, 8, D // 2])
        di = sb("col_dif", [P, 8, D // 2])
        band = [sb(f"band{l}", [P, 3, 8 >> l, D >> l]) for l in (1, 2, 3)]
        low = [sb(f"low{l}", [P, 8 >> l, D >> l]) for l in (1, 2, 3)]
        vs = sb("v_scaled", [P, 4, D // 2])
        junk = sb("junk", [P, 3, 4 * D // 2])
        wlev = [sb(f"wband{l}", [P, 3, (8 >> l) * (D >> l) * 3]) for l in (1, 2, 3)]
        wlow = sb("wlow", [P, D // 8])
        wraw = sb("wraw", [P, 3, 2, D])
        part = sb("part", [P, 10])
        bias = sb("bias", [P, 10])
        gsc = sb("gate_scale", [P, 10])
        osc = sb("out_scale", [P, 10])
        z = sb("z", [P, 10])
        ez = sb("ez", [P, 10])
        m3 = sb("m3", [P, 3])
        s4 = sb("s4", [P, 4])
        gate = sb("gate", [P, 10])
        ngate = sb("ngate", [P, 10])
        blk = sb("same_image", [P, P])
        zsum = ctx.enter_context(nc.psum_tensor("zsum", [P, 512], F32))
        wps = [ctx.enter_context(nc.psum_tensor(f"w_ps{i}", [P, 2, D], F32)) for i in range(3)]

        x_in = [sem(f"x_in{i}") for i in range(2)]
        w_in = sem("w_in")
        wqkv_in = sem("wqkv_in")
        x_used = sem("x_used")
        const0 = sem("const0")
        const_done = sem("const_done")
        part_done = sem("part_done")
        z_ready = sem("z_ready")
        arg_ready = sem("arg_ready")
        exp_ready = sem("exp_ready")
        rec_done = sem("rec_done")
        rec_out = [sem(f"rec_out{i}") for i in range(2)]
        h_in = sem("h_in")
        tc = sem("tok_chain")
        wt_ps = sem("wt_ps")
        wt_hi = sem("wt_hi")
        wt_lo = sem("wt_lo")

        xv = x.rearrange("b (g i) w c -> (b g) (i w c)", i=8)
        hv = h_dram.rearrange("(p i) w -> p (i w)", i=8)
        block = ctx.enter_context(nc.Block())
        NW = 4 * 4 + 4

        @block.sync
        def _(sp):
            sp.dma_start(X[0][:].rearrange("p i w -> p (i w)"), xv[0:P]).then_inc(x_in[0], 16)
            n = 0
            for l in (1, 2, 3):
                w = Wd[3 - l].rearrange("(c g k) o -> g c (k o)", c=3, g=G)
                for b in range(IT):
                    sp.dma_start(wlev[l - 1][b * G:(b + 1) * G], w).then_inc(w_in, 16)
                    n += 1
            for b in range(IT):
                sp.dma_start(wlow[b * G:(b + 1) * G], Wa.rearrange("(g k) o -> g (k o)", g=G)).then_inc(w_in, 16)
                n += 1
            for c0, c1, v in ((0, 1, ba), (1, 4, bd[0]), (4, 7, bd[1]), (7, 10, bd[2])):
                sp.dma_start(bias[:, c0:c1], v.rearrange("(a c) -> a c", a=1).broadcast_to([P, c1 - c0])).then_inc(w_in, 16)
                n += 1
            assert n == NW
            sp.dma_start(X[1][:].rearrange("p i w -> p (i w)"), xv[P:2 * P]).then_inc(x_in[1], 16)
            for i, w in enumerate((Wq, Wk, Wv)):
                sp.dma_start(wraw[:, i], w.rearrange("(t g) d e -> (g d) t e", t=2)).then_inc(wqkv_in, 16)
            for t in range(NTL):
                sp.wait_ge(rec_done, t + 1)
                sp.dma_start(hv[t * P:(t + 1) * P], Y[t % 2][:].rearrange("p i w -> p (i w)")).then_inc(rec_out[t % 2], 16)
                if t + 2 < NTL:
                    sp.dma_start(X[t % 2][:].rearrange("p i w -> p (i w)"), xv[(t + 2) * P:(t + 3) * P]).then_inc(x_in[t % 2], 16)
                sp.wait_ge(rec_out[t % 2], 16 * (t // 2 + 1))
                sp.dma_start(hacc[:, 8 * t:8 * t + 8, :],
                             h_dram.rearrange("(n p) w -> p n w", p=P)[:, 8 * t:8 * t + 8, :]).then_inc(h_in, 16)
            sp.wait_ge(h_in, 16 * NTL)

        @block.gpsimd
        def _(g):
            nc.gpsimd.memset(ident[:], 0.0).then_inc(const0, 1)
            nc.gpsimd.memset(maskS[:], 0.0).then_inc(const0, 1)
            nc.gpsimd.memset(maskT[:], 0.0).then_inc(const0, 1)
            nc.gpsimd.memset(blk[:], 0.0).then_inc(const0, 1)
            g.wait_ge(const0, 4)
            nc.gpsimd.affine_select(out=ident[:], in_=ident[:], compare_op=ALU.not_equal, fill=1.0, base=0,
                                    pattern=[[-1, P]], channel_multiplier=1).then_inc(const_done, 1)
            nc.gpsimd.affine_select(out=maskS[:], in_=maskS[:], compare_op=ALU.is_ge, fill=BIG, base=0,
                                    pattern=[[0, 4], [-1, P]], channel_multiplier=1).then_inc(const_done, 1)
            nc.gpsimd.affine_select(out=maskT[:], in_=maskT[:], compare_op=ALU.is_ge, fill=BIG, base=0,
                                    pattern=[[0, 4], [1, P]], channel_multiplier=-1).then_inc(const_done, 1)
            g.wait_ge(const_done, 3)
            for b in range(IT):
                nc.gpsimd.memset(blk[b * G:(b + 1) * G, b * G:(b + 1) * G], 1.0).then_inc(const_done, 1)
            g.wait_ge(const_done, 3 + IT)
            nc.gpsimd.tensor_copy(ident16[:], ident[:]).then_inc(const_done, 1)
            nc.gpsimd.tensor_copy(identb[:], ident[:]).then_inc(const_done, 1)

        @block.tensor
        def _(pe):
            pe.wait_ge(const_done, 5 + IT)
            pe.wait_ge(wqkv_in, 48)
            for i in range(3):
                for ft in range(2):
                    for kt in range(2):
                        ins = pe.transpose(wps[i][:, kt, ft * P:(ft + 1) * P], wraw[:, i, ft, kt * P:(kt + 1) * P], ident[:])
                ins.then_inc(wt_ps, 1)
            for t in range(NTL):
                pe.wait_ge(part_done, t + 1)
                if t:
                    pe.wait_ge(z_ready, t)
                pe.matmul(zsum[:, 0:10], blk[:], part[:], start=True, stop=True).then_inc(arg_ready, 1)

        @block.scalar
        def _(act):
            for i, m in enumerate("qkv"):
                act.wait_ge(wt_ps, i + 1)
                nc.scalar.activation(WT[m][0][:], wps[i][:], ACT.Copy).then_inc(wt_hi, 1)
            for t in range(NTL):
                act.wait_ge(z_ready, t + 1)
                nc.scalar.activation(ez[:], z[:], ACT.Exp).then_inc(exp_ready, 1)

        @block.vector
        def _(v):
            v.wait_ge(const0, 4)
            c = Chain(v, tc, 0, 0)
            for a, b_, g_, o_ in ((0, 4, 0.125, 1 / 64), (4, 7, 0.25, 1 / 16), (7, 10, 0.5, 1 / 4)):
                c.step(nc.vector.memset(gsc[:, a:b_], g_))
                c.step(nc.vector.memset(osc[:, a:b_], o_))
            V = nc.vector
            for t in range(NTL):
                p = t % 2
                v.wait_ge(x_in[p], 16 * (t // 2 + 1))
                src = X[p]
                for l in range(3):
                    R, C = 8 >> l, D >> l
                    s_, d_ = su[:, 0:R, 0:C // 2], di[:, 0:R, 0:C // 2]
                    pr = src[:].rearrange("p r (c two) -> p r c two", two=2)
                    c.wait()
                    c.step(V.tensor_tensor(s_, pr[:, :, :, 0], pr[:, :, :, 1], ALU.add))
                    c.step(V.tensor_tensor(d_, pr[:, :, :, 0], pr[:, :, :, 1], ALU.subtract))
                    c.wait()
                    sp_ = s_.rearrange("p (r two) c -> p r two c", two=2)
                    dp_ = d_.rearrange("p (r two) c -> p r two c", two=2)
                    c.step(V.tensor_tensor(low[l][:], sp_[:, :, 0], sp_[:, :, 1], ALU.add))
                    c.step(V.tensor_tensor(band[l][:, 0], sp_[:, :, 0], sp_[:, :, 1], ALU.subtract))
                    c.step(V.tensor_tensor(band[l][:, 1], dp_[:, :, 0], dp_[:, :, 1], ALU.add))
                    c.step(V.tensor_tensor(band[l][:, 2], dp_[:, :, 0], dp_[:, :, 1], ALU.subtract))
                    src = low[l]
                c.wait()
                if t == 0:
                    v.wait_ge(w_in, 16 * NW)
                if t:
                    v.wait_ge(arg_ready, t)
                c.step(V.tensor_tensor_reduce(junk[:, 0, 0:D // 8], low[2][:, 0, :], wlow[:], 1.0, 0.0, ALU.mult, ALU.add, part[:, 0:1]))
                for l in (3, 2, 1):
                    n = (8 >> l) * (D >> l)
                    wv_ = wlev[l - 1][:].rearrange("p c (k o) -> p o c k", o=3)
                    for o in range(3):
                        c.wait()
                        col = 1 + 3 * (3 - l) + o
                        c.step(V.tensor_tensor_reduce(junk[:, :, 0:n], band[l - 1][:].rearrange("p c r w -> p c (r w)"), wv_[:, o],
                                                      1.0, 0.0, ALU.mult, ALU.add, part[:, col:col + 1]))
                c.wait()
                V.tensor_copy(z[:], part[:]).then_inc(part_done, 1)
                c.n += 0
                v.wait_ge(arg_ready, t + 1)
                v.wait_ge(part_done, t + 1)
                c.step(V.tensor_tensor(z[:], zsum[:, 0:10], gsc[:], ALU.mult))
                c.wait()
                c.step(V.tensor_tensor(z[:], z[:], bias[:], ALU.add))
                c.wait()
                z3 = z[:, 1:10].rearrange("p (l o) -> p l o", o=3)
                c.step(V.tensor_reduce(m3[:], z3, AX.X, ALU.max))
                c.step(V.tensor_scalar(z[:, 0:1], z[:, 0:1], -1.0, 88.0, ALU.mult, ALU.min))
                c.wait()
                V.tensor_tensor(z3, z3, m3[:].rearrange("p (l o) -> p l o", o=1).broadcast_to([P, 3, 3]), ALU.subtract).then_inc(z_ready, 1)
                v.wait_ge(exp_ready, t + 1)
                e3 = ez[:, 1:10].rearrange("p (l o) -> p l o", o=3)
                c.step(V.tensor_reduce(s4[:, 1:4], e3, AX.X, ALU.add))
                c.step(V.tensor_scalar(s4[:, 0:1], ez[:, 0:1], 1.0, None, ALU.add))
                c.wait()
                c.step(V.reciprocal(s4[:], s4[:]))
                c.wait()
                c.step(V.tensor_tensor(gate[:, 1:10].rearrange("p (l o) -> p l o", o=3), e3,
                                       s4[:, 1:4].rearrange("p (l o) -> p l o", o=1).broadcast_to([P, 3, 3]), ALU.mult))
                c.step(V.tensor_copy(gate[:, 0:1], s4[:, 0:1]))
                c.wait()
                c.step(V.tensor_tensor(gate[:], gate[:], osc[:], ALU.mult))
                c.wait()
                c.step(V.tensor_scalar(ngate[:], gate[:], -1.0, None, ALU.mult))
                c.step(V.tensor_scalar(low[2][:], low[2][:], gate[:, 0:1], None, ALU.mult))
                if t >= 2:
                    v.wait_ge(rec_out[p], 16 * (t // 2))
                for l in (2, 1, 0):
                    R, C = 8 >> (l + 1), D >> (l + 1)
                    g0 = 1 + 3 * (2 - l)
                    sp_ = su[:, 0:2 * R, 0:C].rearrange("p (r two) c -> p r two c", two=2)
                    dp_ = di[:, 0:2 * R, 0:C].rearrange("p (r two) c -> p r two c", two=2)
                    vv = vs[:, 0:R, 0:C]
                    c.wait()
                    c.step(V.scalar_tensor_tensor(sp_[:, :, 0], band[l][:, 0], gate[:, g0:g0 + 1], low[l][:], ALU.mult, ALU.add))
                    c.step(V.scalar_tensor_tensor(sp_[:, :, 1], band[l][:, 0], ngate[:, g0:g0 + 1], low[l][:], ALU.mult, ALU.add))
                    c.step(V.tensor_scalar(vv, band[l][:, 1], gate[:, g0 + 1:g0 + 2], None, ALU.mult))
                    c.wait()
                    c.step(V.scalar_tensor_tensor(dp_[:, :, 0], band[l][:, 2], gate[:, g0 + 2:g0 + 3], vv, ALU.mult, ALU.add))
                    c.step(V.scalar_tensor_tensor(dp_[:, :, 1], band[l][:, 2], ngate[:, g0 + 2:g0 + 3], vv, ALU.mult, ALU.add))
                    c.wait()
                    dst = (low[l - 1] if l else Y[p])[:].rearrange("p r (c two) -> p r c two", two=2)
                    a_, b_ = su[:, 0:2 * R, 0:C], di[:, 0:2 * R, 0:C]
                    c.step(V.tensor_tensor(dst[:, :, :, 0], a_, b_, ALU.add))
                    if l:
                        c.step(V.tensor_tensor(dst[:, :, :, 1], a_, b_, ALU.subtract))
                    else:
                        c.wait()
                        V.tensor_tensor(dst[:, :, :, 1], a_, b_, ALU.subtract).then_inc(rec_done, 1)
                v.wait_ge(rec_done, t + 1)
                if t < 3:
                    m = "qkv"[t]
                    v.wait_ge(wt_hi, t + 1)
                    c.step(V.tensor_tensor(WT[m][1][:], wps[t][:], WT[m][0][:].bitcast(F32), ALU.subtract))


def attention(nc, bq, bk, bv, rw1, rw2, WT, hacc, lnA, lnB, q_dram, k_dram, logit_dram, ident, identb, maskS, maskT, dims):
    B, S, D, H, HD, E = dims
    J = H // 2
    NB = 12
    with ExitStack() as ctx:
        sb = lambda n, s, d=F32: ctx.enter_context(nc.sbuf_tensor(n, s, d))
        sem = lambda n: ctx.enter_context(nc.semaphore(n))
        ps = lambda n, s, d=F32: ctx.enter_context(nc.psum_tensor(n, s, d))
        hn1 = sb("hn1", [P, 2, D])
        hn2 = sb("hn2", [P, 2, D])
        xT = [sb("xT_hi", [P, 2, S], F32R), sb("xT_lo", [P, 2, S], F32R)]
        qf = [sb("q_hi", [P, 2, S], F32R), sb("q_lo", [P, 2, S], F32R)]
        kf = [sb("k_hi", [P, 2, S], F32R), sb("k_lo", [P, 2, S], F32R)]
        QS = [sb(f"q_stack{i}", [P, J, 2, S], F32R) for i in range(2)]
        KS = [sb(f"k_stack{i}", [P, J, S], F32R) for i in range(2)]
        V1 = [sb(f"v_ones{i}", [P, 2, H, HD + 1]) for i in range(2)]
        PT0 = sb("probs_k0", [P, H, S])
        PT1 = sb("probs_k1", [P, H, P])
        mx = sb("row_max", [P, 2, H])
        mT = [sb("negmax_hi", [H, S], F32R), sb("negmax_lo", [H, S], F32R)]
        rden = sb("rden", [P, 2, H])
        on = sb("attn_norm", [P, 2, D])
        bqk = sb("bqk", [P, 2, 2])
        bvb = sb("bv_bcast", [P, D])
        rw1s = sb("rw1s", [P, 2, P])
        rw2s = sb("rw2s", [P, E])
        tick = sb("tick", [P, 3])
        st = sb("stats", [P, 2, 6])
        mv = sb("mean_var", [P, 2, 2])
        rs = sb("rstd", [P, 4, 2])
        hn2T = sb("hn2T", [P, 2, S])
        eh = sb("exp_neg", [P, S])
        rh = sb("silu", [P, S])
        d16 = sb("ln_rest", [P, 2, D])
        lg = sb("logits", [E, S])
        R3 = [ps(f"scores_ps{i}", [P, 512]) for i in range(3)]
        OP = [ps(f"out_ps{i}", [P, 512]) for i in range(2)]
        M = [ps(f"mix_ps{i}", [P, 2, 256]) for i in range(2)]
        RP = ps("router_ps", [P, 512])

        c_in, zero_done, ones_done = sem("c_in"), sem("zero_done"), sem("ones_done")
        ln_chain = [sem("ln1_chain"), sem("ln2_chain")]
        ln1_done, ln2_done = sem("ln1_done"), sem("ln2_done")
        xT_ps, xT_hi, xT_lo = sem("xT_ps"), sem("s_xT_hi"), sem("s_xT_lo")
        q_ps, k_ps, v_ps = sem("q_ps"), sem("k_ps"), sem("v_ps")
        qk_hi, q_lo, k_lo = sem("qk_hi"), sem("s_q_lo"), sem("s_k_lo")
        v_done = sem("v_done")
        qk_written, stack_in = sem("qk_written"), sem("stack_in")
        s_ps, s_max = sem("s_ps"), sem("s_max")
        m_ps, m_hi, m_lo, m_in = sem("m_ps"), sem("m_hi"), sem("m_lo"), sem("m_in")
        st_ps, exp_done = sem("st_ps"), sem("exp_done")
        av_done = sem("av_done")
        norm_chain, h_done = sem("norm_chain"), sem("h_done")
        lnA_done, rest_done, lnB_done = sem("lnA_done"), sem("rest_done"), sem("lnB_done")
        hT_ps, hT_done, rh_ps, rexp_done, silu_chain, silu_done = (sem("hT_ps"), sem("hT_done"), sem("rh_ps"),
            sem("rexp_done"), sem("silu_chain"), sem("silu_done"))
        lg_ps, lg_done, lg_out = sem("lg_ps"), sem("lg_done"), sem("lg_out")
        block = ctx.enter_context(nc.Block())
        T, A, V = nc.tensor, nc.scalar, nc.vector

        def images(eng, one):
            one(0, 0, False, True, True)
            one(1, 1, True, True, True)
            with eng.Fori(2, B - 3, 2) as i:
                one(i, 0, True, True, True)
                one(i + 1, 1, True, True, True)
            one(B - 2, 0, True, True, False)
            one(B - 1, 1, True, False, False)

        @block.sync
        def _(sp):
            with nc.allow_non_contiguous_dma(reason="biases, once"):
                sp.dma_start(bqk[:, 0, :], bq.rearrange("(t g) d -> (g d) t", t=2)).then_inc(c_in, 16)
                sp.dma_start(bqk[:, 1, :], bk.rearrange("(t g) d -> (g d) t", t=2)).then_inc(c_in, 16)
            sp.dma_start(bvb[:], bv.rearrange("(o h) d -> o (h d)", o=1).broadcast_to([P, D])).then_inc(c_in, 16)
            sp.dma_start(rw1s[:], rw1.rearrange("(t p) n -> p t n", p=P)).then_inc(c_in, 16)
            sp.dma_start(rw2s[:], rw2).then_inc(c_in, 16)
            sp.wait_ge(zero_done, 2)
            sp.wait_ge(ones_done, 4)

            def write_qk(b, p):
                sp.wait_ge(q_lo, 2 * (b + 1))
                for x in range(2):
                    sp.dma_start(q_dram[p, x].rearrange("(f p) q -> p f q", p=P), qf[x][:].bitcast(F32)).then_inc(qk_written, 16)
                sp.wait_ge(k_lo, 2 * (b + 1))
                for x in range(2):
                    sp.dma_start(k_dram[p, x].rearrange("(f p) q -> p f q", p=P), kf[x][:].bitcast(F32)).then_inc(qk_written, 16)

            def read_stack(b, p):
                sp.wait_ge(qk_written, 64 * (b + 1))
                if not isinstance(b, int) or b >= 2:
                    sp.wait_ge(av_done, b - 1)
                for a in range(2):
                    for t, (xq, xk) in enumerate(((0, 0), (1, 0), (0, 1))):
                        r = 48 * a + 16 * t
                        qsrc = q_dram[p, xq].rearrange("(j a d) q -> a d j q", a=2, d=HD)[a]
                        ksrc = k_dram[p, xk].rearrange("(j a d) q -> a d j q", a=2, d=HD)[a]
                        sp.dma_start(QS[p][r:r + HD, :, a, :].bitcast(F32), qsrc).then_inc(stack_in, 16)
                        sp.dma_start(KS[p][r:r + HD, :, :].bitcast(F32), ksrc).then_inc(stack_in, 16)

            def write_max(b, p):
                sp.wait_ge(m_lo, b + 1)
                for a in range(2):
                    for x in range(2):
                        r = 96 + 2 * a + x
                        sp.dma_start(QS[p][r:r + 1, :, a, :].bitcast(F32), mT[x][a:H:2, :].bitcast(F32)).then_inc(m_in, 16)

            def write_logits(b):
                row = b * E if isinstance(b, int) else sp.snap(b * E)
                rows = logit_dram[bass.ds(row, E)]
                sp.wait_ge(lg_done, b + 1)
                sp.dma_start(rows, lg[:]).then_inc(lg_out, 16)

            write_qk(0, 0)
            read_stack(0, 0)

            def one(i, p, router, front, front2):
                if front:
                    write_qk(i + 1, 1 - p)
                write_max(i, p)
                if front:
                    read_stack(i + 1, 1 - p)
                if router:
                    write_logits(i - 1)
            images(sp, one)
            write_logits(B - 1)
            sp.wait_ge(lg_out, 16 * B)

        @block.tensor
        def _(pe):
            pe.wait_ge(c_in, 16 * 5)
            pe.wait_ge(ones_done, 4)
            pe.wait_ge(zero_done, 2)

            def turn_x(b):
                pe.wait_ge(ln1_done, b + 1)
                if not isinstance(b, int) or b:
                    pe.wait_ge(v_done, b)
                for tt in range(2):
                    for kt in range(2):
                        ins = pe.transpose(M[0][:, kt, tt * P:(tt + 1) * P], hn1[:, tt, kt * P:(kt + 1) * P], ident[:])
                ins.then_inc(xT_ps, 1)

            def project(b, m, bank, done):
                W = WT[m]
                for o in range(2):
                    n = 0
                    for kt in range(2):
                        for wi, xi in ((0, 0), (0, 1), (1, 0)):
                            if m == "v":
                                lhsT, rhs = xT[xi][:, kt, o * P:(o + 1) * P], W[wi][:, kt, :]
                            else:
                                lhsT, rhs = W[wi][:, kt, o * P:(o + 1) * P], xT[xi][:, kt, :]
                            ins = pe.matmul(M[bank][:, o, :], lhsT, rhs, start=(n == 0), stop=(n == 5))
                            n += 1
                ins.then_inc(done, 1)

            def scores(b, p):
                pe.wait_ge(stack_in, 192 * (b + 1))
                for n in range(NB):
                    bank = R3[n % 3]
                    if n >= 3:
                        pe.wait_ge(s_max, NB * b + n - 2)
                    elif not isinstance(b, int) or b:
                        pe.wait_ge(exp_done, NB * b - 2 + n)
                    if n < 4:
                        for x in range(4):
                            j, a = 2 * n + x // 2, x % 2
                            pe.matmul(bank[:, x * P:(x + 1) * P], QS[p][0:96, j, a, 0:P], KS[p][0:96, j, 0:P],
                                      start=(x == 0), stop=False, skip_group_check=True)
                        ins = pe.matmul(bank[:], identb[:], maskS[:].rearrange("p a k -> p (a k)"), start=False, stop=True,
                                        skip_group_check=True)
                    else:
                        j = n - 4
                        for a in range(2):
                            pe.matmul(bank[:, a * S:(a + 1) * S], QS[p][0:96, j, a, P:S], KS[p][0:96, j, :],
                                      start=(a == 0), stop=False, skip_group_check=True)
                        ins = pe.matmul(bank[:].rearrange("p (a k) -> p a k", a=2)[:, :, P:S], identb[:], maskS[:, 0:2, :],
                                        start=False, stop=True, skip_group_check=True)
                    ins.then_inc(s_ps, 1)

            def turn_max(b, q_next):
                pe.wait_ge(s_max, NB * (b + 1))
                if q_next:
                    pe.wait_ge(q_lo, 2 * (b + 2))
                else:
                    pe.wait_ge(hT_done, b)
                for tt in range(2):
                    ins = pe.transpose(M[1][0:H, 0, tt * P:(tt + 1) * P], mx[:, tt, :], ident[:])
                ins.then_inc(m_ps, 1)

            def exp_scores(b, p, g):
                if g == 0:
                    pe.wait_ge(m_in, 64 * (b + 1))
                for y in range(3):
                    n = 3 * g + y
                    bank = R3[n % 3]
                    if n >= 3:
                        pe.wait_ge(exp_done, NB * b + n - 2)
                    else:
                        pe.wait_ge(s_max, NB * b + NB - 2 + n)
                    if y < 2:
                        j = 2 * g + y
                        pe.matmul(bank[:], KS[p][0:100, j, 0:P], QS[p][0:100, j, :, :].rearrange("p a q -> p (a q)"),
                                  start=True, stop=False, skip_group_check=True)
                        ins = pe.matmul(bank[:].rearrange("p (a q) -> p a q", a=2)[:, :, 0:P], identb[:], maskT[:, 0:2, :],
                                        start=False, stop=True, skip_group_check=True)
                    else:
                        for x in range(2):
                            j = 2 * g + x
                            pe.matmul(bank[:].rearrange("p (x a q) -> p x a q", x=2, a=2)[:, x], KS[p][0:100, j, P:S],
                                      QS[p][0:100, j, :, P:S], start=(x == 0), stop=False, skip_group_check=True)
                        ins = pe.matmul(bank[:], identb[:], maskT[:].rearrange("p a k -> p (a k)"), start=False, stop=True,
                                        skip_group_check=True)
                    ins.then_inc(st_ps, 1)

            def times_v(b, p, g):
                pe.wait_ge(exp_done, NB * b + 3 * (g + 1))
                if g == 0:
                    pe.wait_ge(v_done, b + 1)
                    if not isinstance(b, int) or b:
                        pe.wait_ge(h_done, b)
                W = HD + 1
                for h in range(4 * g, 4 * g + 4):
                    o0, o1 = OP[0][:, h * W:(h + 1) * W], OP[1][:, h * W:(h + 1) * W]
                    pe.matmul(o0, PT0[:, h, 0:P], V1[p][:, 0, h, :], start=True, stop=True)
                    pe.matmul(o1, PT0[:, h, P:S], V1[p][:, 0, h, :], start=True, stop=False)
                    ins = pe.matmul(o1, PT1[:, h, :], V1[p][:, 1, h, :], start=False, stop=True)
                if g == 3:
                    ins.then_inc(av_done, 1)

            def turn_h(b):
                pe.wait_ge(ln2_done, b + 1)
                pe.wait_ge(m_lo, b + 1)
                for tt in range(2):
                    for kt in range(2):
                        ins = pe.transpose(M[1][:, kt, tt * P:(tt + 1) * P], hn2[:, tt, kt * P:(kt + 1) * P], ident[:])
                ins.then_inc(hT_ps, 1)

            def router_1(b):
                pe.wait_ge(hT_done, b + 1)
                if not isinstance(b, int) or b:
                    pe.wait_ge(lg_done, b)
                for kt in range(2):
                    ins = pe.matmul(RP[:, 0:S], rw1s[:, kt, :], hn2T[:, kt, :], start=(kt == 0), stop=(kt == 1))
                ins.then_inc(rh_ps, 1)

            def router_2(b):
                pe.wait_ge(silu_done, b + 1)
                pe.matmul(RP[0:E, S:2 * S], rw2s[:], rh[:], start=True, stop=True).then_inc(lg_ps, 1)

            def front_k(b):
                pe.wait_ge(xT_lo, b + 1)
                project(b, "k", 0, k_ps)

            def front_v(b):
                pe.wait_ge(k_lo, 2 * (b + 1))
                project(b, "v", 0, v_ps)

            turn_x(0)
            pe.wait_ge(xT_lo, 1)
            project(0, "q", 1, q_ps)
            front_k(0)
            front_v(0)

            def one(i, p, router, front, front2):
                if front:
                    turn_x(i + 1)
                if router:
                    turn_h(i - 1)
                scores(i, p)
                if front:
                    pe.wait_ge(xT_lo, i + 2)
                    if router:
                        pe.wait_ge(hT_done, i)
                    else:
                        pe.wait_ge(q_lo, 2 * (i + 1))
                    project(i + 1, "q", 1, q_ps)
                    front_k(i + 1)
                turn_max(i, front)
                if front:
                    front_v(i + 1)
                if router:
                    router_1(i - 1)
                for g in range(4):
                    exp_scores(i, p, g)
                    if g:
                        times_v(i, p, g - 1)
                times_v(i, p, 3)
                if router:
                    router_2(i - 1)
            images(pe, one)
            turn_h(B - 1)
            router_1(B - 1)
            router_2(B - 1)

        @block.scalar
        def _(act):
            act.wait_ge(c_in, 16 * 5)

            def x_hi(b):
                act.wait_ge(xT_ps, b + 1)
                if not isinstance(b, int) or b:
                    act.wait_ge(v_ps, b)
                A.activation(xT[0][:], M[0][:], ACT.Copy).then_inc(xT_hi, 1)

            def qk_parts(b, m, bank, full, dst):
                act.wait_ge(full, b + 1)
                if not isinstance(b, int) or b:
                    act.wait_ge(qk_written, 64 * b)
                for ft in range(2):
                    A.activation(dst[0][:, ft, :], M[bank][:, ft, :], ACT.Identity,
                                 bias=bqk[:, m, ft:ft + 1]).then_inc(qk_hi, 1)

            def max_hi(b):
                act.wait_ge(m_ps, b + 1)
                if not isinstance(b, int) or b:
                    act.wait_ge(m_in, 64 * b)
                A.activation(mT[0][:], M[1][0:H, 0, :], ACT.Copy, scale=-1.0).then_inc(m_hi, 1)

            def exps(b):
                for g in range(4):
                    for y in range(3):
                        n = 3 * g + y
                        act.wait_ge(st_ps, NB * b + n + 1)
                        if n == 0 and (not isinstance(b, int) or b):
                            act.wait_ge(av_done, b)
                        if y < 2:
                            dst = PT0[:, 4 * g + 2 * y:4 * g + 2 * y + 2, :]
                            src = R3[n % 3][:].rearrange("p (a q) -> p a q", a=2)
                        else:
                            dst = PT1[:, 4 * g:4 * g + 4, :]
                            src = R3[n % 3][:].rearrange("p (a q) -> p a q", a=4)
                        A.activation(dst, src, ACT.Exp, scale=float(HD) ** -0.5).then_inc(exp_done, 1)

            def hT_copy(b):
                act.wait_ge(hT_ps, b + 1)
                if not isinstance(b, int) or b:
                    act.wait_ge(rh_ps, b)
                A.activation(hn2T[:], M[1][:], ACT.Copy).then_inc(hT_done, 1)

            def router_exp(b):
                act.wait_ge(rh_ps, b + 1)
                if not isinstance(b, int) or b:
                    act.wait_ge(silu_done, b)
                A.activation(eh[:], RP[:, 0:S], ACT.Exp, scale=-1.0).then_inc(rexp_done, 1)

            def logits(b):
                act.wait_ge(lg_ps, b + 1)
                if not isinstance(b, int) or b:
                    act.wait_ge(lg_out, 16 * b)
                A.activation(lg[:], RP[0:E, S:2 * S], ACT.Copy).then_inc(lg_done, 1)

            def ln_parts(b):
                act.wait_ge(ln2_done, b + 1)
                ts = slice(2 * b, 2 * b + 2) if isinstance(b, int) else bass.ds(2 * b, 2)
                A.activation(lnA[:, ts, :], hn2[:], ACT.Copy).then_inc(lnA_done, 1)
                act.wait_ge(rest_done, b + 1)
                A.activation(lnB[:, ts, :], d16[:], ACT.Copy, scale=2048.0).then_inc(lnB_done, 1)

            x_hi(0)
            qk_parts(0, 0, 1, q_ps, qf)
            qk_parts(0, 1, 0, k_ps, kf)

            def one(i, p, router, front, front2):
                if front:
                    x_hi(i + 1)
                if router:
                    hT_copy(i - 1)
                if front:
                    qk_parts(i + 1, 0, 1, q_ps, qf)
                    qk_parts(i + 1, 1, 0, k_ps, kf)
                max_hi(i)
                if router:
                    router_exp(i - 1)
                exps(i)
                if router:
                    logits(i - 1)
                ln_parts(i)
            images(act, one)
            hT_copy(B - 1)
            router_exp(B - 1)
            logits(B - 1)

        @block.vector
        def _(v):
            for p in range(2):
                V.memset(QS[p][:].bitcast(F32), 0.0).then_inc(zero_done, 1)
                V.memset(KS[p][96:P].bitcast(F32), 1.0).then_inc(ones_done, 1)
                V.memset(V1[p][:, :, :, HD:HD + 1], 1.0).then_inc(ones_done, 1)
            v.wait_ge(c_in, 16 * 5)

            def layernorm(b, which, dst, done):
                ts = slice(2 * b, 2 * b + 2) if isinstance(b, int) else bass.ds(2 * b, 2)
                h = hacc[:, ts, :]
                c = Chain(v, ln_chain[which], 18, b)
                if which == 1:
                    v.wait_ge(h_done, b + 1)
                    V.memset(tick[:, 0:1], 0.0)
                xx, xh, y, u = rs[:, 0], rs[:, 1], rs[:, 2], rs[:, 3]
                for tt in range(2):
                    c.step(V.bn_stats(st[:, tt, :], h[:, tt, :]))
                c.wait()
                V.memset(tick[:, 1 + which:2 + which], 0.0)
                for tt in range(2):
                    c.step(V.bn_aggr(mv[:, tt, :], st[:, tt, :]))
                c.wait()
                c.step(V.tensor_scalar(xx, mv[:, :, 1], EPS, None, ALU.add))
                c.wait()
                c.step(V.tensor_scalar(xh, xx, -0.5, None, ALU.mult))
                c.step(V.tensor_scalar(u.bitcast(I32), xx.bitcast(I32), 1, None, ALU.logical_shift_right))
                c.wait()
                c.step(V.tensor_scalar(y.bitcast(I32), u.bitcast(I32), -1.0, float(0x5F3759DF), ALU.mult, ALU.add))
                for _ in range(3):
                    c.wait()
                    c.step(V.tensor_tensor(u, y, y, ALU.mult))
                    c.wait()
                    c.step(V.tensor_tensor(u, u, xh, ALU.mult))
                    c.wait()
                    c.step(V.scalar_tensor_tensor(y, u, 1.5, y, ALU.add, ALU.mult))
                c.wait()
                if which == 0:
                    if not isinstance(b, int) or b:
                        v.wait_ge(xT_ps, b)
                elif not isinstance(b, int) or b:
                    v.wait_ge(hT_ps, b)
                    v.wait_ge(lnA_done, b)
                for tt in range(2):
                    ins = V.tensor_scalar(dst[:, tt, :], h[:, tt, :], mv[:, tt, 0:1], y[:, tt:tt + 1], ALU.subtract, ALU.mult)
                    if tt == 0:
                        c.step(ins)
                    else:
                        ins.then_inc(done, 1)
                c.end()

            def x_lo(b):
                v.wait_ge(xT_hi, b + 1)
                V.tensor_tensor(xT[1][:], M[0][:], xT[0][:].bitcast(F32), ALU.subtract).then_inc(xT_lo, 1)

            def qk_lo_parts(b, m, bank, src, done):
                if not isinstance(b, int) or b:
                    v.wait_ge(qk_written, 64 * b)
                v.wait_ge(qk_hi, 4 * b + 2 * m + 2)
                for ft in range(2):
                    V.scalar_tensor_tensor(src[1][:, ft, :], M[bank][:, ft, :], bqk[:, m, ft:ft + 1],
                                           src[0][:, ft, :].bitcast(F32), ALU.add, ALU.subtract).then_inc(done, 1)

            def max_scores(b):
                for n in range(NB):
                    v.wait_ge(s_ps, NB * b + n + 1)
                    if n == 0 and (not isinstance(b, int) or b):
                        v.wait_ge(m_ps, b)
                    bank = R3[n % 3][:]
                    if n < 4:
                        V.tensor_reduce(mx[:, 0, 4 * n:4 * n + 4], bank.rearrange("p (a k) -> p a k", a=4), AX.X,
                                        ALU.max).then_inc(s_max, 1)
                    else:
                        j = n - 4
                        V.tensor_reduce(mx[:, 1, 2 * j:2 * j + 2], bank.rearrange("p (a k) -> p a k", a=2), AX.X,
                                        ALU.max).then_inc(s_max, 1)

            def max_lo(b):
                v.wait_ge(m_hi, b + 1)
                if not isinstance(b, int) or b:
                    v.wait_ge(m_in, 64 * b)
                V.scalar_tensor_tensor(mT[1][:], M[1][0:H, 0, :], -1.0, mT[0][:].bitcast(F32), ALU.mult,
                                       ALU.subtract).then_inc(m_lo, 1)

            def v_bias(b, p):
                v.wait_ge(v_ps, b + 1)
                if not isinstance(b, int) or b >= 2:
                    v.wait_ge(av_done, b - 1)
                V.tensor_tensor(V1[p][:, :, :, 0:HD], M[0][:].rearrange("p t (h d) -> p t h d", d=HD),
                                bvb[:].rearrange("p (o h d) -> p o h d", o=1, d=HD).broadcast_to([P, 2, H, HD]),
                                ALU.add).then_inc(v_done, 1)

            def silu(b):
                v.wait_ge(rexp_done, b + 1)
                c = Chain(v, silu_chain, 2, b)
                c.step(V.tensor_scalar(rh[:], eh[:], 1.0, None, ALU.add))
                c.wait()
                c.step(V.reciprocal(rh[:], rh[:]))
                c.wait()
                V.tensor_tensor(rh[:], RP[:, 0:S], rh[:], ALU.mult).then_inc(silu_done, 1)
                c.end()

            def add_attention(b):
                v.wait_ge(av_done, b + 1)
                ts = slice(2 * b, 2 * b + 2) if isinstance(b, int) else bass.ds(2 * b, 2)
                c = Chain(v, norm_chain, 4, b)
                o = [OP[tt][:, 0:H * (HD + 1)].rearrange("p (h c) -> p h c", c=HD + 1) for tt in range(2)]
                for tt in range(2):
                    c.step(V.reciprocal(rden[:, tt, :], o[tt][:, :, HD]))
                c.wait()
                for tt in range(2):
                    c.step(V.tensor_tensor(on[:, tt, :].rearrange("p (h d) -> p h d", d=HD), o[tt][:, :, 0:HD],
                                           rden[:, tt, :].rearrange("p (h o) -> p h o", o=1).broadcast_to([P, H, HD]),
                                           ALU.mult))
                c.wait()
                V.tensor_tensor(hacc[:, ts, :], hacc[:, ts, :], on[:], ALU.add).then_inc(h_done, 1)
                c.end()

            def ln_rest(b):
                v.wait_ge(lnA_done, b + 1)
                if not isinstance(b, int) or b:
                    v.wait_ge(lnB_done, b)
                ts = slice(2 * b, 2 * b + 2) if isinstance(b, int) else bass.ds(2 * b, 2)
                V.tensor_tensor(d16[:], hn2[:], lnA[:, ts, :], ALU.subtract).then_inc(rest_done, 1)

            layernorm(0, 0, hn1, ln1_done)
            x_lo(0)
            qk_lo_parts(0, 0, 1, qf, q_lo)
            qk_lo_parts(0, 1, 0, kf, k_lo)
            v_bias(0, 0)
            layernorm(1, 0, hn1, ln1_done)

            def one(i, p, router, front, front2):
                if front:
                    x_lo(i + 1)
                max_scores(i)
                if front:
                    qk_lo_parts(i + 1, 0, 1, qf, q_lo)
                    qk_lo_parts(i + 1, 1, 0, kf, k_lo)
                max_lo(i)
                if front:
                    v_bias(i + 1, 1 - p)
                if router:
                    silu(i - 1)
                add_attention(i)
                layernorm(i, 1, hn2, ln2_done)
                if front2:
                    layernorm(i + 2, 0, hn1, ln1_done)
                ln_rest(i)
            images(v, one)
            silu(B - 1)


def top_tokens(nc, hold, logit_dram, ident, dims):
    B, S, D, E, F, CAP = dims
    R = B * E // P
    posT = hold("posT", [P, 2, B * E], F16)
    wT = hold("wT", [P, 2, B * E, 3], BF16)
    iota = hold("slot_number", [P, CAP], F16)
    with ExitStack() as ctx:
        sb = lambda n, s, d=F32: ctx.enter_context(nc.sbuf_tensor(n, s, d))
        sem = lambda n: ctx.enter_context(nc.semaphore(n))
        L = sb("L", [P, R, S])
        wk = sb("work", [P, R, S])
        top = sb("top8", [P, R, CAP])
        nm = sb("neg_max", [P, R])
        ex = sb("ex", [P, R, S])
        Z = sb("Z", [P, R])
        sel = sb("sel", [P, R, S])
        cum = sb("cum", [P, R, S])
        pos = sb("pos", [P, R, S])
        tot = sb("tot", [P, R])
        ones = sb("ones_row", [P, CAP])
        r1 = sb("w_rest", [P, 2, B * E])
        posP = ctx.enter_context(nc.psum_tensor("pos_ps", [P, 2, B * E], F32))
        wP = ctx.enter_context(nc.psum_tensor("w_ps", [P, 2, B * E], F32))
        l_in, nm_done, ex_done, chain, pos_done, w_done, pos_ps, w_ps = (sem(n) for n in (
            "l_in", "nm_done", "ex_done", "top_chain", "pos_done", "w_done", "pos_psd", "w_psd"))
        block = ctx.enter_context(nc.Block())
        V = nc.vector

        @block.sync
        def _(sp):
            sp.dma_start(L[:], logit_dram.rearrange("(r p) s -> p r s", p=P)).then_inc(l_in, 16)

        @block.scalar
        def _(act):
            for r in range(R):
                act.wait_ge(nm_done, r + 1)
                nc.scalar.activation(ex[:, r], L[:, r], ACT.Exp, bias=nm[:, r:r + 1], accum_out=Z[:, r:r + 1]).then_inc(ex_done, 1)

        @block.tensor
        def _(pe):
            for done, src, dst, full in ((pos_done, pos, posP, pos_ps), (w_done, ex, wP, w_ps)):
                pe.wait_ge(done, R)
                for r in range(R):
                    for tt in range(2):
                        ins = pe.transpose(dst[:, tt, r * P:(r + 1) * P], src[:, r, tt * P:(tt + 1) * P], ident[:])
                ins.then_inc(full, 1)

        @block.vector
        def _(v):
            c = Chain(v, chain, 0, 0)
            c.step(V.memset(ones[:], 1.0))
            c.wait()
            c.step(V.tensor_tensor_scan(iota[:], ones[:], ones[:], 0.0, ALU.add, ALU.bypass))
            v.wait_ge(l_in, 16)
            for k in range(CAP // 8):
                for r in range(R):
                    src = (L if k == 0 else wk)[:, r]
                    if k:
                        c.wait()
                    c.step(V.max(top[:, r, 8 * k:8 * k + 8], src))
                    if k == 0:
                        c.wait()
                        V.tensor_scalar(nm[:, r:r + 1], top[:, r, 0:1], -1.0, None, ALU.mult).then_inc(nm_done, 1)
                for r in range(R):
                    src = (L if k == 0 else wk)[:, r]
                    c.wait()
                    c.step(V.match_replace(wk[:, r], top[:, r, 8 * k:8 * k + 8], src, BIG))
            c.wait()
            c.step(V.tensor_scalar(sel[:], wk[:], BIG, None, ALU.is_le))
            c.wait()
            for r in range(R):
                c.step(V.tensor_tensor_scan(cum[:, r], sel[:, r], sel[:, r], 0.0, ALU.add, ALU.bypass))
            c.wait()
            V.tensor_tensor(pos[:], cum[:], sel[:], ALU.mult).then_inc(pos_done, R)
            v.wait_ge(ex_done, R)
            c.step(V.reciprocal(Z[:], Z[:]))
            c.wait()
            for r in range(R):
                c.step(V.scalar_tensor_tensor(wk[:, r], ex[:, r], Z[:, r:r + 1], sel[:, r], ALU.mult, ALU.mult))
            c.wait()
            c.step(V.tensor_reduce(tot[:], wk[:], AX.X, ALU.add))
            c.wait()
            c.step(V.tensor_scalar(tot[:], tot[:], 1e-9, None, ALU.add))
            c.wait()
            c.step(V.reciprocal(tot[:], tot[:]))
            c.wait()
            for r in range(R):
                V.tensor_scalar(ex[:, r], wk[:, r], tot[:, r:r + 1], None, ALU.mult).then_inc(w_done, 1)
            v.wait_ge(pos_ps, 1)
            c.step(V.tensor_copy(posT[:], posP[:]))
            v.wait_ge(w_ps, 1)
            c.step(V.tensor_copy(wT[:, :, :, 0], wP[:]))
            c.wait()
            c.step(V.tensor_tensor(r1[:], wP[:], wT[:, :, :, 0], ALU.subtract))
            c.wait()
            c.step(V.tensor_copy(wT[:, :, :, 1], r1[:]))
            c.wait()
            c.step(V.tensor_tensor(r1[:], r1[:], wT[:, :, :, 1], ALU.subtract))
            c.wait()
            c.step(V.tensor_copy(wT[:, :, :, 2], r1[:]))
            c.wait()
    return posT, wT, iota


def ffn(nc, ctx, w1, w2, w3, hacc, lnA, lnB, logit_dram, ident, ident16, out, dims):
    B, S, D, E, F = dims
    CAP = -(-512 * 2 // E)
    hold = lambda n, s, d=F32: ctx.enter_context(nc.sbuf_tensor(n, s, d))
    posT, wT, iota = top_tokens(nc, hold, logit_dram, ident, (B, S, D, E, F, CAP))
    PR = E // 2
    FT = F // P
    HB = B // 2
    N = HB * CAP
    ST = N // P
    assert (FT, HB, N, CAP) == (4, 8, 512, 64)
    sb = hold
    sem = lambda n: ctx.enter_context(nc.semaphore(n))
    ps = lambda n, s, d=F32: ctx.enter_context(nc.psum_tensor(n, s, d))
    raw = [sb(f"w_raw{i}", [P, 1024]) for i in range(2)]
    Wx = [[[sb(f"w{m + 1}_{x}{i}", [P, 1024], F32R) for x in ("hi", "lo")] for m in range(3)] for i in range(2)]
    OH = [sb(f"onehot{i}", [P, 2, B, 2, CAP], F16) for i in range(2)]
    ohT = [sb(f"onehotT{i}", [P, 2, S], F32R) for i in range(2)]
    xg = [[sb(f"xg_{x}{i}", [P, 2, N], F32R) for x in ("hi", "lo")] for i in range(2)]
    sg = [sb(f"silu_g{i}", [P, N]) for i in range(2)]
    hf = [sb(f"hidden{i}", [P, N]) for i in range(2)]
    hp = [sb(f"hidden_{x}", [P, FT, N], F32R) for x in ("hi", "lo")]
    Y = [sb(f"y_{x}", [P, B, D], F32R) for x in ("hi", "lo")]
    ws = sb("slot_weight", [P, 2, HB])
    GP = [ps(f"gate_ps{i}", [P, N]) for i in range(2)]
    VP = [ps(f"value_ps{i}", [P, N]) for i in range(2)]
    YP = [ps(f"y_ps{i}", [P, 2, D]) for i in range(2)]
    XP = ps("gather_ps", [P, N])
    TP = ps("turn_ps", [P, 512])
    TP16 = TP[:, 0:256].bitcast(F16)

    zero = sb("zero_col", [P, 1])
    zeroed = sem("zeroed")
    raw_in = [sem(f"raw_in{i}") for i in range(2)]
    (wsplit, oh_done, ws_ps, ws_done, g_ps, v_ps, silu_done, hf_done, hh_done, hl_done, gath_ps, xh_done, xl_done,
     y_ps, y_hi, y_lo, comb_ps, comb_add, oht_ps, oht_done, out_done) = (sem(n) for n in (
         "wsplit", "oh_done", "slotw_ps", "slotw_done", "s_g_ps", "s_v_ps", "silu_g_done", "hf_done", "hh_done",
         "hl_done", "s_gath_ps", "xh_done", "xl_done", "s_y_ps", "y_hi_done", "y_lo_done", "comb_ps", "comb_add",
         "oht_ps", "oht_done", "out_done"))
    block = ctx.enter_context(nc.Block())
    T, A, V = nc.tensor, nc.scalar, nc.vector
    PASSES = ((0, 0), (0, 1), (1, 0))

    def pairs(eng, one):
        one(0, 0, True, False)
        with eng.Fori(1, PR - 2, 2) as pr:
            one(pr, 1, False, False)
            one(pr + 1, 0, False, False)
        one(PR - 1, 1, False, True)

    later = lambda n: not isinstance(n, int) or n > 0

    @block.sync
    def _(sp):
        def one(pr, par, first, last):
            for e2 in range(2):
                for m, w in enumerate((w1, w2, w3)):
                    n = 3 * e2 + m
                    e = 2 * pr + e2 if isinstance(pr, int) else sp.snap(2 * pr + e2)
                    src = w[e] if isinstance(pr, int) else w[bass.ds(e, 1)].rearrange("o a b -> (o a) b")
                    if not first or n >= 2:
                        sp.wait_ge(wsplit, 12 * pr + 2 * (n - 1))
                    sp.dma_start(raw[n % 2][:].rearrange("p (t c) -> p t c", c=src.shape[1]),
                                 src.rearrange("(t p) c -> p t c", p=P)).then_inc(raw_in[n % 2], 16)
        pairs(sp, one)
        for s in range(B // 2):
            sp.wait_ge(comb_add, 2 * HB * (PR - 1) + 2 * s + 2)
            sp.dma_start(out.rearrange("b (t p) d -> p (b t) d", p=P)[:, 4 * s:4 * s + 4, :],
                         hacc[:, 4 * s:4 * s + 4, :]).then_inc(out_done, 16)
        sp.wait_ge(out_done, 16 * (B // 2))

    @block.gpsimd
    def _(g):
        nc.gpsimd.memset(zero[:], 0.0).then_inc(zeroed, 1)
        g.wait_ge(zeroed, 1)

        def one(pr, par, first, last):
            for e2 in range(2):
                if not first:
                    g.wait_ge(y_ps, 2 * (4 * (pr - 1) + 2 * e2 + 2))
                for m in range(3):
                    n = 3 * e2 + m
                    g.wait_ge(raw_in[n % 2], 16 * (3 * pr + n // 2 + 1))
                    hi, lo = Wx[e2][m]
                    nc.gpsimd.tensor_tensor(hi[:], raw[n % 2][:], zero[:].broadcast_to([P, 1024]), ALU.add).then_inc(wsplit, 1)
                    g.wait_ge(wsplit, 12 * pr + 2 * n + 1)
                    nc.gpsimd.tensor_tensor(lo[:], raw[n % 2][:], hi[:].bitcast(F32), ALU.subtract).then_inc(wsplit, 1)
        pairs(g, one)

    @block.tensor
    def _(pe):
        def gather(Tn, par, e2, c, n):
            m, part = n // 2, n % 2
            if n:
                pe.wait_ge((xl_done, xh_done)[part], 2 * Tn + (n + 1) // 2)
            elif later(Tn):
                pe.wait_ge(xl_done, 2 * Tn)
            src = (lnA, lnB)[part]
            for b in range(HB):
                for tt in range(2):
                    ins = pe.matmul(XP[:, b * CAP:(b + 1) * CAP], src[:, 2 * (HB * c + b) + tt, m * P:(m + 1) * P],
                                    OH[par][:, tt, HB * c + b, e2, :], start=(tt == 0), stop=(tt == 1))
            ins.then_inc(gath_ps, 1)

        def slot_weights(pr, par):
            if later(pr):
                pe.wait_ge(oht_done, 8 * (pr - 1) + 1)
            for b in range(B):
                for tt in range(2):
                    if isinstance(pr, int):
                        w_ = wT[:, tt, b * E + 2 * pr:b * E + 2 * pr + 2, :]
                    else:
                        w_ = wT[:, tt, bass.ds(2 * pr + b * E, 2), :]
                    ins = pe.matmul(TP[:, 256 + 6 * b:256 + 6 * b + 6], OH[par][:, tt, b].rearrange("p e s -> p (e s)"),
                                    w_.rearrange("p e x -> p (e x)"), start=(tt == 0), stop=(tt == 1))
            ins.then_inc(ws_ps, 1)

        def turn_onehot(pp, par, s):
            if s or later(pp):
                pe.wait_ge(oht_done, 8 * pp + s)
            if s == 0:
                pe.wait_ge(ws_done, 4 * (pp + 1))
            for x in range(2):
                for tt in range(2):
                    ins = pe.transpose(TP16[:, x * S + tt * P:x * S + (tt + 1) * P],
                                       OH[par][:, tt, 2 * s + x].rearrange("p e s -> p (e s)"), ident16[:])
            ins.then_inc(oht_ps, 1)

        def combine(pp, s):
            pe.wait_ge(oht_done, 8 * pp + s + 1)
            for x in range(2):
                if s % 4:
                    pe.wait_ge(comb_add, 2 * HB * pp + 2 * s - 1 + x)
                for tt in range(2):
                    for y in range(2):
                        ins = pe.matmul(YP[x][:, tt, :], ohT[s % 2][:, x, tt * P:(tt + 1) * P], Y[y][:, 2 * s + x, :],
                                        start=(y == 0), stop=(y == 1))
                ins.then_inc(comb_ps, 1)

        def unit(pr, par, e2, c, first, last):
            U = 4 * pr + 2 * e2 + c
            pe.wait_ge(xh_done, 2 * (U + 1))
            pe.wait_ge(xl_done, 2 * (U + 1))
            for ft in range(FT):
                for m, bank, used, full in ((0, GP, silu_done, g_ps), (1, VP, hf_done, v_ps)):
                    if ft >= 2 or later(U):
                        pe.wait_ge(used, 4 * U + ft - 1)
                    if ft == 0 and c == 0:
                        pe.wait_ge(wsplit, 12 * pr + 6 * e2 + 2 * (m + 1))
                    n = 0
                    for kt in range(2):
                        for wi, xi in PASSES:
                            ins = pe.matmul(bank[ft % 2][:], Wx[e2][m][wi][:, kt * F + ft * P:kt * F + (ft + 1) * P],
                                            xg[c][xi][:, kt, :], start=(n == 0), stop=(n == 5))
                            n += 1
                    ins.then_inc(full, 1)
                if c == 0:
                    gather(U + 1, par, e2, 1, ft)
                elif e2 == 0:
                    gather(U + 1, par, 1, 0, ft)
                elif not last:
                    if ft == 0:
                        pe.wait_ge(oh_done, 2 * (pr + 2))
                    gather(U + 1, 1 - par, 0, 0, ft)
                if e2 == 0 and not first:
                    s = 4 * c + ft
                    if ft == 0:
                        pe.wait_ge(y_lo, 8 * U)
                    combine(pr - 1, s)
                    if s + 1 < 8:
                        if s == 0:
                            pe.wait_ge(ws_done, 4 * (pr + 1))
                        turn_onehot(pr - 1, 1 - par, s + 1)
            if e2 == 0 and not first:
                pe.wait_ge(comb_add, 2 * HB * (pr - 1) + 8 * (c + 1))
            elif later(U):
                pe.wait_ge(y_lo, 8 * U)
            if c == 0:
                pe.wait_ge(wsplit, 12 * pr + 6 * e2 + 6)
            for ft in range(FT):
                pe.wait_ge(hl_done, 4 * U + ft + 1)
                for st in range(ST):
                    for q, (hi_, wi) in enumerate(PASSES):
                        ins = pe.matmul(YP[st // 2][:, st % 2, :], hp[hi_][:, ft, st * P:(st + 1) * P],
                                        Wx[e2][2][wi][:, ft * D:(ft + 1) * D], start=(ft == 0 and st % 2 == 0 and q == 0),
                                        stop=(ft == FT - 1 and q == 2), skip_group_check=True)
                    if ft == FT - 1 and st % 2 == 1:
                        ins.then_inc(y_ps, 1)

        def one(pr, par, first, last):
            if first:
                pe.wait_ge(oh_done, 2)
                for n in range(4):
                    gather(0, 0, 0, 0, n)
            slot_weights(pr, par)
            for e2 in range(2):
                for c in range(2):
                    unit(pr, par, e2, c, first, last)
            turn_onehot(pr, par, 0)
        pairs(pe, one)
        for s in range(8):
            if s == 0:
                pe.wait_ge(y_lo, 8 * 4 * PR)
            elif s == 4:
                pe.wait_ge(comb_add, 2 * HB * (PR - 1) + 8)
            combine(PR - 1, s)
            if s < 7:
                turn_onehot(PR - 1, 1, s + 1)

    @block.scalar
    def _(act):
        def x_hi(Tn, c, m):
            act.wait_ge(gath_ps, 4 * Tn + 2 * m + 1)
            A.activation(xg[c][0][:, m, :], XP[:], ACT.Copy).then_inc(xh_done, 1)

        def turned(pp, s):
            act.wait_ge(oht_ps, 8 * pp + s + 1)
            A.activation(ohT[s % 2][:], TP16.rearrange("p (x t) -> p x t", x=2), ACT.Copy).then_inc(oht_done, 1)

        def hidden_hi(U, ft):
            act.wait_ge(hf_done, 4 * U + ft + 1)
            A.activation(hp[0][:, ft, :], hf[ft % 2][:], ACT.Copy).then_inc(hh_done, 1)

        def unit(pr, e2, c, first, last):
            U = 4 * pr + 2 * e2 + c
            for ft in range(FT):
                act.wait_ge(g_ps, 4 * U + ft + 1)
                if ft >= 2 or later(U):
                    act.wait_ge(hf_done, 4 * U + ft - 1)
                A.activation(sg[ft % 2][:], GP[ft % 2][:], ACT.Silu).then_inc(silu_done, 1)
                if ft:
                    hidden_hi(U, ft - 1)
                if ft % 2 == 0 and not (last and e2 and c):
                    x_hi(U + 1, 1 - c, ft // 2)
                if e2 == 0 and not first and 4 * c + ft + 1 < 8:
                    turned(pr - 1, 4 * c + ft + 1)
            hidden_hi(U, FT - 1)
            for st in range(ST):
                if st % 2 == 0:
                    act.wait_ge(y_ps, 2 * U + st // 2 + 1)
                if st == 0:
                    act.wait_ge(ws_done, 4 * (pr + 1))
                for b2 in range(2):
                    r, o = 64 * b2, 64 * e2
                    A.activation(Y[0][o:o + 64, HB * c + 2 * st + b2, :], YP[st // 2][r:r + 64, st % 2, :], ACT.Copy,
                                 scale=ws[r:r + 64, e2, (HB // 2) * c + st:(HB // 2) * c + st + 1]).then_inc(y_hi, 1)

        def one(pr, par, first, last):
            if first:
                for m in range(2):
                    x_hi(0, 0, m)
            for e2 in range(2):
                for c in range(2):
                    unit(pr, e2, c, first, last)
            turned(pr, 0)
        pairs(act, one)
        for s in range(1, 8):
            turned(PR - 1, s)

    @block.vector
    def _(v):
        def onehot(pr, par):
            for tt in range(2):
                p_ = posT[:, tt, :].rearrange("p (b e o) -> p b e o", e=E, o=1)
                p_ = p_[:, :, 2 * pr:2 * pr + 2] if isinstance(pr, int) else p_[:, :, bass.ds(2 * pr, 2)]
                V.tensor_tensor(OH[par][:, tt], iota[:].rearrange("p (b e s) -> p b e s", b=1, e=1).broadcast_to([P, B, 2, CAP]),
                                p_.broadcast_to([P, B, 2, CAP]), ALU.is_equal).then_inc(oh_done, 1)

        def slot_weights(pr):
            v.wait_ge(ws_ps, pr + 1)
            if later(pr):
                v.wait_ge(y_hi, 32 * pr)
                v.wait_ge(y_lo, 32 * pr)
            for e2 in range(2):
                src = TP[64 * e2:64 * e2 + 64, 256:256 + 6 * B].rearrange("p (b two e x) -> p two e b x", two=2, e=2, x=3)
                for b2 in range(2):
                    V.tensor_reduce(ws[64 * b2:64 * b2 + 64, e2, :], src[:, b2, e2], AX.X, ALU.add).then_inc(ws_done, 1)

        def x_lo(Tn, c, m):
            v.wait_ge(gath_ps, 4 * Tn + 2 * m + 2)
            V.tensor_scalar(xg[c][1][:, m, :], XP[:], 1.0 / 2048, None, ALU.mult).then_inc(xl_done, 1)

        def hidden_lo(U, ft):
            v.wait_ge(hh_done, 4 * U + ft + 1)
            V.tensor_tensor(hp[1][:, ft, :], hf[ft % 2][:], hp[0][:, ft, :].bitcast(F32), ALU.subtract).then_inc(hl_done, 1)

        def add(pp, s):
            for x in range(2):
                b = 2 * s + x
                v.wait_ge(comb_ps, 2 * HB * pp + b + 1)
                V.tensor_tensor(hacc[:, 2 * b:2 * b + 2, :], YP[x][:], hacc[:, 2 * b:2 * b + 2, :], ALU.add).then_inc(comb_add, 1)

        def unit(pr, par, e2, c, first, last):
            U = 4 * pr + 2 * e2 + c
            for ft in range(FT):
                v.wait_ge(silu_done, 4 * U + ft + 1)
                v.wait_ge(v_ps, 4 * U + ft + 1)
                if ft >= 2:
                    v.wait_ge(hh_done, 4 * U + ft - 1)
                if ft >= 2 or later(U):
                    v.wait_ge(hl_done, 4 * U + ft - 1)
                V.tensor_tensor(hf[ft % 2][:], sg[ft % 2][:], VP[ft % 2][:], ALU.mult).then_inc(hf_done, 1)
                if ft:
                    hidden_lo(U, ft - 1)
                if ft % 2 and not (last and e2 and c):
                    x_lo(U + 1, 1 - c, ft // 2)
                if e2 == 0 and not first:
                    add(pr - 1, 4 * c + ft)
            hidden_lo(U, FT - 1)
            if e2 == 1 and c == 0 and not last:
                onehot(pr + 1, 1 - par)
            for st in range(ST):
                for b2 in range(2):
                    r, o = 64 * b2, 64 * e2
                    b = HB * c + 2 * st + b2
                    if st % 2 == 0 and b2 == 0:
                        v.wait_ge(y_hi, 8 * U + 2 * st + 4)
                    V.scalar_tensor_tensor(Y[1][o:o + 64, b, :], YP[st // 2][r:r + 64, st % 2, :],
                                           ws[r:r + 64, e2, (HB // 2) * c + st:(HB // 2) * c + st + 1],
                                           Y[0][o:o + 64, b, :].bitcast(F32), ALU.mult, ALU.subtract).then_inc(y_lo, 1)

        def one(pr, par, first, last):
            if first:
                onehot(0, 0)
                for m in range(2):
                    x_lo(0, 0, m)
            slot_weights(pr)
            for e2 in range(2):
                for c in range(2):
                    unit(pr, par, e2, c, first, last)
        pairs(v, one)
        for s in range(8):
            add(PR - 1, s)


_INS = ["x", "L0_tok_Wa", "L0_tok_ba", "L0_tok_Wd1", "L0_tok_bd1", "L0_tok_Wd2", "L0_tok_bd2", "L0_tok_Wd3", "L0_tok_bd3",
        "L0_attn_Wq", "L0_attn_bq", "L0_attn_Wk", "L0_attn_bk", "L0_attn_Wv", "L0_attn_bv", "L0_ffn_router_w1",
        "L0_ffn_router_w2", "L0_ffn_w1", "L0_ffn_w2", "L0_ffn_w3"]


def kernel(**inputs):
    import numpy as _np
    import concourse.bacc as _bacc
    from concourse.bass_utils import run_bass_kernel_spmd as _run

    nc = _bacc.Bacc("TRN2", target_bir_lowering=False, num_devices=1, dynamic_dma_scratch_size=1024)
    arrays, args = {}, []
    for name in _INS:
        a = _np.ascontiguousarray(inputs[name])
        arrays[f"in_{name}"] = a
        args.append(nc.dram_tensor(f"in_{name}", a.shape, mybir.dt.from_np(a.dtype), kind="ExternalInput").ap())
    shape = inputs["x"].shape[:3]
    args.append(nc.dram_tensor("out_0", shape, F32, kind="ExternalOutput").ap())
    build_program(nc, *args)
    r = _run(nc, [arrays], core_ids=[0])
    return r.results[0]["out_0"]
```

```python
import math
from contextlib import ExitStack

import concourse.bass as bass
from concourse import mybir

ALU = mybir.AluOpType
ACT = mybir.ActivationFunctionType
AX = mybir.AxisListType
F32 = mybir.dt.float32
F32R = mybir.dt.float32r
F16 = mybir.dt.float16
BF16 = mybir.dt.bfloat16
I32 = mybir.dt.int32

P = 128
BIG = -3.0e38
EPS = 1e-5


class Chain:

    def __init__(self, eng, sem, per, run):
        self.eng, self.sem, self.per, self.base, self.n = eng, sem, per, run * per, 0

    def step(self, ins):
        ins.then_inc(self.sem, 1)
        self.n += 1

    def wait(self):
        self.eng.wait_ge(self.sem, self.base + self.n)

    def end(self):
        assert self.n == self.per, (self.n, self.per)


def build_program(nc, x, Wa, ba, Wd1, bd1, Wd2, bd2, Wd3, bd3, Wq, bq, Wk, bk, Wv, bv, rw1, rw2, w1, w2, w3, out):
    B, S, D, _ = x.shape
    H, HD, _ = Wq.shape
    E, _, F = w1.shape
    RH = rw1.shape[1]
    TT = S // P
    KT = D // P
    NT = B * TT
    J = H // 2
    CAP = -(-512 * 2 // E)
    IT = 4
    G = S // 8
    assert (P, KT, TT, H * HD, RH, IT * G) == (128, 2, 2, D, 128, P)

    h_dram = nc.dram_tensor("h_scratch", [B * S, D], F32, kind="Internal").ap()
    q_dram = nc.dram_tensor("q_scratch", [2, 2, KT * P, S], F32, kind="Internal").ap()
    k_dram = nc.dram_tensor("k_scratch", [2, 2, KT * P, S], F32, kind="Internal").ap()

    rh_dram = nc.dram_tensor("router_scratch", [P, B * S], F32, kind="Internal").ap()
    assert J * 2 * S == B * S

    with ExitStack() as ctx:
        sb = lambda n, s, d=F32: ctx.enter_context(nc.sbuf_tensor(n, s, d))
        hacc = sb("hacc", [P, NT + TT, D])
        lnA = sb("lnA", [P, NT, D], F16)
        lnB = sb("lnB", [P, NT, D], F16)
        ident = sb("ident", [P, P])
        ident16 = sb("ident16", [P, P], F16)
        identb = sb("identb", [P, P], BF16)

        small = sb("small", [P, 1024])
        posT = small[:, 0:B * E].bitcast(F16).rearrange("p (t c) -> p t c", t=2)
        wT = small[:, B * E:4 * B * E].bitcast(BF16).rearrange("p (t c x) -> p t c x", t=2, x=3)
        iota = sb("slot_number", [P, CAP], F16)

        with ExitStack() as mid:
            sbm = lambda n, s, d=F32: mid.enter_context(nc.sbuf_tensor(n, s, d))
            WT = {}
            for m in "qkv":
                WT[m] = [sbm(f"W{m}T_hi", [P, KT, D], F32R), sbm(f"W{m}T_lo", [P, KT, D], F32R)]
            maskS = sbm("maskS", [P, 1, P], BF16)
            maskT = sbm("maskT", [P, 1, P], BF16)
            tokenizer(nc, x, Wa, ba, [Wd1, Wd2, Wd3], [bd1, bd2, bd3], Wq, Wk, Wv, WT, hacc, h_dram,
                      ident, ident16, identb, maskS, maskT)
            QS0 = sbm("q_stack0", [P, J, 2, S], F32R)
            rh = QS0[:].rearrange("p j a q -> p (j a q)").bitcast(F32)
            attention(nc, bq, bk, bv, rw1, WT, hacc, lnA, lnB, QS0, small, rh, q_dram, k_dram, rh_dram, ident, identb,
                      maskS, maskT, (B, S, D, H, HD, E))
            top_tokens(nc, rh, rw2, posT, wT, iota, ident, (B, S, D, E, F, CAP))
        ffn(nc, ctx, w1, w2, w3, hacc, lnA, lnB, posT, wT, iota, ident16, out, (B, S, D, E, F, CAP))


def tokenizer(nc, x, Wa, ba, Wd, bd, Wq, Wk, Wv, WT, hacc, h_dram, ident, ident16, identb, maskS, maskT):
    B, S, D, _ = x.shape
    IT, G = 4, S // 8
    NTL = B // IT
    with ExitStack() as ctx:
        sb = lambda n, s, d=F32: ctx.enter_context(nc.sbuf_tensor(n, s, d))
        sem = lambda n: ctx.enter_context(nc.semaphore(n))
        X = [sb(f"x_tile{i}", [P, 8, D]) for i in range(2)]
        Y = [sb(f"rec_tile{i}", [P, 8, D]) for i in range(2)]
        su = sb("col_sum", [P, 8, D // 2])
        di = sb("col_dif", [P, 8, D // 2])
        band = [sb(f"band{l}", [P, 3, 8 >> l, D >> l]) for l in (1, 2, 3)]
        low = [sb(f"low{l}", [P, 8 >> l, D >> l]) for l in (1, 2, 3)]
        vs = sb("v_scaled", [P, 4, D // 2])
        junk = sb("junk", [P, 3, 4 * D // 2])
        wlev = [sb(f"wband{l}", [P, 3, (8 >> l) * (D >> l) * 3]) for l in (1, 2, 3)]
        wlow = sb("wlow", [P, D // 8])
        wraw = sb("wraw", [P, 3, 2, D])
        part = sb("part", [P, 10])
        bias = sb("bias", [P, 10])
        gsc = sb("gate_scale", [P, 10])
        osc = sb("out_scale", [P, 10])
        z = sb("z", [P, 10])
        ez = sb("ez", [P, 10])
        m3 = sb("m3", [P, 3])
        s4 = sb("s4", [P, 4])
        gate = sb("gate", [P, 10])
        ngate = sb("ngate", [P, 10])
        blk = sb("same_image", [P, P])
        zsum = ctx.enter_context(nc.psum_tensor("zsum", [P, 512], F32))
        wps = [ctx.enter_context(nc.psum_tensor(f"w_ps{i}", [P, 2, D], F32)) for i in range(3)]

        x_in = [sem(f"x_in{i}") for i in range(2)]
        w_in = sem("w_in")
        wqkv_in = sem("wqkv_in")
        x_used = sem("x_used")
        const0 = sem("const0")
        const_done = sem("const_done")
        part_done = sem("part_done")
        z_ready = sem("z_ready")
        arg_ready = sem("arg_ready")
        exp_ready = sem("exp_ready")
        rec_done = sem("rec_done")
        rec_out = [sem(f"rec_out{i}") for i in range(2)]
        h_in = sem("h_in")
        h_zero = sem("h_zero")
        tc = sem("tok_chain")
        wt_ps = sem("wt_ps")
        wt_hi = sem("wt_hi")
        wt_lo = sem("wt_lo")

        xv = x.rearrange("b (g i) w c -> (b g) (i w c)", i=8)
        hv = h_dram.rearrange("(p i) w -> p (i w)", i=8)
        block = ctx.enter_context(nc.Block())
        NW = 4 * 4 + 4

        @block.sync
        def _(sp):
            sp.dma_start(X[0][:].rearrange("p i w -> p (i w)"), xv[0:P]).then_inc(x_in[0], 16)
            n = 0
            for l in (1, 2, 3):
                w = Wd[3 - l].rearrange("(c g k) o -> g c (k o)", c=3, g=G)
                for b in range(IT):
                    sp.dma_start(wlev[l - 1][b * G:(b + 1) * G], w).then_inc(w_in, 16)
                    n += 1
            for b in range(IT):
                sp.dma_start(wlow[b * G:(b + 1) * G], Wa.rearrange("(g k) o -> g (k o)", g=G)).then_inc(w_in, 16)
                n += 1
            for c0, c1, v in ((0, 1, ba), (1, 4, bd[0]), (4, 7, bd[1]), (7, 10, bd[2])):
                sp.dma_start(bias[:, c0:c1], v.rearrange("(a c) -> a c", a=1).broadcast_to([P, c1 - c0])).then_inc(w_in, 16)
                n += 1
            assert n == NW
            sp.dma_start(X[1][:].rearrange("p i w -> p (i w)"), xv[P:2 * P]).then_inc(x_in[1], 16)
            for i, w in enumerate((Wq, Wk, Wv)):
                sp.dma_start(wraw[:, i], w.rearrange("(t g) d e -> (g d) t e", t=2)).then_inc(wqkv_in, 16)
            for t in range(NTL):
                sp.wait_ge(rec_done, t + 1)
                sp.dma_start(hv[t * P:(t + 1) * P], Y[t % 2][:].rearrange("p i w -> p (i w)")).then_inc(rec_out[t % 2], 16)
                if t + 2 < NTL:
                    sp.dma_start(X[t % 2][:].rearrange("p i w -> p (i w)"), xv[(t + 2) * P:(t + 3) * P]).then_inc(x_in[t % 2], 16)
                sp.wait_ge(rec_out[t % 2], 16 * (t // 2 + 1))
                sp.dma_start(hacc[:, 8 * t:8 * t + 8, :],
                             h_dram.rearrange("(n p) w -> p n w", p=P)[:, 8 * t:8 * t + 8, :]).then_inc(h_in, 16)
            sp.wait_ge(h_in, 16 * NTL)

        @block.gpsimd
        def _(g):
            nc.gpsimd.memset(ident[:], 0.0).then_inc(const0, 1)
            nc.gpsimd.memset(maskS[:], 0.0).then_inc(const0, 1)
            nc.gpsimd.memset(maskT[:], 0.0).then_inc(const0, 1)
            nc.gpsimd.memset(blk[:], 0.0).then_inc(const0, 1)
            g.wait_ge(const0, 4)
            nc.gpsimd.affine_select(out=ident[:], in_=ident[:], compare_op=ALU.not_equal, fill=1.0, base=0,
                                    pattern=[[-1, P]], channel_multiplier=1).then_inc(const_done, 1)
            nc.gpsimd.affine_select(out=maskS[:], in_=maskS[:], compare_op=ALU.is_ge, fill=BIG, base=0,
                                    pattern=[[0, 1], [-1, P]], channel_multiplier=1).then_inc(const_done, 1)
            nc.gpsimd.affine_select(out=maskT[:], in_=maskT[:], compare_op=ALU.is_ge, fill=BIG, base=0,
                                    pattern=[[0, 1], [1, P]], channel_multiplier=-1).then_inc(const_done, 1)
            g.wait_ge(const_done, 3)
            for b in range(IT):
                nc.gpsimd.memset(blk[b * G:(b + 1) * G, b * G:(b + 1) * G], 1.0).then_inc(const_done, 1)
            g.wait_ge(const_done, 3 + IT)
            nc.gpsimd.tensor_copy(ident16[:], ident[:]).then_inc(const_done, 1)
            nc.gpsimd.tensor_copy(identb[:], ident[:]).then_inc(const_done, 1)

        @block.tensor
        def _(pe):
            pe.wait_ge(const_done, 5 + IT)
            pe.wait_ge(wqkv_in, 48)
            for i in range(3):
                for ft in range(2):
                    for kt in range(2):
                        ins = pe.transpose(wps[i][:, kt, ft * P:(ft + 1) * P], wraw[:, i, ft, kt * P:(kt + 1) * P], ident[:])
                ins.then_inc(wt_ps, 1)
            for t in range(NTL):
                pe.wait_ge(part_done, t + 1)
                if t:
                    pe.wait_ge(z_ready, t)
                pe.matmul(zsum[:, 0:10], blk[:], part[:], start=True, stop=True).then_inc(arg_ready, 1)

        @block.scalar
        def _(act):
            for i, m in enumerate("qkv"):
                act.wait_ge(wt_ps, i + 1)
                nc.scalar.activation(WT[m][0][:], wps[i][:], ACT.Copy).then_inc(wt_hi, 1)
            for t in range(NTL):
                act.wait_ge(z_ready, t + 1)
                nc.scalar.activation(ez[:], z[:], ACT.Exp).then_inc(exp_ready, 1)

        @block.vector
        def _(v):
            nc.vector.memset(hacc[:, 2 * B:, :], 0.0).then_inc(h_zero, 1)
            v.wait_ge(const0, 4)
            c = Chain(v, tc, 0, 0)
            for a, b_, g_, o_ in ((0, 4, 0.125, 1 / 64), (4, 7, 0.25, 1 / 16), (7, 10, 0.5, 1 / 4)):
                c.step(nc.vector.memset(gsc[:, a:b_], g_))
                c.step(nc.vector.memset(osc[:, a:b_], o_))
            V = nc.vector
            for t in range(NTL):
                p = t % 2
                v.wait_ge(x_in[p], 16 * (t // 2 + 1))
                src = X[p]
                for l in range(3):
                    R, C = 8 >> l, D >> l
                    s_, d_ = su[:, 0:R, 0:C // 2], di[:, 0:R, 0:C // 2]
                    pr = src[:].rearrange("p r (c two) -> p r c two", two=2)
                    c.wait()
                    c.step(V.tensor_tensor(s_, pr[:, :, :, 0], pr[:, :, :, 1], ALU.add))
                    c.step(V.tensor_tensor(d_, pr[:, :, :, 0], pr[:, :, :, 1], ALU.subtract))
                    c.wait()
                    sp_ = s_.rearrange("p (r two) c -> p r two c", two=2)
                    dp_ = d_.rearrange("p (r two) c -> p r two c", two=2)
                    c.step(V.tensor_tensor(low[l][:], sp_[:, :, 0], sp_[:, :, 1], ALU.add))
                    c.step(V.tensor_tensor(band[l][:, 0], sp_[:, :, 0], sp_[:, :, 1], ALU.subtract))
                    c.step(V.tensor_tensor(band[l][:, 1], dp_[:, :, 0], dp_[:, :, 1], ALU.add))
                    c.step(V.tensor_tensor(band[l][:, 2], dp_[:, :, 0], dp_[:, :, 1], ALU.subtract))
                    src = low[l]
                c.wait()
                if t == 0:
                    v.wait_ge(w_in, 16 * NW)
                if t:
                    v.wait_ge(arg_ready, t)
                c.step(V.tensor_tensor_reduce(junk[:, 0, 0:D // 8], low[2][:, 0, :], wlow[:], 1.0, 0.0, ALU.mult, ALU.add, part[:, 0:1]))
                for l in (3, 2, 1):
                    n = (8 >> l) * (D >> l)
                    wv_ = wlev[l - 1][:].rearrange("p c (k o) -> p o c k", o=3)
                    for o in range(3):
                        c.wait()
                        col = 1 + 3 * (3 - l) + o
                        c.step(V.tensor_tensor_reduce(junk[:, :, 0:n], band[l - 1][:].rearrange("p c r w -> p c (r w)"), wv_[:, o],
                                                      1.0, 0.0, ALU.mult, ALU.add, part[:, col:col + 1]))
                c.wait()
                V.tensor_copy(z[:], part[:]).then_inc(part_done, 1)
                c.n += 0
                v.wait_ge(arg_ready, t + 1)
                v.wait_ge(part_done, t + 1)
                c.step(V.tensor_tensor(z[:], zsum[:, 0:10], gsc[:], ALU.mult))
                c.wait()
                c.step(V.tensor_tensor(z[:], z[:], bias[:], ALU.add))
                c.wait()
                z3 = z[:, 1:10].rearrange("p (l o) -> p l o", o=3)
                c.step(V.tensor_reduce(m3[:], z3, AX.X, ALU.max))
                c.step(V.tensor_scalar(z[:, 0:1], z[:, 0:1], -1.0, 88.0, ALU.mult, ALU.min))
                c.wait()
                V.tensor_tensor(z3, z3, m3[:].rearrange("p (l o) -> p l o", o=1).broadcast_to([P, 3, 3]), ALU.subtract).then_inc(z_ready, 1)
                v.wait_ge(exp_ready, t + 1)
                e3 = ez[:, 1:10].rearrange("p (l o) -> p l o", o=3)
                c.step(V.tensor_reduce(s4[:, 1:4], e3, AX.X, ALU.add))
                c.step(V.tensor_scalar(s4[:, 0:1], ez[:, 0:1], 1.0, None, ALU.add))
                c.wait()
                c.step(V.reciprocal(s4[:], s4[:]))
                c.wait()
                c.step(V.tensor_tensor(gate[:, 1:10].rearrange("p (l o) -> p l o", o=3), e3,
                                       s4[:, 1:4].rearrange("p (l o) -> p l o", o=1).broadcast_to([P, 3, 3]), ALU.mult))
                c.step(V.tensor_copy(gate[:, 0:1], s4[:, 0:1]))
                c.wait()
                c.step(V.tensor_tensor(gate[:], gate[:], osc[:], ALU.mult))
                c.wait()
                c.step(V.tensor_scalar(ngate[:], gate[:], -1.0, None, ALU.mult))
                c.step(V.tensor_scalar(low[2][:], low[2][:], gate[:, 0:1], None, ALU.mult))
                if t >= 2:
                    v.wait_ge(rec_out[p], 16 * (t // 2))
                for l in (2, 1, 0):
                    R, C = 8 >> (l + 1), D >> (l + 1)
                    g0 = 1 + 3 * (2 - l)
                    sp_ = su[:, 0:2 * R, 0:C].rearrange("p (r two) c -> p r two c", two=2)
                    dp_ = di[:, 0:2 * R, 0:C].rearrange("p (r two) c -> p r two c", two=2)
                    vv = vs[:, 0:R, 0:C]
                    c.wait()
                    c.step(V.scalar_tensor_tensor(sp_[:, :, 0], band[l][:, 0], gate[:, g0:g0 + 1], low[l][:], ALU.mult, ALU.add))
                    c.step(V.scalar_tensor_tensor(sp_[:, :, 1], band[l][:, 0], ngate[:, g0:g0 + 1], low[l][:], ALU.mult, ALU.add))
                    c.step(V.tensor_scalar(vv, band[l][:, 1], gate[:, g0 + 1:g0 + 2], None, ALU.mult))
                    c.wait()
                    c.step(V.scalar_tensor_tensor(dp_[:, :, 0], band[l][:, 2], gate[:, g0 + 2:g0 + 3], vv, ALU.mult, ALU.add))
                    c.step(V.scalar_tensor_tensor(dp_[:, :, 1], band[l][:, 2], ngate[:, g0 + 2:g0 + 3], vv, ALU.mult, ALU.add))
                    c.wait()
                    dst = (low[l - 1] if l else Y[p])[:].rearrange("p r (c two) -> p r c two", two=2)
                    a_, b_ = su[:, 0:2 * R, 0:C], di[:, 0:2 * R, 0:C]
                    c.step(V.tensor_tensor(dst[:, :, :, 0], a_, b_, ALU.add))
                    if l:
                        c.step(V.tensor_tensor(dst[:, :, :, 1], a_, b_, ALU.subtract))
                    else:
                        c.wait()
                        V.tensor_tensor(dst[:, :, :, 1], a_, b_, ALU.subtract).then_inc(rec_done, 1)
                v.wait_ge(rec_done, t + 1)
                if t < 3:
                    m = "qkv"[t]
                    v.wait_ge(wt_hi, t + 1)
                    c.step(V.tensor_tensor(WT[m][1][:], wps[t][:], WT[m][0][:].bitcast(F32), ALU.subtract))


def attention(nc, bq, bk, bv, rw1, WT, hacc, lnA, lnB, QS0, small, rh, q_dram, k_dram, rh_dram, ident, identb,
              maskS, maskT, dims):
    B, S, D, H, HD, E = dims
    J = H // 2
    NB = 12
    with ExitStack() as ctx:
        sb = lambda n, s, d=F32: ctx.enter_context(nc.sbuf_tensor(n, s, d))
        sem = lambda n: ctx.enter_context(nc.semaphore(n))
        ps = lambda n, s, d=F32: ctx.enter_context(nc.psum_tensor(n, s, d))
        hn1 = sb("hn1", [P, 2, D])
        hn2 = sb("hn2", [P, 2, D])
        xT = [sb("xT_hi", [P, 2, S], F32R), sb("xT_lo", [P, 2, S], F32R)]
        qf = [sb("q_hi", [P, 2, S], F32R), sb("q_lo", [P, 2, S], F32R)]
        kf = [sb("k_hi", [P, 2, S], F32R), sb("k_lo", [P, 2, S], F32R)]
        QS = [QS0, sb("q_stack1", [P, J, 2, S], F32R)]
        KS = [sb(f"k_stack{i}", [P, J, S], F32R) for i in range(2)]
        VW = 3 * HD + 1
        V1 = [sb(f"v_ones{i}", [P, 2, H, VW], BF16) for i in range(4)]
        PT0 = [[sb(f"probs_k0_{x}_{i}", [P, H, S], F16) for x in range(2)] for i in range(2)]
        PT1 = [[sb(f"probs_k1_{x}_{i}", [P, H, P], F16) for x in range(2)] for i in range(2)]
        pf = [sb(f"probs_full{i}", [P, 512]) for i in range(3)]
        shift = sb("log_2048", [P, 1])
        mx = sb("row_max", [P, 2, H])
        mT = [sb("negmax_hi", [H, S], F32R), sb("negmax_lo", [H, S], F32R)]
        rden = sb("rden", [P, H // 2])
        on = sb("attn_norm", [P, 2, D])
        bqk = sb("bqk", [P, 2, 2])
        bvb = sb("bv_bcast", [P, D])
        rw1s = sb("rw1s", [P, 2, P])
        tick = sb("tick", [P, 2])
        padding = sb("pad_steps", [P, 32])
        st = sb("stats", [P, 4, 6])
        mv = sb("mean_var", [P, 4, 2])
        rs = sb("rstd", [P, 4, 4])
        hn2T = sb("hn2T", [P, 2, S])
        vf = small[:, 0:512].rearrange("p (t d) -> p t d", t=2)
        osum = small[:, 512:640].rearrange("p (h d) -> p h d", d=HD)
        rh_buf = small[:, 640:640 + S]
        SR = [ps(f"scores_ps{i}", [P, 512]) for i in range(2)]
        TR = [ps(f"scoresT_ps{i}", [P, 512]) for i in range(2)]
        OP = [ps(f"out_ps{i}", [P, 512]) for i in range(2)]
        M = [ps(f"mix_ps{i}", [P, 2, 256]) for i in range(2)]

        (c_in, filled, chain, ln1_done, ln2_done, xT_ps, xT_hi, xT_lo, q_ps, k_ps, v_ps, qk_hi, q_lo, k_lo, v_done,
         qk_written, stack_in, s_ps, s_max, m_ps, m_hi, m_lo, m_in, st_ps, exp_done, pa_done, pb_done, o_ps, o_left, o_done,
         v_sum, v_hi, v_rest, v_mid,
         h_done, lnA_done, rest_done, lnB_done, hT_ps, hT_done, rh_ps, rh_done, router_dma) = (sem("a_" + n) for n in (
             "c_in", "filled", "chain", "ln1_done", "ln2_done", "xT_ps", "xT_hi", "xT_lo", "q_ps", "k_ps", "v_ps",
             "qk_hi", "q_lo", "k_lo", "v_done", "qk_written", "stack_in", "s_ps", "s_max", "m_ps", "m_hi", "m_lo",
             "m_in", "st_ps", "exp_done", "pa_done", "pb_done", "o_ps", "o_left", "o_done",
             "v_sum", "v_hi", "v_rest", "v_mid", "h_done", "lnA_done", "rest_done",
             "lnB_done", "hT_ps", "hT_done", "rh_ps", "rh_done", "router_dma"))
        block = ctx.enter_context(nc.Block())
        A, V = nc.scalar, nc.vector

        def turns(eng, one):
            for i in range(-3, 2):
                one(i, i % 4)
            with eng.Fori(2, B - 5, 4) as i:
                for y in range(4):
                    one(i + y, (2 + y) % 4)
            for i in range(B - 2, B + 2):
                one(i, i % 4)

        banks_of = [[], []] + [[0, 1], [2, 3]] + [[n] for n in range(4, NB)]
        has = lambda i, d: not isinstance(i, int) or 0 <= i + d < B
        tiles = lambda b: slice(2 * b, 2 * b + 2) if isinstance(b, int) else bass.ds(2 * b, 2)

        def v_part(y, x):
            return V1[(y + 2) % 4][:, :, :, x * HD:(x + 1) * HD]

        def probs(p, x, n):
            g, y = n // 3, n % 3
            return PT1[p][x][:, 4 * g:4 * g + 4, :] if y == 2 else PT0[p][x][:, 4 * g + 2 * y:4 * g + 2 * y + 2, :]

        @block.gpsimd
        def _(g):
            def one(i, y):
                if has(i, 0):
                    for n in range(NB):
                        g.wait_ge(pa_done, NB * i + n + 1)
                        heads = 4 if n % 3 == 2 else 2
                        nc.gpsimd.tensor_tensor(probs(y % 2, 1, n), pf[n % 3][:].rearrange("p (a q) -> p a q", a=heads),
                                                probs(y % 2, 0, n), ALU.subtract).then_inc(pb_done, 1)
            turns(g, one)

        @block.sync
        def _(sp):
            with nc.allow_non_contiguous_dma(reason="biases, once"):
                sp.dma_start(bqk[:, 0, :], bq.rearrange("(t g) d -> (g d) t", t=2)).then_inc(c_in, 16)
                sp.dma_start(bqk[:, 1, :], bk.rearrange("(t g) d -> (g d) t", t=2)).then_inc(c_in, 16)
            sp.dma_start(bvb[:], bv.rearrange("(o h) d -> o (h d)", o=1).broadcast_to([P, D])).then_inc(c_in, 16)
            sp.dma_start(rw1s[:], rw1.rearrange("(t p) n -> p t n", p=P)).then_inc(router_dma, 16)
            sp.wait_ge(filled, 10)

            def one(i, y):
                p = y % 2
                if has(i, 2):
                    b = i + 2
                    sp.wait_ge(q_lo, 2 * (b + 1))
                    for x in range(2):
                        sp.dma_start(q_dram[p, x].rearrange("(f p) q -> p f q", p=P), qf[x][:].bitcast(F32)).then_inc(qk_written, 16)
                    sp.wait_ge(k_lo, 2 * (b + 1))
                    sp.dma_start(k_dram[p, 0].rearrange("(f p) q -> p f q", p=P), kf[0][:].bitcast(F32)).then_inc(qk_written, 16)
                    if has(i, 0):
                        sp.wait_ge(st_ps, NB * (i + 1))
                    sp.dma_start(k_dram[p, 1].rearrange("(f p) q -> p f q", p=P), kf[1][:].bitcast(F32)).then_inc(qk_written, 16)
                    sp.wait_ge(qk_written, 64 * (b + 1))
                    for a in range(2):
                        for t, (xq, xk) in enumerate(((0, 0), (1, 0), (0, 1))):
                            r = 48 * a + 16 * t
                            qsrc = q_dram[p, xq].rearrange("(j a d) q -> a d j q", a=2, d=HD)[a]
                            ksrc = k_dram[p, xk].rearrange("(j a d) q -> a d j q", a=2, d=HD)[a]
                            sp.dma_start(QS[p][r:r + HD, :, a, :].bitcast(F32), qsrc).then_inc(stack_in, 16)
                            sp.dma_start(KS[p][r:r + HD, :, :].bitcast(F32), ksrc).then_inc(stack_in, 16)
                if has(i, 1):
                    sp.wait_ge(m_lo, i + 2)
                    for a in range(2):
                        for x in range(2):
                            r = 96 + 2 * a + x
                            sp.dma_start(QS[1 - p][r:r + 1, :, a, :].bitcast(F32), mT[x][a:H:2, :].bitcast(F32)).then_inc(m_in, 16)
                if isinstance(i, int) and i == B - 1:
                    sp.wait_ge(st_ps, NB * (B - 1))
                    sp.wait_ge(router_dma, 16 * (B - 2))
                    sp.dma_start(rh[:, 0:(B - 3) * S], rh_dram[:, 0:(B - 3) * S]).then_inc(router_dma, 16)
                if isinstance(i, int) and i >= B - 1:
                    sp.wait_ge(rh_done, i - 1)
                    sp.dma_start(rh[:, (i - 2) * S:(i - 1) * S], rh_buf).then_inc(router_dma, 16)
                elif has(i, -2):
                    cols = slice((i - 2) * S, (i - 1) * S) if isinstance(i, int) else bass.ds((i - 2) * S, S)
                    sp.wait_ge(rh_done, i - 1)
                    sp.dma_start(rh_dram[:, cols], rh_buf).then_inc(router_dma, 16)
            turns(sp, one)
            sp.wait_ge(router_dma, 16 * (B + 2))

        @block.tensor
        def _(pe):
            pe.wait_ge(router_dma, 16)
            pe.wait_ge(filled, 10)

            def project(m, bank, o, done):
                W = WT[m]
                n = 0
                for kt in range(2):
                    for wi, xi in ((0, 0), (0, 1), (1, 0)):
                        if m == "v":
                            lhsT, rhs = xT[xi][:, kt, o * P:(o + 1) * P], W[wi][:, kt, :]
                        else:
                            lhsT, rhs = W[wi][:, kt, o * P:(o + 1) * P], xT[xi][:, kt, :]
                        ins = pe.matmul(M[bank][:, o, :], lhsT, rhs, start=(n == 0), stop=(n == 5))
                        n += 1
                if o:
                    ins.then_inc(done, 1)

            def scores(b, p, n):
                if n == 0:
                    pe.wait_ge(stack_in, 192 * (b + 1))
                if n >= 2 or not isinstance(b, int) or b:
                    pe.wait_ge(s_max, NB * b + n - 1)
                bank = SR[n % 2]
                if n < 4:
                    for x in range(4):
                        j, a = 2 * n + x // 2, x % 2
                        pe.matmul(bank[:, x * P:(x + 1) * P], QS[p][0:96, j, a, 0:P], KS[p][0:96, j, 0:P],
                                  start=(x == 0), stop=False, skip_group_check=True)
                    ins = pe.matmul(bank[:].rearrange("p (a k) -> p a k", a=4), identb[:], maskS[:].broadcast_to([P, 4, P]), start=False, stop=True,
                                    skip_group_check=True)
                else:
                    j = n - 4
                    for a in range(2):
                        pe.matmul(bank[:, a * S:(a + 1) * S], QS[p][0:96, j, a, P:S], KS[p][0:96, j, :],
                                  start=(a == 0), stop=False, skip_group_check=True)
                    ins = pe.matmul(bank[:].rearrange("p (a k) -> p a k", a=2)[:, :, P:S], identb[:], maskS[:].broadcast_to([P, 2, P]),
                                    start=False, stop=True, skip_group_check=True)
                ins.then_inc(s_ps, 1)

            def exp_scores(b, p, n):
                if n == 0:
                    pe.wait_ge(m_in, 64 * (b + 1))
                if n >= 2 or not isinstance(b, int) or b:
                    pe.wait_ge(exp_done, NB * b + n - 1)
                bank, g, y = TR[n % 2], n // 3, n % 3
                if y < 2:
                    j = 2 * g + y
                    pe.matmul(bank[:], KS[p][0:100, j, 0:P], QS[p][0:100, j, :, :].rearrange("p a q -> p (a q)"),
                              start=True, stop=False, skip_group_check=True)
                    ins = pe.matmul(bank[:].rearrange("p (a q) -> p a q", a=2)[:, :, 0:P], identb[:], maskT[:].broadcast_to([P, 2, P]),
                                    start=False, stop=True, skip_group_check=True)
                else:
                    for x in range(2):
                        j = 2 * g + x
                        pe.matmul(bank[:].rearrange("p (x a q) -> p x a q", x=2, a=2)[:, x], KS[p][0:100, j, P:S],
                                  QS[p][0:100, j, :, P:S], start=(x == 0), stop=False, skip_group_check=True)
                    ins = pe.matmul(bank[:].rearrange("p (a k) -> p a k", a=4), identb[:], maskT[:].broadcast_to([P, 4, P]), start=False, stop=True,
                                    skip_group_check=True)
                ins.then_inc(st_ps, 1)

            def times_v(b, p, vb, s):
                u, hs = ((s // 2, range(4 * s, 4 * s + 4)) if s < 4 else
                         (2, range(2 * s - 8, 2 * s - 6)) if s < 8 else (3, range(2 * s - 8, 2 * s - 6)))
                t, first, last = u // 2, s in (0, 2, 4, 8), s in (1, 3, 7, 11)
                if s == 0:
                    pe.wait_ge(v_done, b + 1)
                if first:
                    pe.wait_ge(pb_done, NB * b + (5, 11, 6, 12)[u])
                    if u >= 2 or not isinstance(b, int) or b:
                        pe.wait_ge(o_left, 2 * (4 * b + u - 1))
                for h in hs:
                    o = OP[u % 2][:, (h % 8) * VW:(h % 8 + 1) * VW]
                    n, N = 0, 2 * (t + 1)
                    for kt in range(t + 1):
                        for x in range(2):
                            src = PT1[p][x][:, h, :] if kt else PT0[p][x][:, h, t * P:(t + 1) * P]
                            ins = pe.matmul(o, src, V1[vb][:, kt, h, :], start=(n == 0), stop=(n == N - 1))
                            n += 1
                if last:
                    ins.then_inc(o_ps, 1)

            def one(i, y):
                for s in range(12):
                    if has(i, -1):
                        times_v(i - 1, (y - 1) % 2, (y - 1) % 4, s)
                    if has(i, 1):
                        scores(i + 1, (y + 1) % 2, s)
                    if has(i, 0):
                        for n in banks_of[s]:
                            exp_scores(i, y % 2, n)
                    if has(i, 2):
                        b = i + 2
                        if s == 1:
                            pe.wait_ge(ln1_done, b + 1)
                            if has(i, 0):
                                pe.wait_ge(m_lo, i + 1)
                            for tt in range(2):
                                for kt in range(2):
                                    ins = pe.transpose(M[0][:, kt, tt * P:(tt + 1) * P], hn1[:, tt, kt * P:(kt + 1) * P], ident[:])
                            ins.then_inc(xT_ps, 1)
                        if s == 2:
                            pe.wait_ge(xT_lo, b + 1)
                            if has(i, -3):
                                if isinstance(i, int):
                                    pe.wait_ge(rh_done, i - 2)
                            if has(i, 1):
                                pe.wait_ge(v_sum, i + 2)
                            project("q", 1, 0, q_ps)
                        if s == 3:
                            project("q", 1, 1, q_ps)
                        if s == 4:
                            project("k", 0, 0, k_ps)
                        if s == 5:
                            project("k", 0, 1, k_ps)
                        if s == 6:
                            pe.wait_ge(q_lo, 2 * (b + 1))
                            project("v", 1, 0, v_ps)
                        if s == 7:
                            project("v", 1, 1, v_ps)
                    if has(i, -2):
                        b = i - 2
                        if s == 9:
                            pe.wait_ge(ln2_done, b + 1)
                            if has(i, 2):
                                pe.wait_ge(k_lo, 2 * (i + 3))
                            elif has(i, 0):
                                pe.wait_ge(m_lo, i + 1)
                            if isinstance(b, int) and b:
                                pe.wait_ge(hT_done, b)
                            for tt in range(2):
                                for kt in range(2):
                                    ins = pe.transpose(M[0][:, kt, tt * P:(tt + 1) * P], hn2[:, tt, kt * P:(kt + 1) * P], ident[:])
                            ins.then_inc(hT_ps, 1)
                        if s == 11:
                            pe.wait_ge(hT_done, b + 1)
                            if has(i, 2):
                                pe.wait_ge(v_sum, i + 3)
                            elif isinstance(b, int) and b:
                                pe.wait_ge(rh_done, b)
                            for kt in range(2):
                                ins = pe.matmul(M[1][:, 0, :], rw1s[:, kt, :], hn2T[:, kt, :], start=(kt == 0), stop=(kt == 1))
                            ins.then_inc(rh_ps, 1)
                if has(i, 1):
                    pe.wait_ge(s_max, NB * (i + 2))
                    if has(i, -2):
                        pe.wait_ge(hT_done, i - 1)
                    elif has(i, 2):
                        pe.wait_ge(k_lo, 2 * (i + 3))
                    for tt in range(2):
                        ins = pe.transpose(M[0][0:H, 0, tt * P:(tt + 1) * P], mx[:, tt, :], ident[:])
                    ins.then_inc(m_ps, 1)
            turns(pe, one)

        @block.scalar
        def _(act):
            act.wait_ge(c_in, 16 * 3)
            act.wait_ge(filled, 10)

            def exps(b, p, n):
                act.wait_ge(st_ps, NB * b + n + 1)
                if n == 0 and (not isinstance(b, int) or b >= 2):
                    act.wait_ge(o_ps, 4 * (b - 1))
                if n >= 3 or not isinstance(b, int) or b:
                    act.wait_ge(pb_done, NB * b + n - 2)
                A.activation(pf[n % 3][:], TR[n % 2][:], ACT.Exp, bias=shift[:], scale=float(HD) ** -0.5).then_inc(exp_done, 1)

            def probs_hi(b, p, n):
                act.wait_ge(exp_done, NB * b + n + 1)
                A.activation(probs(p, 0, n), pf[n % 3][:].rearrange("p (a q) -> p a q", a=4 if n % 3 == 2 else 2),
                             ACT.Copy).then_inc(pa_done, 1)

            def parts_hi(b, m, bank, full, dst):
                act.wait_ge(full, b + 1)
                if not isinstance(b, int) or b:
                    act.wait_ge(qk_written, 64 * b)
                for ft in range(2):
                    A.activation(dst[0][:, ft, :], M[bank][:, ft, :], ACT.Identity,
                                 bias=bqk[:, m, ft:ft + 1]).then_inc(qk_hi, 1)

            def one(i, y):
                for s in range(12):
                    if has(i, 2) and s == 1:
                        act.wait_ge(xT_ps, i + 3)
                        A.activation(xT[0][:], M[0][:], ACT.Copy).then_inc(xT_hi, 1)
                    if has(i, 0):
                        for n in banks_of[s]:
                            exps(i, y % 2, n)
                            if n:
                                probs_hi(i, y % 2, n - 1)
                    if has(i, 2) and s == 3:
                        parts_hi(i + 2, 0, 1, q_ps, qf)
                    if has(i, 2) and s == 5:
                        parts_hi(i + 2, 1, 0, k_ps, kf)
                    if has(i, -2):
                        b = i - 2
                        if s == 8:
                            act.wait_ge(ln2_done, b + 1)
                            A.activation(lnA[:, tiles(b), :], hn2[:], ACT.Copy).then_inc(lnA_done, 1)
                        if s == 9:
                            act.wait_ge(hT_ps, b + 1)
                            A.activation(hn2T[:], M[0][:], ACT.Copy).then_inc(hT_done, 1)
                        if s == 11:
                            act.wait_ge(rest_done, b + 1)
                            A.activation(lnB[:, tiles(b), :], hn2[:], ACT.Copy, scale=2048.0).then_inc(lnB_done, 1)
                            act.wait_ge(rh_ps, b + 1)
                            if not isinstance(b, int) or b:
                                act.wait_ge(router_dma, 16 * (b + 2 if isinstance(b, int) and b > B - 3 else b + 1))
                            A.activation(rh_buf, M[1][:, 0, :], ACT.Copy).then_inc(rh_done, 1)
                    if has(i, 2) and s in (9, 11):
                        act.wait_ge(v_rest if s == 11 else v_sum, i + 3)
                        A.activation(v_part(y, (s - 9) // 2), vf.rearrange("p t (h d) -> p t h d", d=HD),
                                     ACT.Copy).then_inc(v_mid if s == 11 else v_hi, 1)
                if has(i, 0):
                    probs_hi(i, y % 2, NB - 1)
                if has(i, 1):
                    act.wait_ge(m_ps, i + 2)
                    if has(i, 0):
                        act.wait_ge(m_in, 64 * (i + 1))
                    A.activation(mT[0][:], M[0][0:H, 0, :], ACT.Copy, scale=-1.0).then_inc(m_hi, 1)
            turns(act, one)

        @block.vector
        def _(v):
            for p in range(2):
                V.memset(QS[p][:].bitcast(F32), 0.0).then_inc(filled, 1)
                V.memset(KS[p][96:P].bitcast(F32), 1.0).then_inc(filled, 1)
            for p in range(4):
                V.memset(V1[p][:, :, :, 3 * HD:VW], 1.0).then_inc(filled, 1)
            V.memset(mv[:], 1.0).then_inc(filled, 1)
            V.memset(shift[:], math.log(2048.0)).then_inc(filled, 1)
            v.wait_ge(c_in, 16 * 3)
            v.wait_ge(filled, 10)
            O = [OP[u][:, 0:8 * VW].rearrange("p (h c) -> p h c", c=VW) for u in range(2)]
            xx, xh, yy, u = rs[:, 0], rs[:, 1], rs[:, 2], rs[:, 3]
            STEPS = 5 + 5 + 13 + 1 + 1

            def max_scores(b, n):
                v.wait_ge(s_ps, NB * b + n + 1)
                if n < 4:
                    V.tensor_reduce(mx[:, 0, 4 * n:4 * n + 4], SR[n % 2][:].rearrange("p (a k) -> p a k", a=4), AX.X,
                                    ALU.max).then_inc(s_max, 1)
                else:
                    j = n - 4
                    V.tensor_reduce(mx[:, 1, 2 * j:2 * j + 2], SR[n % 2][:].rearrange("p (a k) -> p a k", a=2), AX.X,
                                    ALU.max).then_inc(s_max, 1)

            def parts_lo(b, m, bank, src, done):
                v.wait_ge(qk_hi, 4 * b + 2 * m + 2)
                if not isinstance(b, int) or b:
                    v.wait_ge(qk_written, 64 * b)
                for ft in range(2):
                    V.scalar_tensor_tensor(src[1][:, ft, :], M[bank][:, ft, :], bqk[:, m, ft:ft + 1],
                                           src[0][:, ft, :].bitcast(F32), ALU.add, ALU.subtract).then_inc(done, 1)

            def outputs(b, u):
                v.wait_ge(o_ps, 4 * b + u + 1)
                if u or not isinstance(b, int) or b:
                    v.wait_ge(o_done, 4 * b + u)
                V.tensor_reduce(osum, O[u % 2][:, :, 0:3 * HD].rearrange("p h (x d) -> p h d x", d=HD), AX.X,
                                ALU.add).then_inc(o_left, 1)
                V.reciprocal(rden[:], O[u % 2][:, :, 3 * HD]).then_inc(o_left, 1)
                v.wait_ge(o_left, 2 * (4 * b + u + 1))
                V.tensor_tensor(on[:, u // 2, (u % 2) * P:(u % 2 + 1) * P].rearrange("p (h d) -> p h d", d=HD), osum,
                                rden[:].rearrange("p (h o) -> p h o", o=1).broadcast_to([P, H // 2, HD]),
                                ALU.mult).then_inc(o_done, 1)

            def newton(c, k):
                c.wait()
                if k == 0:
                    c.step(V.tensor_scalar(xx, mv[:, :, 1], EPS, None, ALU.add))
                elif k == 1:
                    c.step(V.tensor_scalar(xh, xx, -0.5, None, ALU.mult))
                    c.step(V.tensor_scalar(u.bitcast(I32), xx.bitcast(I32), 1, None, ALU.logical_shift_right))
                elif k == 2:
                    c.step(V.tensor_scalar(yy.bitcast(I32), u.bitcast(I32), -1.0, float(0x5F3759DF), ALU.mult, ALU.add))
                elif k % 3 == 0:
                    c.step(V.tensor_tensor(u, yy, yy, ALU.mult))
                elif k % 3 == 1:
                    c.step(V.tensor_tensor(u, u, xh, ALU.mult))
                else:
                    c.step(V.scalar_tensor_tensor(yy, u, 1.5, yy, ALU.add, ALU.mult))

            def normalise(c, b, k, dst, done):
                for tt in range(2):
                    ins = V.tensor_scalar(dst[:, tt, :], hacc[:, tiles(b), :][:, tt, :], mv[:, k + tt, 0:1], yy[:, k + tt:k + tt + 1],
                                          ALU.subtract, ALU.mult)
                    if tt == 0:
                        c.step(ins)
                    else:
                        ins.then_inc(done, 1)

            def one(i, y):
                c = Chain(v, chain, STEPS, i + 3)
                pad = lambda n: [c.step(V.memset(padding[:, c.n:c.n + 1], 0.0)) for _ in range(n)]
                for s in range(12):
                    if has(i, 1):
                        if s == 0 and has(i, 0):
                            v.wait_ge(m_ps, i + 1)
                        max_scores(i + 1, s)
                    if s == 0 and has(i, -2):
                        outputs(i - 2, 3)
                    if s in (2, 4, 8) and has(i, -1):
                        outputs(i - 1, (2, 4, 8).index(s))
                    if s == 1:
                        if has(i, -2):
                            v.wait_ge(o_done, 4 * (i - 1))
                            h_ = hacc[:, tiles(i - 2), :]
                            V.tensor_tensor(h_, h_, on[:], ALU.add).then_inc(h_done, 1)
                            v.wait_ge(h_done, i - 1)
                            c.step(V.memset(tick[:, 0:1], 0.0))
                            for tt in range(2):
                                c.step(V.bn_stats(st[:, tt, :], hacc[:, tiles(i - 2), :][:, tt, :]))
                        else:
                            pad(3)
                        if has(i, 3):
                            for tt in range(2):
                                c.step(V.bn_stats(st[:, 2 + tt, :], hacc[:, tiles(i + 3), :][:, tt, :]))
                        else:
                            pad(2)
                    if s == 2:
                        c.wait()
                        c.step(V.memset(tick[:, 1:2], 0.0))
                        for tt in range(4):
                            if has(i, -2 if tt < 2 else 3):
                                c.step(V.bn_aggr(mv[:, tt, :], st[:, tt, :]))
                            else:
                                pad(1)
                        if has(i, 2):
                            v.wait_ge(xT_hi, i + 3)
                            V.tensor_tensor(xT[1][:], M[0][:], xT[0][:].bitcast(F32), ALU.subtract).then_inc(xT_lo, 1)
                    if s == 3:
                        for k in range(4):
                            newton(c, k)
                    if s == 4:
                        if has(i, 2):
                            parts_lo(i + 2, 0, 1, qf, q_lo)
                        for k in range(4, 6):
                            newton(c, k)
                    if s == 5:
                        for k in range(6, 9):
                            newton(c, k)
                    if s == 6:
                        if has(i, 2):
                            parts_lo(i + 2, 1, 0, kf, k_lo)
                        for k in range(9, 12):
                            newton(c, k)
                    if s == 7:
                        c.wait()
                        if has(i, -2):
                            if not has(i, 2) and isinstance(i, int) and i - 2 > 0:
                                v.wait_ge(lnB_done, i - 2)
                            normalise(c, i - 2, 0, hn2, ln2_done)
                        else:
                            pad(1)
                    if s == 8 and has(i, 2):
                        v.wait_ge(v_ps, i + 3)
                        if has(i, 1):
                            v.wait_ge(v_done, i + 2)
                        V.tensor_tensor(vf, M[1][:], bvb[:].rearrange("p (o n) -> p o n", o=1).broadcast_to([P, 2, D]),
                                        ALU.add).then_inc(v_sum, 1)
                    if s == 10 and has(i, 2):
                        v.wait_ge(v_hi, i + 3)
                        V.tensor_tensor(vf.rearrange("p t (h d) -> p t h d", d=HD), vf.rearrange("p t (h d) -> p t h d", d=HD),
                                        v_part(y, 0), ALU.subtract).then_inc(v_rest, 1)
                    if s == 10 and has(i, -2):
                        v.wait_ge(lnA_done, i - 1)
                        v.wait_ge(hT_ps, i - 1)
                        V.tensor_tensor(hn2[:], hn2[:], lnA[:, tiles(i - 2), :], ALU.subtract).then_inc(rest_done, 1)
                    if s == 9:
                        if has(i, 3):
                            if has(i, 2):
                                v.wait_ge(xT_ps, i + 3)
                            normalise(c, i + 3, 2, hn1, ln1_done)
                        else:
                            pad(1)
                if has(i, 2):
                    v.wait_ge(v_mid, i + 3)
                    V.tensor_tensor(v_part(y, 2), vf.rearrange("p t (h d) -> p t h d", d=HD), v_part(y, 1),
                                    ALU.subtract).then_inc(v_done, 1)
                if has(i, 1):
                    v.wait_ge(m_hi, i + 2)
                    if has(i, 0):
                        v.wait_ge(m_in, 64 * (i + 1))
                    V.scalar_tensor_tensor(mT[1][:], M[0][0:H, 0, :], -1.0, mT[0][:].bitcast(F32), ALU.mult,
                                           ALU.subtract).then_inc(m_lo, 1)
                c.end()
            turns(v, one)


def top_tokens(nc, rh, rw2, posT, wT, iota, ident, dims):
    B, S, D, E, F, CAP = dims
    R = B * E // P
    IR = B // R
    with ExitStack() as ctx:
        sb = lambda n, s, d=F32: ctx.enter_context(nc.sbuf_tensor(n, s, d))
        sem = lambda n: ctx.enter_context(nc.semaphore(n))
        hid = sb("hid", [P, B * S])
        rw2s = sb("rw2s", [P, E])
        rw2p = sb("rw2_shifted", [P, IR, P])
        L = sb("L", [P, R, S])
        wk = sb("work", [P, R, S])
        top = sb("top8", [P, R, CAP])
        nm = sb("neg_max", [P, R])
        ex = sb("ex", [P, R, S])
        Z = sb("Z", [P, R])
        sel = sb("sel", [P, R, S])
        cum = sb("cum", [P, R, S])
        pos = sb("pos", [P, R, S])
        tot = sb("tot", [P, R])
        ones = sb("ones_row", [P, CAP])
        r1 = sb("w_rest", [P, 2, B * E])
        posP = ctx.enter_context(nc.psum_tensor("pos_ps", [P, 2, B * E], F32))
        wP = ctx.enter_context(nc.psum_tensor("w_ps", [P, 2, B * E], F32))
        LP = [ctx.enter_context(nc.psum_tensor(f"logit_ps{r}", [P, 512], F32)) for r in range(R)]
        rw2_in, rw2_done, silu_done, lg_ps = sem("rw2_in"), sem("rw2_done"), sem("silu_done"), sem("lg_ps")
        nm_done, ex_done, chain, pos_done, w_done, pos_ps, w_ps = (sem(n) for n in (
            "nm_done", "ex_done", "top_chain", "pos_done", "w_done", "pos_psd", "w_psd"))
        block = ctx.enter_context(nc.Block())
        V = nc.vector

        @block.sync
        def _(sp):
            sp.dma_start(rw2s[:], rw2).then_inc(rw2_in, 16)

        @block.scalar
        def _(act):
            for n in range(B // 2):
                nc.scalar.activation(hid[:, 512 * n:512 * (n + 1)], rh[:, 512 * n:512 * (n + 1)], ACT.Silu).then_inc(silu_done, 1)
            for r in range(R):
                act.wait_ge(nm_done, r + 1)
                nc.scalar.activation(ex[:, r], L[:, r], ACT.Exp, bias=nm[:, r:r + 1], accum_out=Z[:, r:r + 1]).then_inc(ex_done, 1)

        @block.tensor
        def _(pe):
            pe.wait_ge(rw2_done, 1 + IR)
            for b in range(B):
                pe.wait_ge(silu_done, b // 2 + 1)
                ins = pe.matmul(LP[b // IR][:, 0:S], rw2p[:, b % IR, :], hid[:, b * S:(b + 1) * S], start=(b % IR == 0),
                                stop=(b % IR == IR - 1))
                if b % IR == IR - 1:
                    ins.then_inc(lg_ps, 1)
            for done, src, dst, full in ((pos_done, pos, posP, pos_ps), (w_done, ex, wP, w_ps)):
                pe.wait_ge(done, R)
                for r in range(R):
                    for tt in range(2):
                        ins = pe.transpose(dst[:, tt, r * P:(r + 1) * P], src[:, r, tt * P:(tt + 1) * P], ident[:])
                ins.then_inc(full, 1)

        @block.vector
        def _(v):
            c = Chain(v, chain, 0, 0)
            c.step(V.memset(ones[:], 1.0))
            c.wait()
            c.step(V.tensor_tensor_scan(iota[:], ones[:], ones[:], 0.0, ALU.add, ALU.bypass))
            V.memset(rw2p[:], 0.0).then_inc(rw2_done, 1)
            v.wait_ge(rw2_in, 16)
            v.wait_ge(rw2_done, 1)
            for i in range(IR):
                V.tensor_copy(rw2p[:, i, i * E:(i + 1) * E], rw2s[:]).then_inc(rw2_done, 1)
            for r in range(R):
                v.wait_ge(lg_ps, r + 1)
                c.step(V.tensor_copy(L[:, r], LP[r][:, 0:S]))
            c.wait()
            for k in range(CAP // 8):
                for r in range(R):
                    src = (L if k == 0 else wk)[:, r]
                    if k:
                        c.wait()
                    c.step(V.max(top[:, r, 8 * k:8 * k + 8], src))
                    if k == 0:
                        c.wait()
                        V.tensor_scalar(nm[:, r:r + 1], top[:, r, 0:1], -1.0, None, ALU.mult).then_inc(nm_done, 1)
                for r in range(R):
                    src = (L if k == 0 else wk)[:, r]
                    c.wait()
                    c.step(V.match_replace(wk[:, r], top[:, r, 8 * k:8 * k + 8], src, BIG))
            c.wait()
            c.step(V.tensor_scalar(sel[:], wk[:], BIG, None, ALU.is_le))
            c.wait()
            for r in range(R):
                c.step(V.tensor_tensor_scan(cum[:, r], sel[:, r], sel[:, r], 0.0, ALU.add, ALU.bypass))
            c.wait()
            V.tensor_tensor(pos[:], cum[:], sel[:], ALU.mult).then_inc(pos_done, R)
            v.wait_ge(ex_done, R)
            c.step(V.reciprocal(Z[:], Z[:]))
            c.wait()
            for r in range(R):
                c.step(V.scalar_tensor_tensor(wk[:, r], ex[:, r], Z[:, r:r + 1], sel[:, r], ALU.mult, ALU.mult))
            c.wait()
            c.step(V.tensor_reduce(tot[:], wk[:], AX.X, ALU.add))
            c.wait()
            c.step(V.tensor_scalar(tot[:], tot[:], 1e-9, None, ALU.add))
            c.wait()
            c.step(V.reciprocal(tot[:], tot[:]))
            c.wait()
            for r in range(R):
                V.tensor_scalar(ex[:, r], wk[:, r], tot[:, r:r + 1], None, ALU.mult).then_inc(w_done, 1)
            v.wait_ge(pos_ps, 1)
            c.step(V.tensor_copy(posT[:], posP[:]))
            v.wait_ge(w_ps, 1)
            c.step(V.tensor_copy(wT[:, :, :, 0], wP[:]))
            c.wait()
            c.step(V.tensor_tensor(r1[:], wP[:], wT[:, :, :, 0], ALU.subtract))
            c.wait()
            c.step(V.tensor_copy(wT[:, :, :, 1], r1[:]))
            c.wait()
            c.step(V.tensor_tensor(r1[:], r1[:], wT[:, :, :, 1], ALU.subtract))
            c.wait()
            c.step(V.tensor_copy(wT[:, :, :, 2], r1[:]))
            c.wait()


def ffn(nc, ctx, w1, w2, w3, hacc, lnA, lnB, posT, wT, iota, ident16, out, dims):
    B, S, D, E, F, CAP = dims
    PR = E // 2
    FT = F // P
    HB = B // 2
    N = HB * CAP
    ST = N // P
    assert (FT, HB, N, CAP) == (4, 8, 512, 64)
    sb = lambda n, s, d=F32: ctx.enter_context(nc.sbuf_tensor(n, s, d))
    sem = lambda n: ctx.enter_context(nc.semaphore(n))
    ps = lambda n, s, d=F32: ctx.enter_context(nc.psum_tensor(n, s, d))
    raw = [sb(f"w_raw{i}", [P, 1024]) for i in range(2)]
    Wx = [[[sb(f"w{m + 1}_{x}{i}", [P, 1024], F32R) for x in ("hi", "lo")] for m in range(3)] for i in range(2)]
    OH = [sb(f"onehot{i}", [P, 2, B, 2, CAP], F16) for i in range(2)]
    ohT = [sb(f"onehotT{i}", [P, 2, S], F32R) for i in range(2)]
    xg = [[sb(f"xg_{x}{i}", [P, 2, N], F32R) for x in ("hi", "lo")] for i in range(2)]
    sg = [sb(f"silu_g{i}", [P, N]) for i in range(2)]
    hf = [sb(f"hidden{i}", [P, N]) for i in range(2)]
    hp = [sb(f"hidden_{x}", [P, FT, N], F32R) for x in ("hi", "lo")]
    Y = [sb(f"y_{x}", [P, B, D], F32R) for x in ("hi", "lo")]
    wpair = [sb(f"pair_weight{i}", [P, 2, B, 6], BF16) for i in range(2)]
    ws = [sb(f"slot_weight{i}", [P, 2, HB]) for i in range(2)]
    GP = [ps(f"gate_ps{i}", [P, N]) for i in range(2)]
    VP = [ps(f"value_ps{i}", [P, N]) for i in range(2)]
    YP = [ps(f"y_ps{i}", [P, 2, D]) for i in range(2)]
    XP = ps("gather_ps", [P, N])
    TP = ps("turn_ps", [P, 512])
    TP16 = TP[:, 0:256].bitcast(F16)

    zero = sb("zero_col", [P, 1])
    zeroed = sem("zeroed")
    raw_in = [sem(f"raw_in{i}") for i in range(2)]
    (wsplit, oh_done, ws_ps, ws_done, g_ps, v_ps, silu_done, hf_done, hh_done, hl_done, gath_ps, xh_done, xl_done,
     y_ps, y_hi, y_lo, comb_ps, comb_add, oht_ps, oht_done, out_done) = (sem(n) for n in (
         "wsplit", "oh_done", "slotw_ps", "slotw_done", "s_g_ps", "s_v_ps", "silu_g_done", "hf_done", "hh_done",
         "hl_done", "s_gath_ps", "xh_done", "xl_done", "s_y_ps", "y_hi_done", "y_lo_done", "comb_ps", "comb_add",
         "oht_ps", "oht_done", "out_done"))
    block = ctx.enter_context(nc.Block())
    T, A, V = nc.tensor, nc.scalar, nc.vector
    PASSES = ((0, 0), (0, 1), (1, 0))

    def pairs(eng, one):
        one(0, 0, True, False)
        with eng.Fori(1, PR - 2, 2) as pr:
            one(pr, 1, False, False)
            one(pr + 1, 0, False, False)
        one(PR - 1, 1, False, True)

    later = lambda n: not isinstance(n, int) or n > 0

    @block.sync
    def _(sp):
        def one(pr, par, first, last):
            for e2 in range(2):
                for m, w in enumerate((w1, w2, w3)):
                    n = 3 * e2 + m
                    e = 2 * pr + e2 if isinstance(pr, int) else sp.snap(2 * pr + e2)
                    src = w[e] if isinstance(pr, int) else w[bass.ds(e, 1)].rearrange("o a b -> (o a) b")
                    if not first or n >= 2:
                        sp.wait_ge(wsplit, 12 * pr + 2 * (n - 1))
                    sp.dma_start(raw[n % 2][:].rearrange("p (t c) -> p t c", c=src.shape[1]),
                                 src.rearrange("(t p) c -> p t c", p=P)).then_inc(raw_in[n % 2], 16)
        pairs(sp, one)
        for s in range(B // 2):
            sp.wait_ge(comb_add, 2 * HB * (PR - 1) + 2 * s + 2)
            sp.dma_start(out.rearrange("b (t p) d -> p (b t) d", p=P)[:, 4 * s:4 * s + 4, :],
                         hacc[:, 4 * s:4 * s + 4, :]).then_inc(out_done, 16)
        sp.wait_ge(out_done, 16 * (B // 2))

    @block.gpsimd
    def _(g):
        nc.gpsimd.memset(zero[:], 0.0).then_inc(zeroed, 1)
        g.wait_ge(zeroed, 1)

        def one(pr, par, first, last):
            for e2 in range(2):
                if not first:
                    g.wait_ge(y_ps, 2 * (4 * (pr - 1) + 2 * e2 + 2))
                for m in range(3):
                    n = 3 * e2 + m
                    g.wait_ge(raw_in[n % 2], 16 * (3 * pr + n // 2 + 1))
                    hi, lo = Wx[e2][m]
                    nc.gpsimd.tensor_tensor(hi[:], raw[n % 2][:], zero[:].broadcast_to([P, 1024]), ALU.add).then_inc(wsplit, 1)
                    g.wait_ge(wsplit, 12 * pr + 2 * n + 1)
                    nc.gpsimd.tensor_tensor(lo[:], raw[n % 2][:], hi[:].bitcast(F32), ALU.subtract).then_inc(wsplit, 1)
        pairs(g, one)

    @block.tensor
    def _(pe):
        def gather(Tn, par, e2, c, n):
            m, part = n // 2, n % 2
            if n:
                pe.wait_ge((xl_done, xh_done)[part], 2 * Tn + (n + 1) // 2)
            elif later(Tn):
                pe.wait_ge(xl_done, 2 * Tn)
            src = (lnA, lnB)[part]
            for b in range(HB):
                for tt in range(2):
                    ins = pe.matmul(XP[:, b * CAP:(b + 1) * CAP], src[:, 2 * (HB * c + b) + tt, m * P:(m + 1) * P],
                                    OH[par][:, tt, HB * c + b, e2, :], start=(tt == 0), stop=(tt == 1))
            ins.then_inc(gath_ps, 1)

        def slot_weights(pr, par):
            if later(pr - 1):
                pe.wait_ge(oht_done, 8 * (pr - 1))
            for b in range(B):
                for tt in range(2):
                    ins = pe.matmul(TP[:, 256 + 6 * b:256 + 6 * b + 6], OH[par][:, tt, b].rearrange("p e s -> p (e s)"),
                                    wpair[par][:, tt, b, :], start=(tt == 0), stop=(tt == 1))
            ins.then_inc(ws_ps, 1)

        def turn_onehot(pp, par, s):
            if s or later(pp):
                pe.wait_ge(oht_done, 8 * pp + s)
            if s == 0:
                pe.wait_ge(ws_done, 4 * PR if isinstance(pp, int) and pp == PR - 1 else 4 * (pp + 2))
            for x in range(2):
                for tt in range(2):
                    ins = pe.transpose(TP16[:, x * S + tt * P:x * S + (tt + 1) * P],
                                       OH[par][:, tt, 2 * s + x].rearrange("p e s -> p (e s)"), ident16[:])
            ins.then_inc(oht_ps, 1)

        def combine(pp, s):
            pe.wait_ge(oht_done, 8 * pp + s + 1)
            for x in range(2):
                if s % 4:
                    pe.wait_ge(comb_add, 2 * HB * pp + 2 * s - 1 + x)
                for tt in range(2):
                    for y in range(2):
                        ins = pe.matmul(YP[x][:, tt, :], ohT[s % 2][:, x, tt * P:(tt + 1) * P], Y[y][:, 2 * s + x, :],
                                        start=(y == 0), stop=(y == 1))
                ins.then_inc(comb_ps, 1)

        def combine_two(pr, par, e2, c, ft, U, first):
            if e2 or first:
                return
            s = 4 * c + ft
            if ft == 0:
                pe.wait_ge(y_lo, 8 * U)
            combine(pr - 1, s)
            if s + 1 < 8:
                turn_onehot(pr - 1, 1 - par, s + 1)

        def unit(pr, par, e2, c, first, last):
            U = 4 * pr + 2 * e2 + c
            pe.wait_ge(xh_done, 2 * (U + 1))
            pe.wait_ge(xl_done, 2 * (U + 1))
            for ft in range(FT):
                for m, bank, used, full in ((0, GP, silu_done, g_ps), (1, VP, hf_done, v_ps)):
                    if m == 1 and ft:
                        combine_two(pr, par, e2, c, ft, U, first)
                    if ft >= 2 or later(U):
                        pe.wait_ge(used, 4 * U + ft - 1)
                    if ft == 0 and c == 0:
                        pe.wait_ge(wsplit, 12 * pr + 6 * e2 + 2 * (m + 1))
                    n = 0
                    for kt in range(2):
                        for wi, xi in PASSES:
                            ins = pe.matmul(bank[ft % 2][:], Wx[e2][m][wi][:, kt * F + ft * P:kt * F + (ft + 1) * P],
                                            xg[c][xi][:, kt, :], start=(n == 0), stop=(n == 5))
                            n += 1
                    ins.then_inc(full, 1)
                if c == 0:
                    gather(U + 1, par, e2, 1, ft)
                elif e2 == 0:
                    gather(U + 1, par, 1, 0, ft)
                elif not last:
                    if ft == 0:
                        pe.wait_ge(oh_done, 3 * (pr + 2))
                    gather(U + 1, 1 - par, 0, 0, ft)
                    if ft == 1:
                        slot_weights(pr + 1, 1 - par)
                if ft == 0:
                    combine_two(pr, par, e2, c, 0, U, first)
            if e2 == 0 and not first:
                pe.wait_ge(comb_add, 2 * HB * (pr - 1) + 8 * (c + 1))
            elif later(U):
                pe.wait_ge(y_lo, 8 * U)
            if c == 0:
                pe.wait_ge(wsplit, 12 * pr + 6 * e2 + 6)
            for ft in range(FT):
                pe.wait_ge(hl_done, 4 * U + ft + 1)
                for st in range(ST):
                    for q, (hi_, wi) in enumerate(PASSES):
                        ins = pe.matmul(YP[st // 2][:, st % 2, :], hp[hi_][:, ft, st * P:(st + 1) * P],
                                        Wx[e2][2][wi][:, ft * D:(ft + 1) * D], start=(ft == 0 and st % 2 == 0 and q == 0),
                                        stop=(ft == FT - 1 and q == 2), skip_group_check=True)
                    if ft == FT - 1 and st % 2 == 1:
                        ins.then_inc(y_ps, 1)

        def one(pr, par, first, last):
            if first:
                pe.wait_ge(oh_done, 3)
                for n in range(4):
                    gather(0, 0, 0, 0, n)
                slot_weights(0, 0)
            for e2 in range(2):
                for c in range(2):
                    unit(pr, par, e2, c, first, last)
            turn_onehot(pr, par, 0)
        pairs(pe, one)
        for s in range(8):
            if s == 0:
                pe.wait_ge(y_lo, 8 * 4 * PR)
            elif s == 4:
                pe.wait_ge(comb_add, 2 * HB * (PR - 1) + 8)
            combine(PR - 1, s)
            if s < 7:
                turn_onehot(PR - 1, 1, s + 1)

    @block.scalar
    def _(act):
        def x_hi(Tn, c, m):
            act.wait_ge(gath_ps, 4 * Tn + 2 * m + 1)
            A.activation(xg[c][0][:, m, :], XP[:], ACT.Copy).then_inc(xh_done, 1)

        def turned(pp, s):
            act.wait_ge(oht_ps, 8 * pp + s + 1)
            A.activation(ohT[s % 2][:], TP16.rearrange("p (x t) -> p x t", x=2), ACT.Copy).then_inc(oht_done, 1)

        def hidden_hi(U, ft):
            act.wait_ge(hf_done, 4 * U + ft + 1)
            A.activation(hp[0][:, ft, :], hf[ft % 2][:], ACT.Copy).then_inc(hh_done, 1)

        def unit(pr, par, e2, c, first, last):
            U = 4 * pr + 2 * e2 + c
            for ft in range(FT):
                act.wait_ge(g_ps, 4 * U + ft + 1)
                if ft >= 2 or later(U):
                    act.wait_ge(hf_done, 4 * U + ft - 1)
                A.activation(sg[ft % 2][:], GP[ft % 2][:], ACT.Silu).then_inc(silu_done, 1)
                if ft:
                    hidden_hi(U, ft - 1)
                if ft % 2 == 0 and not (last and e2 and c):
                    x_hi(U + 1, 1 - c, ft // 2)
                if e2 == 0 and not first and 4 * c + ft + 1 < 8:
                    turned(pr - 1, 4 * c + ft + 1)
            hidden_hi(U, FT - 1)
            for st in range(ST):
                if st % 2 == 0:
                    act.wait_ge(y_ps, 2 * U + st // 2 + 1)
                if st == 0:
                    act.wait_ge(ws_done, 4 * (pr + 1))
                for b2 in range(2):
                    r, o = 64 * b2, 64 * e2
                    A.activation(Y[0][o:o + 64, HB * c + 2 * st + b2, :], YP[st // 2][r:r + 64, st % 2, :], ACT.Copy,
                                 scale=ws[par][r:r + 64, e2, (HB // 2) * c + st:(HB // 2) * c + st + 1]).then_inc(y_hi, 1)

        def one(pr, par, first, last):
            if first:
                for m in range(2):
                    x_hi(0, 0, m)
            for e2 in range(2):
                for c in range(2):
                    unit(pr, par, e2, c, first, last)
            turned(pr, 0)
        pairs(act, one)
        for s in range(1, 8):
            turned(PR - 1, s)

    @block.vector
    def _(v):
        def onehot(pr, par):
            w_ = wT[:].rearrange("p t (b e) x -> p t b (e x)", e=E)
            w_ = w_[:, :, :, 6 * pr:6 * pr + 6] if isinstance(pr, int) else w_[:, :, :, bass.ds(6 * pr, 6)]
            V.tensor_copy(wpair[par][:], w_).then_inc(oh_done, 1)
            for tt in range(2):
                p_ = posT[:, tt, :].rearrange("p (b e o) -> p b e o", e=E, o=1)
                p_ = p_[:, :, 2 * pr:2 * pr + 2] if isinstance(pr, int) else p_[:, :, bass.ds(2 * pr, 2)]
                V.tensor_tensor(OH[par][:, tt], iota[:].rearrange("p (b e s) -> p b e s", b=1, e=1).broadcast_to([P, B, 2, CAP]),
                                p_.broadcast_to([P, B, 2, CAP]), ALU.is_equal).then_inc(oh_done, 1)

        def slot_weights(pr, par):
            v.wait_ge(ws_ps, pr + 1)
            if later(pr - 1):
                v.wait_ge(y_hi, 32 * (pr - 1))
                v.wait_ge(y_lo, 32 * (pr - 1))
            for e2 in range(2):
                src = TP[64 * e2:64 * e2 + 64, 256:256 + 6 * B].rearrange("p (b two e x) -> p two e b x", two=2, e=2, x=3)
                for b2 in range(2):
                    V.tensor_reduce(ws[par][64 * b2:64 * b2 + 64, e2, :], src[:, b2, e2], AX.X, ALU.add).then_inc(ws_done, 1)

        def x_lo(Tn, c, m):
            v.wait_ge(gath_ps, 4 * Tn + 2 * m + 2)
            V.tensor_scalar(xg[c][1][:, m, :], XP[:], 1.0 / 2048, None, ALU.mult).then_inc(xl_done, 1)

        def hidden_lo(U, ft):
            v.wait_ge(hh_done, 4 * U + ft + 1)
            V.tensor_tensor(hp[1][:, ft, :], hf[ft % 2][:], hp[0][:, ft, :].bitcast(F32), ALU.subtract).then_inc(hl_done, 1)

        def add(pp, s):
            for x in range(2):
                b = 2 * s + x
                v.wait_ge(comb_ps, 2 * HB * pp + b + 1)
                V.tensor_tensor(hacc[:, 2 * b:2 * b + 2, :], YP[x][:], hacc[:, 2 * b:2 * b + 2, :], ALU.add).then_inc(comb_add, 1)

        def unit(pr, par, e2, c, first, last):
            U = 4 * pr + 2 * e2 + c
            for ft in range(FT):
                if ft and e2 == 0 and not first:
                    add(pr - 1, 4 * c + ft)
                v.wait_ge(silu_done, 4 * U + ft + 1)
                v.wait_ge(v_ps, 4 * U + ft + 1)
                if ft >= 2:
                    v.wait_ge(hh_done, 4 * U + ft - 1)
                if ft >= 2 or later(U):
                    v.wait_ge(hl_done, 4 * U + ft - 1)
                V.tensor_tensor(hf[ft % 2][:], sg[ft % 2][:], VP[ft % 2][:], ALU.mult).then_inc(hf_done, 1)
                if ft:
                    hidden_lo(U, ft - 1)
                if ft == 2 and e2 and c and not last:
                    slot_weights(pr + 1, 1 - par)
                if ft % 2 and not (last and e2 and c):
                    x_lo(U + 1, 1 - c, ft // 2)
                if ft == 0 and e2 == 0 and not first:
                    add(pr - 1, 4 * c)
            hidden_lo(U, FT - 1)
            if e2 == 1 and c == 0 and not last:
                onehot(pr + 1, 1 - par)
            for st in range(ST):
                for b2 in range(2):
                    r, o = 64 * b2, 64 * e2
                    b = HB * c + 2 * st + b2
                    if st % 2 == 0 and b2 == 0:
                        v.wait_ge(y_hi, 8 * U + 2 * st + 4)
                    V.scalar_tensor_tensor(Y[1][o:o + 64, b, :], YP[st // 2][r:r + 64, st % 2, :],
                                           ws[par][r:r + 64, e2, (HB // 2) * c + st:(HB // 2) * c + st + 1],
                                           Y[0][o:o + 64, b, :].bitcast(F32), ALU.mult, ALU.subtract).then_inc(y_lo, 1)

        def one(pr, par, first, last):
            if first:
                onehot(0, 0)
                for m in range(2):
                    x_lo(0, 0, m)
                slot_weights(0, 0)
            for e2 in range(2):
                for c in range(2):
                    unit(pr, par, e2, c, first, last)
        pairs(v, one)
        for s in range(8):
            add(PR - 1, s)


_INS = ["x", "L0_tok_Wa", "L0_tok_ba", "L0_tok_Wd1", "L0_tok_bd1", "L0_tok_Wd2", "L0_tok_bd2", "L0_tok_Wd3", "L0_tok_bd3",
        "L0_attn_Wq", "L0_attn_bq", "L0_attn_Wk", "L0_attn_bk", "L0_attn_Wv", "L0_attn_bv", "L0_ffn_router_w1",
        "L0_ffn_router_w2", "L0_ffn_w1", "L0_ffn_w2", "L0_ffn_w3"]


def kernel(**inputs):
    import numpy as _np
    import concourse.bacc as _bacc
    from concourse.bass_utils import run_bass_kernel_spmd as _run

    nc = _bacc.Bacc("TRN2", target_bir_lowering=False, num_devices=1, dynamic_dma_scratch_size=1024)
    arrays, args = {}, []
    for name in _INS:
        a = _np.ascontiguousarray(inputs[name])
        arrays[f"in_{name}"] = a
        args.append(nc.dram_tensor(f"in_{name}", a.shape, mybir.dt.from_np(a.dtype), kind="ExternalInput").ap())
    shape = inputs["x"].shape[:3]
    args.append(nc.dram_tensor("out_0", shape, F32, kind="ExternalOutput").ap())
    build_program(nc, *args)
    r = _run(nc, [arrays], core_ids=[0])
    return r.results[0]["out_0"]
```

```python
import math
from contextlib import ExitStack

import concourse.bass as bass
from concourse import mybir

ALU = mybir.AluOpType
ACT = mybir.ActivationFunctionType
AX = mybir.AxisListType
F32 = mybir.dt.float32
F32R = mybir.dt.float32r
F16 = mybir.dt.float16
BF16 = mybir.dt.bfloat16
I32 = mybir.dt.int32

P = 128
BIG = -3.0e38
EPS = 1e-5


class Chain:

    def __init__(self, eng, sem, per, run):
        self.eng, self.sem, self.per, self.base, self.n = eng, sem, per, run * per, 0

    def step(self, ins):
        ins.then_inc(self.sem, 1)
        self.n += 1

    def wait(self):
        self.eng.wait_ge(self.sem, self.base + self.n)

    def end(self):
        assert self.n == self.per, (self.n, self.per)


def build_program(nc, x, Wa, ba, Wd1, bd1, Wd2, bd2, Wd3, bd3, Wq, bq, Wk, bk, Wv, bv, rw1, rw2, w1, w2, w3, out):
    B, S, D, _ = x.shape
    H, HD, _ = Wq.shape
    E, _, F = w1.shape
    RH = rw1.shape[1]
    TT = S // P
    KT = D // P
    NT = B * TT
    J = H // 2
    CAP = -(-512 * 2 // E)
    IT = 4
    G = S // 8
    assert (P, KT, TT, H * HD, RH, IT * G) == (128, 2, 2, D, 128, P)

    h_dram = nc.dram_tensor("h_scratch", [B * S, D], F32, kind="Internal").ap()
    q_dram = nc.dram_tensor("q_scratch", [2, 2, KT * P, S], F32, kind="Internal").ap()
    k_dram = nc.dram_tensor("k_scratch", [2, 2, KT * P, S], F32, kind="Internal").ap()

    rh_dram = nc.dram_tensor("router_scratch", [P, B * S], F32, kind="Internal").ap()
    assert J * 2 * S == B * S

    with ExitStack() as ctx:
        sb = lambda n, s, d=F32: ctx.enter_context(nc.sbuf_tensor(n, s, d))
        hacc = sb("hacc", [P, NT + TT, D])
        lnA = sb("lnA", [P, NT, D], F16)
        lnB = sb("lnB", [P, NT, D], F16)
        ident = sb("ident", [P, P])
        ident16 = sb("ident16", [P, P], F16)
        identb = sb("identb", [P, P], BF16)

        small = sb("small", [P, 1024])
        posT = small[:, 0:B * E].bitcast(F16).rearrange("p (t c) -> p t c", t=2)
        wT = small[:, B * E:4 * B * E].bitcast(BF16).rearrange("p (t c x) -> p t c x", t=2, x=3)
        iota = sb("slot_number", [P, CAP], F16)

        with ExitStack() as mid:
            sbm = lambda n, s, d=F32: mid.enter_context(nc.sbuf_tensor(n, s, d))
            WT = {}
            for m in "qkv":
                WT[m] = [sbm(f"W{m}T_hi", [P, KT, D], F32R), sbm(f"W{m}T_lo", [P, KT, D], F32R)]
            maskS = sbm("maskS", [P, 1, P], BF16)
            maskT = sbm("maskT", [P, 1, P], BF16)
            tokenizer(nc, x, Wa, ba, [Wd1, Wd2, Wd3], [bd1, bd2, bd3], Wq, Wk, Wv, WT, hacc, h_dram,
                      ident, ident16, identb, maskS, maskT)
            QS0 = sbm("q_stack0", [P, J, 2, S], F32R)
            rh = QS0[:].rearrange("p j a q -> p (j a q)").bitcast(F32)
            attention(nc, bq, bk, bv, rw1, WT, hacc, lnA, lnB, QS0, small, rh, q_dram, k_dram, rh_dram, ident, identb,
                      h_dram, maskS, maskT, (B, S, D, H, HD, E))
            top_tokens(nc, rh, rw2, posT, wT, iota, ident, (B, S, D, E, F, CAP))
        ffn(nc, ctx, w1, w2, w3, hacc, lnA, lnB, posT, wT, iota, ident16, out, (B, S, D, E, F, CAP))


def tokenizer(nc, x, Wa, ba, Wd, bd, Wq, Wk, Wv, WT, hacc, h_dram, ident, ident16, identb, maskS, maskT):
    B, S, D, _ = x.shape
    IT, G = 4, S // 8
    NTL = B // IT
    with ExitStack() as ctx:
        sb = lambda n, s, d=F32: ctx.enter_context(nc.sbuf_tensor(n, s, d))
        sem = lambda n: ctx.enter_context(nc.semaphore(n))
        X = [sb(f"x_tile{i}", [P, 8, D]) for i in range(2)]
        Y = [sb(f"rec_tile{i}", [P, 8, D]) for i in range(2)]
        su = sb("col_sum", [P, 8, D // 2])
        di = sb("col_dif", [P, 8, D // 2])
        su_a = sb("col_sum_a", [P, 8, D // 2])
        di_a = sb("col_dif_a", [P, 8, D // 2])
        band = [[sb(f"band{l}_{i}", [P, 3, 8 >> l, D >> l]) for l in (1, 2, 3)] for i in range(2)]
        low = [[sb(f"low{l}_{i}", [P, 8 >> l, D >> l]) for l in (1, 2, 3)] for i in range(2)]
        vs = sb("v_scaled", [P, 4, D // 2])
        junk = sb("junk", [P, 3, 4 * D // 2])
        wlev = [sb(f"wband{l}", [P, 3, (8 >> l) * (D >> l) * 3]) for l in (1, 2, 3)]
        wlow = sb("wlow", [P, D // 8])
        wraw = sb("wraw", [P, 3, 2, D])
        part = sb("part", [P, 10])
        bias = sb("bias", [P, 10])
        gsc = sb("gate_scale", [P, 10])
        osc = sb("out_scale", [P, 10])
        z = sb("z", [P, 10])
        ez = sb("ez", [P, 10])
        m3 = sb("m3", [P, 3])
        s4 = sb("s4", [P, 4])
        gate = sb("gate", [P, 10])
        ngate = sb("ngate", [P, 10])
        blk = sb("same_image", [P, P])
        tick = sb("tick_split", [P, 1])
        zsum = ctx.enter_context(nc.psum_tensor("zsum", [P, 512], F32))
        wps = [ctx.enter_context(nc.psum_tensor(f"w_ps{i}", [P, 2, D], F32)) for i in range(3)]

        x_in = [sem(f"x_in{i}") for i in range(2)]
        w_in = sem("w_in")
        wqkv_in = sem("wqkv_in")
        x_used = sem("x_used")
        const0 = sem("const0")
        const_done = sem("const_done")
        part_done = sem("part_done")
        z_ready = sem("z_ready")
        arg_ready = sem("arg_ready")
        exp_ready = sem("exp_ready")
        rec_done = sem("rec_done")
        tiles_split = sem("tiles_split")
        split_chain = sem("split_chain")
        syn_done = sem("syn_done")
        rec_out = [sem(f"rec_out{i}") for i in range(2)]
        h_in = sem("h_in")
        h_zero = sem("h_zero")
        tc = sem("tok_chain")
        wt_ps = sem("wt_ps")
        wt_hi = sem("wt_hi")
        wt_lo = sem("wt_lo")

        def analysis(c, eng, src, low, band, su, di):
            for l in range(3):
                R, C = 8 >> l, D >> l
                s_, d_ = su[:, 0:R, 0:C // 2], di[:, 0:R, 0:C // 2]
                pr = src[:].rearrange("p r (c two) -> p r c two", two=2)
                c.wait()
                c.step(eng.tensor_tensor(s_, pr[:, :, :, 0], pr[:, :, :, 1], ALU.add))
                if eng is nc.gpsimd:
                    c.wait()
                c.step(eng.tensor_tensor(d_, pr[:, :, :, 0], pr[:, :, :, 1], ALU.subtract))
                c.wait()
                sp_ = s_.rearrange("p (r two) c -> p r two c", two=2)
                dp_ = d_.rearrange("p (r two) c -> p r two c", two=2)
                for dst, a, op in ((low[l][:], sp_, ALU.add), (band[l][:, 0], sp_, ALU.subtract),
                                   (band[l][:, 1], dp_, ALU.add), (band[l][:, 2], dp_, ALU.subtract)):
                    if eng is nc.gpsimd:
                        c.wait()
                    c.step(eng.tensor_tensor(dst, a[:, :, 0], a[:, :, 1], op))
                src = low[l]

        xv = x.rearrange("b (g i) w c -> (b g) (i w c)", i=8)
        hv = h_dram.rearrange("(p i) w -> p (i w)", i=8)
        block = ctx.enter_context(nc.Block())
        NW = 4 * 4 + 4

        @block.sync
        def _(sp):
            sp.dma_start(X[0][:].rearrange("p i w -> p (i w)"), xv[0:P]).then_inc(x_in[0], 16)
            n = 0
            for l in (1, 2, 3):
                w = Wd[3 - l].rearrange("(c g k) o -> g c (k o)", c=3, g=G)
                for b in range(IT):
                    sp.dma_start(wlev[l - 1][b * G:(b + 1) * G], w).then_inc(w_in, 16)
                    n += 1
            for b in range(IT):
                sp.dma_start(wlow[b * G:(b + 1) * G], Wa.rearrange("(g k) o -> g (k o)", g=G)).then_inc(w_in, 16)
                n += 1
            for c0, c1, v in ((0, 1, ba), (1, 4, bd[0]), (4, 7, bd[1]), (7, 10, bd[2])):
                sp.dma_start(bias[:, c0:c1], v.rearrange("(a c) -> a c", a=1).broadcast_to([P, c1 - c0])).then_inc(w_in, 16)
                n += 1
            assert n == NW
            sp.dma_start(X[1][:].rearrange("p i w -> p (i w)"), xv[P:2 * P]).then_inc(x_in[1], 16)
            for i, w in enumerate((Wq, Wk, Wv)):
                sp.dma_start(wraw[:, i], w.rearrange("(t g) d e -> (g d) t e", t=2)).then_inc(wqkv_in, 16)
            for t in range(NTL):
                sp.wait_ge(rec_done, t + 1)
                sp.dma_start(hv[t * P:(t + 1) * P], Y[t % 2][:].rearrange("p i w -> p (i w)")).then_inc(rec_out[t % 2], 16)
                if t + 2 < NTL:
                    sp.dma_start(X[t % 2][:].rearrange("p i w -> p (i w)"), xv[(t + 2) * P:(t + 3) * P]).then_inc(x_in[t % 2], 16)
                sp.wait_ge(rec_out[t % 2], 16 * (t // 2 + 1))
                if t < NTL - 1:
                    sp.dma_start(hacc[:, 8 * t:8 * t + 8, :],
                                 h_dram.rearrange("(n p) w -> p n w", p=P)[:, 8 * t:8 * t + 8, :]).then_inc(h_in, 16)
            sp.wait_ge(h_in, 16 * (NTL - 1))

        @block.gpsimd
        def _(g):
            nc.gpsimd.memset(ident[:], 0.0).then_inc(const0, 1)
            nc.gpsimd.memset(maskS[:], 0.0).then_inc(const0, 1)
            nc.gpsimd.memset(maskT[:], 0.0).then_inc(const0, 1)
            nc.gpsimd.memset(blk[:], 0.0).then_inc(const0, 1)
            g.wait_ge(const0, 4)
            nc.gpsimd.affine_select(out=ident[:], in_=ident[:], compare_op=ALU.not_equal, fill=1.0, base=0,
                                    pattern=[[-1, P]], channel_multiplier=1).then_inc(const_done, 1)
            nc.gpsimd.affine_select(out=maskS[:], in_=maskS[:], compare_op=ALU.is_ge, fill=BIG, base=0,
                                    pattern=[[0, 1], [-1, P]], channel_multiplier=1).then_inc(const_done, 1)
            nc.gpsimd.affine_select(out=maskT[:], in_=maskT[:], compare_op=ALU.is_ge, fill=BIG, base=0,
                                    pattern=[[0, 1], [1, P]], channel_multiplier=-1).then_inc(const_done, 1)
            g.wait_ge(const_done, 3)
            for b in range(IT):
                nc.gpsimd.memset(blk[b * G:(b + 1) * G, b * G:(b + 1) * G], 1.0).then_inc(const_done, 1)
            g.wait_ge(const_done, 3 + IT)
            nc.gpsimd.tensor_copy(ident16[:], ident[:]).then_inc(const_done, 1)
            nc.gpsimd.tensor_copy(identb[:], ident[:]).then_inc(const_done, 1)
            g.wait_ge(const_done, 5 + IT)
            c = Chain(g, split_chain, 0, 0)
            for t in range(1, NTL):
                g.wait_ge(x_in[t % 2], 16 * (t // 2 + 1))
                if t >= 2:
                    g.wait_ge(rec_done, t - 1)
                analysis(c, nc.gpsimd, X[t % 2], low[t % 2], band[t % 2], su_a, di_a)
                c.wait()
                nc.gpsimd.memset(tick[:], 0.0).then_inc(tiles_split, 1)

        @block.tensor
        def _(pe):
            pe.wait_ge(const_done, 5 + IT)
            pe.wait_ge(wqkv_in, 48)
            for i in range(3):
                for ft in range(2):
                    for kt in range(2):
                        ins = pe.transpose(wps[i][:, kt, ft * P:(ft + 1) * P], wraw[:, i, ft, kt * P:(kt + 1) * P], ident[:])
                ins.then_inc(wt_ps, 1)
            for t in range(NTL):
                pe.wait_ge(part_done, t + 1)
                if t:
                    pe.wait_ge(z_ready, t)
                pe.matmul(zsum[:, 0:10], blk[:], part[:], start=True, stop=True).then_inc(arg_ready, 1)

        @block.scalar
        def _(act):
            for i, m in enumerate("qkv"):
                act.wait_ge(wt_ps, i + 1)
                nc.scalar.activation(WT[m][0][:], wps[i][:], ACT.Copy).then_inc(wt_hi, 1)
            for t in range(NTL):
                act.wait_ge(z_ready, t + 1)
                nc.scalar.activation(ez[:], z[:], ACT.Exp).then_inc(exp_ready, 1)

        @block.vector
        def _(v):
            nc.vector.memset(hacc[:, 2 * B:, :], 0.0).then_inc(h_zero, 1)
            v.wait_ge(const0, 4)
            c = Chain(v, tc, 0, 0)
            for a, b_, g_, o_ in ((0, 4, 0.125, 1 / 64), (4, 7, 0.25, 1 / 16), (7, 10, 0.5, 1 / 4)):
                c.step(nc.vector.memset(gsc[:, a:b_], g_))
                c.step(nc.vector.memset(osc[:, a:b_], o_))
            V = nc.vector
            for t in range(NTL):
                p = t % 2
                v.wait_ge(x_in[p], 16 * (t // 2 + 1))
                if t == 0:
                    analysis(c, V, X[0], low[0], band[0], su, di)
                    c.wait()
                else:
                    v.wait_ge(tiles_split, t)
                low_, band_ = low[p], band[p]
                if t == 0:
                    v.wait_ge(w_in, 16 * NW)
                if t:
                    v.wait_ge(arg_ready, t)
                c.step(V.tensor_tensor_reduce(junk[:, 0, 0:D // 8], low_[2][:, 0, :], wlow[:], 1.0, 0.0, ALU.mult, ALU.add, part[:, 0:1]))
                for l in (3, 2, 1):
                    n = (8 >> l) * (D >> l)
                    wv_ = wlev[l - 1][:].rearrange("p c (k o) -> p o c k", o=3)
                    for o in range(3):
                        c.wait()
                        col = 1 + 3 * (3 - l) + o
                        c.step(V.tensor_tensor_reduce(junk[:, :, 0:n], band_[l - 1][:].rearrange("p c r w -> p c (r w)"), wv_[:, o],
                                                      1.0, 0.0, ALU.mult, ALU.add, part[:, col:col + 1]))
                c.wait()
                V.tensor_copy(z[:], part[:]).then_inc(part_done, 1)
                c.n += 0
                v.wait_ge(arg_ready, t + 1)
                v.wait_ge(part_done, t + 1)
                c.step(V.tensor_tensor(z[:], zsum[:, 0:10], gsc[:], ALU.mult))
                c.wait()
                c.step(V.tensor_tensor(z[:], z[:], bias[:], ALU.add))
                c.wait()
                z3 = z[:, 1:10].rearrange("p (l o) -> p l o", o=3)
                c.step(V.tensor_reduce(m3[:], z3, AX.X, ALU.max))
                c.step(V.tensor_scalar(z[:, 0:1], z[:, 0:1], -1.0, 88.0, ALU.mult, ALU.min))
                c.wait()
                V.tensor_tensor(z3, z3, m3[:].rearrange("p (l o) -> p l o", o=1).broadcast_to([P, 3, 3]), ALU.subtract).then_inc(z_ready, 1)
                v.wait_ge(exp_ready, t + 1)
                e3 = ez[:, 1:10].rearrange("p (l o) -> p l o", o=3)
                c.step(V.tensor_reduce(s4[:, 1:4], e3, AX.X, ALU.add))
                c.step(V.tensor_scalar(s4[:, 0:1], ez[:, 0:1], 1.0, None, ALU.add))
                c.wait()
                c.step(V.reciprocal(s4[:], s4[:]))
                c.wait()
                c.step(V.tensor_tensor(gate[:, 1:10].rearrange("p (l o) -> p l o", o=3), e3,
                                       s4[:, 1:4].rearrange("p (l o) -> p l o", o=1).broadcast_to([P, 3, 3]), ALU.mult))
                c.step(V.tensor_copy(gate[:, 0:1], s4[:, 0:1]))
                c.wait()
                c.step(V.tensor_tensor(gate[:], gate[:], osc[:], ALU.mult))
                c.wait()
                c.step(V.tensor_scalar(ngate[:], gate[:], -1.0, None, ALU.mult))
                c.step(V.tensor_scalar(low_[2][:], low_[2][:], gate[:, 0:1], None, ALU.mult))
                if t >= 2:
                    v.wait_ge(rec_out[p], 16 * (t // 2))
                for l in (2, 1, 0):
                    R, C = 8 >> (l + 1), D >> (l + 1)
                    g0 = 1 + 3 * (2 - l)
                    sp_ = su[:, 0:2 * R, 0:C].rearrange("p (r two) c -> p r two c", two=2)
                    dp_ = di[:, 0:2 * R, 0:C].rearrange("p (r two) c -> p r two c", two=2)
                    vv = vs[:, 0:R, 0:C]
                    c.wait()
                    c.step(V.scalar_tensor_tensor(sp_[:, :, 0], band_[l][:, 0], gate[:, g0:g0 + 1], low_[l][:], ALU.mult, ALU.add))
                    c.step(V.scalar_tensor_tensor(sp_[:, :, 1], band_[l][:, 0], ngate[:, g0:g0 + 1], low_[l][:], ALU.mult, ALU.add))
                    c.step(V.tensor_scalar(vv, band_[l][:, 1], gate[:, g0 + 1:g0 + 2], None, ALU.mult))
                    c.wait()
                    c.step(V.scalar_tensor_tensor(dp_[:, :, 0], band_[l][:, 2], gate[:, g0 + 2:g0 + 3], vv, ALU.mult, ALU.add))
                    c.step(V.scalar_tensor_tensor(dp_[:, :, 1], band_[l][:, 2], ngate[:, g0 + 2:g0 + 3], vv, ALU.mult, ALU.add))
                    c.wait()
                    dst = (low_[l - 1] if l else Y[p])[:].rearrange("p r (c two) -> p r c two", two=2)
                    a_, b_ = su[:, 0:2 * R, 0:C], di[:, 0:2 * R, 0:C]
                    c.step(V.tensor_tensor(dst[:, :, :, 0], a_, b_, ALU.add))
                    if l:
                        c.step(V.tensor_tensor(dst[:, :, :, 1], a_, b_, ALU.subtract))
                    else:
                        c.wait()
                        V.tensor_tensor(dst[:, :, :, 1], a_, b_, ALU.subtract).then_inc(rec_done, 1)
                v.wait_ge(rec_done, t + 1)
                if t < 3:
                    m = "qkv"[t]
                    v.wait_ge(wt_hi, t + 1)
                    c.step(V.tensor_tensor(WT[m][1][:], wps[t][:], WT[m][0][:].bitcast(F32), ALU.subtract))


def attention(nc, bq, bk, bv, rw1, WT, hacc, lnA, lnB, QS0, small, rh, q_dram, k_dram, rh_dram, ident, identb,
              h_dram, maskS, maskT, dims):
    B, S, D, H, HD, E = dims
    J = H // 2
    NT = B * S // P
    NB = 12
    with ExitStack() as ctx:
        sb = lambda n, s, d=F32: ctx.enter_context(nc.sbuf_tensor(n, s, d))
        sem = lambda n: ctx.enter_context(nc.semaphore(n))
        ps = lambda n, s, d=F32: ctx.enter_context(nc.psum_tensor(n, s, d))
        hn1 = sb("hn1", [P, 2, D])
        hn2 = sb("hn2", [P, 2, D])
        xT = [sb("xT_hi", [P, 2, S], F32R), sb("xT_lo", [P, 2, S], F32R)]
        qf = [sb("q_hi", [P, 2, S], F32R), sb("q_lo", [P, 2, S], F32R)]
        kf = [sb("k_hi", [P, 2, S], F32R), sb("k_lo", [P, 2, S], F32R)]
        QS = [QS0, sb("q_stack1", [P, J, 2, S], F32R)]
        KS = [sb(f"k_stack{i}", [P, J, S], F32R) for i in range(2)]
        VW = 3 * HD + 1
        V1 = [sb(f"v_ones{i}", [P, 2, H, VW], BF16) for i in range(4)]
        PT0 = [[sb(f"probs_k0_{x}_{i}", [P, H, S], F16) for x in range(2)] for i in range(2)]
        PT1 = [[sb(f"probs_k1_{x}_{i}", [P, H, P], F16) for x in range(2)] for i in range(2)]
        pf = [sb(f"probs_full{i}", [P, 512]) for i in range(3)]
        shift = sb("log_2048", [P, 1])
        mx = sb("row_max", [P, 2, H])
        mT = [sb("negmax_hi", [H, S], F32R), sb("negmax_lo", [H, S], F32R)]
        rden = sb("rden", [P, H // 2])
        on = sb("attn_norm", [P, 2, D])
        bqk = sb("bqk", [P, 2, 2])
        bvb = sb("bv_bcast", [P, D])
        rw1s = sb("rw1s", [P, 2, P])
        tick = sb("tick", [P, 2])
        padding = sb("pad_steps", [P, 32])
        st = sb("stats", [P, 4, 6])
        mv = sb("mean_var", [P, 4, 2])
        rs = sb("rstd", [P, 4, 4])
        hn2T = sb("hn2T", [P, 2, S])
        vf = small[:, 0:512].rearrange("p (t d) -> p t d", t=2)
        osum = small[:, 512:640].rearrange("p (h d) -> p h d", d=HD)
        rh_buf = small[:, 640:640 + S]
        SR = [ps(f"scores_ps{i}", [P, 512]) for i in range(2)]
        TR = [ps(f"scoresT_ps{i}", [P, 512]) for i in range(2)]
        OP = [ps(f"out_ps{i}", [P, 512]) for i in range(2)]
        M = [ps(f"mix_ps{i}", [P, 2, 256]) for i in range(2)]

        (c_in, h_last, filled, stack_filled, chain, ln1_done, ln2_done, xT_ps, xT_hi, xT_lo, q_ps, k_ps, v_ps, qk_hi, q_lo, k_lo, v_done,
         q_written, k_written, stack_in, s_ps, s_max, m_ps, m_hi, m_lo, m_in, st_ps, exp_done, pa_done, pb_done, pc_done, o_ps, o_left, o_done,
         v_sum, v_hi, v_rest, v_mid,
         h_done, lnA_done, rest_done, lnB_done, hT_ps, hT_done, rh_ps, rh_done, router_dma) = (sem("a_" + n) for n in (
             "c_in", "h_last", "filled", "stack_filled", "chain", "ln1_done", "ln2_done", "xT_ps", "xT_hi", "xT_lo", "q_ps", "k_ps", "v_ps",
             "qk_hi", "q_lo", "k_lo", "v_done", "q_written", "k_written", "stack_in", "s_ps", "s_max", "m_ps", "m_hi", "m_lo",
             "m_in", "st_ps", "exp_done", "pa_done", "pb_done", "pc_done", "o_ps", "o_left", "o_done",
             "v_sum", "v_hi", "v_rest", "v_mid", "h_done", "lnA_done", "rest_done",
             "lnB_done", "hT_ps", "hT_done", "rh_ps", "rh_done", "router_dma"))
        block = ctx.enter_context(nc.Block())
        A, V = nc.scalar, nc.vector

        def turns(eng, one):
            for i in range(-3, 2):
                one(i, i % 4)
            with eng.Fori(2, B - 5, 4) as i:
                for y in range(4):
                    one(i + y, (2 + y) % 4)
            for i in range(B - 2, B + 2):
                one(i, i % 4)

        exps_of = [[]] * 2 + [[n, n + 1] for n in range(0, NB, 2)] + [[]] * 4
        scores_of = [[], [0], [1], [2, 3], [4], [5, 6], [7], [8, 9], [10, 11], [], [], []]
        has = lambda i, d: not isinstance(i, int) or 0 <= i + d < B
        tiles = lambda b: slice(2 * b, 2 * b + 2) if isinstance(b, int) else bass.ds(2 * b, 2)

        def v_part(y, x):
            return V1[(y + 2) % 4][:, :, :, x * HD:(x + 1) * HD]

        def probs(p, x, n):
            g, y = n // 3, n % 3
            return PT1[p][x][:, 4 * g:4 * g + 4, :] if y == 2 else PT0[p][x][:, 4 * g + 2 * y:4 * g + 2 * y + 2, :]

        @block.gpsimd
        def _(g):
            for p in range(2):
                nc.gpsimd.memset(QS[p][:].bitcast(F32), 0.0).then_inc(stack_filled, 1)
                g.wait_ge(stack_filled, 2 * p + 1)
                nc.gpsimd.memset(KS[p][96:P].bitcast(F32), 1.0).then_inc(stack_filled, 1)
                g.wait_ge(stack_filled, 2 * p + 2)

            def one(i, y):
                if has(i, 0):
                    for n in range(NB):
                        if n % 3 < 2:
                            g.wait_ge(pa_done, NB * i + n + 1)
                            nc.gpsimd.tensor_tensor(probs(y % 2, 1, n), pf[n % 3][:].rearrange("p (a q) -> p a q", a=2),
                                                    probs(y % 2, 0, n), ALU.subtract).then_inc(pb_done, 1)
                heads_of = lambda t: t.rearrange("p t (h d) -> p t h d", d=HD)
                if has(i, 2):
                    g.wait_ge(v_hi, i + 3)
                    nc.gpsimd.tensor_tensor(heads_of(vf), heads_of(vf), v_part(y, 0), ALU.subtract).then_inc(v_rest, 1)
                if has(i, -2):
                    g.wait_ge(lnA_done, i - 1)
                    g.wait_ge(hT_ps, i - 1)
                    nc.gpsimd.tensor_tensor(hn2[:], hn2[:], lnA[:, tiles(i - 2), :], ALU.subtract).then_inc(rest_done, 1)
                if has(i, 2):
                    g.wait_ge(v_mid, i + 3)
                    nc.gpsimd.tensor_tensor(v_part(y, 2), heads_of(vf), v_part(y, 1), ALU.subtract).then_inc(v_done, 1)
            turns(g, one)

        @block.sync
        def _(sp):
            with nc.allow_non_contiguous_dma(reason="biases, once"):
                sp.dma_start(bqk[:, 0, :], bq.rearrange("(t g) d -> (g d) t", t=2)).then_inc(c_in, 16)
                sp.dma_start(bqk[:, 1, :], bk.rearrange("(t g) d -> (g d) t", t=2)).then_inc(c_in, 16)
            sp.dma_start(bvb[:], bv.rearrange("(o h) d -> o (h d)", o=1).broadcast_to([P, D])).then_inc(c_in, 16)
            sp.dma_start(rw1s[:], rw1.rearrange("(t p) n -> p t n", p=P)).then_inc(router_dma, 16)
            n0 = 3 * NT // 4
            sp.dma_start(hacc[:, n0:NT, :], h_dram.rearrange("(n p) w -> p n w", p=P)[:, n0:NT, :]).then_inc(h_last, 16)
            sp.wait_ge(stack_filled, 4)

            def one(i, y):
                p = y % 2
                if has(i, 2):
                    b = i + 2
                    sp.wait_ge(q_lo, 2 * (b + 1))
                    for x in range(2):
                        sp.dma_start(q_dram[p, x].rearrange("(f p) q -> p f q", p=P), qf[x][:].bitcast(F32)).then_inc(q_written, 16)
                    sp.wait_ge(k_lo, 2 * (b + 1))
                    for x in range(2):
                        if x and has(i, 0):
                            sp.wait_ge(st_ps, NB * (i + 1))
                        sp.dma_start(k_dram[p, x].rearrange("(f p) q -> p f q", p=P), kf[x][:].bitcast(F32)).then_inc(k_written, 16)
                    for written, dram, stack, third in ((q_written, q_dram, QS[p], 0), (k_written, k_dram, KS[p], 1)):
                        sp.wait_ge(written, 32 * (b + 1))
                        src = dram[p].rearrange("x (j a d) q -> a x d j q", a=2, d=HD)
                        for a in range(2):
                            for t, x in enumerate((0, 1, 0) if third == 0 else (0, 0, 1)):
                                r = 48 * a + 16 * t
                                dst = stack[r:r + HD, :, a, :] if third == 0 else stack[r:r + HD]
                                sp.dma_start(dst.bitcast(F32), src[a, x]).then_inc(stack_in, 16)
                if has(i, 1):
                    sp.wait_ge(m_lo, i + 2)
                    for x in range(2):
                        sp.dma_start(QS[1 - p][96 + x:97 + x].rearrange("o j a q -> o (j a) q").bitcast(F32),
                                     mT[x][:].bitcast(F32)).then_inc(m_in, 16)
                if isinstance(i, int) and i == B - 1:
                    sp.wait_ge(st_ps, NB * (B - 1))
                    sp.wait_ge(router_dma, 16 * (B - 2))
                    sp.dma_start(rh[:, 0:(B - 3) * S], rh_dram[:, 0:(B - 3) * S]).then_inc(router_dma, 16)
                if isinstance(i, int) and i >= B - 1:
                    sp.wait_ge(rh_done, i - 1)
                    sp.dma_start(rh[:, (i - 2) * S:(i - 1) * S], rh_buf).then_inc(router_dma, 16)
                elif has(i, -2):
                    cols = slice((i - 2) * S, (i - 1) * S) if isinstance(i, int) else bass.ds((i - 2) * S, S)
                    sp.wait_ge(rh_done, i - 1)
                    sp.dma_start(rh_dram[:, cols], rh_buf).then_inc(router_dma, 16)
            turns(sp, one)
            sp.wait_ge(router_dma, 16 * (B + 2))

        @block.tensor
        def _(pe):
            pe.wait_ge(router_dma, 16)
            pe.wait_ge(filled, 6)

            def project(m, bank, o, done):
                W = WT[m]
                n = 0
                for kt in range(2):
                    for wi, xi in ((0, 0), (0, 1), (1, 0)):
                        if m == "v":
                            lhsT, rhs = xT[xi][:, kt, o * P:(o + 1) * P], W[wi][:, kt, :]
                        else:
                            lhsT, rhs = W[wi][:, kt, o * P:(o + 1) * P], xT[xi][:, kt, :]
                        ins = pe.matmul(M[bank][:, o, :], lhsT, rhs, start=(n == 0), stop=(n == 5))
                        n += 1
                if o:
                    ins.then_inc(done, 1)

            def scores(b, p, n):
                if n == 0:
                    pe.wait_ge(stack_in, 192 * (b + 1))
                if n >= 2 or not isinstance(b, int) or b:
                    pe.wait_ge(s_max, NB * b + n - 1)
                bank = SR[n % 2]
                if n < 4:
                    for x in range(4):
                        j, a = 2 * n + x // 2, x % 2
                        pe.matmul(bank[:, x * P:(x + 1) * P], QS[p][0:96, j, a, 0:P], KS[p][0:96, j, 0:P],
                                  start=(x == 0), stop=False, skip_group_check=True)
                    ins = pe.matmul(bank[:].rearrange("p (a k) -> p a k", a=4), identb[:], maskS[:].broadcast_to([P, 4, P]),
                                    start=False, stop=True, skip_group_check=True)
                else:
                    j = n - 4
                    for a in range(2):
                        pe.matmul(bank[:, a * S:(a + 1) * S], QS[p][0:96, j, a, P:S], KS[p][0:96, j, :],
                                  start=(a == 0), stop=False, skip_group_check=True)
                    ins = pe.matmul(bank[:].rearrange("p (a k) -> p a k", a=2)[:, :, P:S], identb[:], maskS[:].broadcast_to([P, 2, P]),
                                    start=False, stop=True, skip_group_check=True)
                ins.then_inc(s_ps, 1)

            def exp_scores(b, p, n):
                if n == 0:
                    pe.wait_ge(m_in, 32 * (b + 1))
                if n >= 2 or not isinstance(b, int) or b:
                    pe.wait_ge(exp_done, NB * b + n - 1)
                bank, g, y = TR[n % 2], n // 3, n % 3
                if y < 2:
                    j = 2 * g + y
                    pe.matmul(bank[:], KS[p][0:98, j, 0:P], QS[p][0:98, j, :, :].rearrange("p a q -> p (a q)"),
                              start=True, stop=False, skip_group_check=True)
                    ins = pe.matmul(bank[:].rearrange("p (a q) -> p a q", a=2)[:, :, 0:P], identb[:], maskT[:].broadcast_to([P, 2, P]),
                                    start=False, stop=True, skip_group_check=True)
                else:
                    for x in range(2):
                        j = 2 * g + x
                        pe.matmul(bank[:].rearrange("p (x a q) -> p x a q", x=2, a=2)[:, x], KS[p][0:98, j, P:S],
                                  QS[p][0:98, j, :, P:S], start=(x == 0), stop=False, skip_group_check=True)
                    ins = pe.matmul(bank[:].rearrange("p (a k) -> p a k", a=4), identb[:], maskT[:].broadcast_to([P, 4, P]),
                                    start=False, stop=True, skip_group_check=True)
                ins.then_inc(st_ps, 1)

            def times_v(b, p, vb, s):
                u, hs = ((s // 2, range(4 * s, 4 * s + 4)) if s < 4 else
                         (2, range(2 * s - 8, 2 * s - 6)) if s < 8 else (3, range(2 * s - 8, 2 * s - 6)))
                t, first, last = u // 2, s in (0, 2, 4, 8), s in (1, 3, 7, 11)
                if s == 0:
                    pe.wait_ge(v_done, b + 1)
                if first:
                    pe.wait_ge((pb_done, pc_done)[t], (8, 4)[t] * b + (4, 8, 2, 4)[u])
                    if u >= 2 or not isinstance(b, int) or b:
                        pe.wait_ge(o_left, 2 * (4 * b + u - 1))
                for h in hs:
                    o = OP[u % 2][:, (h % 8) * VW:(h % 8 + 1) * VW]
                    n, N = 0, 2 * (t + 1)
                    for kt in range(t + 1):
                        for x in range(2):
                            src = PT1[p][x][:, h, :] if kt else PT0[p][x][:, h, t * P:(t + 1) * P]
                            ins = pe.matmul(o, src, V1[vb][:, kt, h, :], start=(n == 0), stop=(n == N - 1))
                            n += 1
                if last:
                    ins.then_inc(o_ps, 1)

            def one(i, y):
                for s in range(12):
                    for x in range(2):
                        if x == 1 and has(i, -1):
                            times_v(i - 1, (y - 1) % 2, (y - 1) % 4, s)
                        if has(i, 1) and x < len(scores_of[s]):
                            scores(i + 1, (y + 1) % 2, scores_of[s][x])
                        if has(i, 0) and x < len(exps_of[s]):
                            exp_scores(i, y % 2, exps_of[s][x])
                    if has(i, 2):
                        b = i + 2
                        if s == 0:
                            pe.wait_ge(ln1_done, b + 1)
                            if has(i, 0):
                                pe.wait_ge(m_lo, i + 1)
                            for tt in range(2):
                                for kt in range(2):
                                    ins = pe.transpose(M[0][:, kt, tt * P:(tt + 1) * P], hn1[:, tt, kt * P:(kt + 1) * P], ident[:])
                            ins.then_inc(xT_ps, 1)
                        if s == 1:
                            pe.wait_ge(xT_lo, b + 1)
                            if has(i, -3):
                                if isinstance(i, int):
                                    pe.wait_ge(rh_done, i - 2)
                            if has(i, 1):
                                pe.wait_ge(v_sum, i + 2)
                            project("q", 1, 0, q_ps)
                        if s == 2:
                            project("q", 1, 1, q_ps)
                        if s == 3:
                            project("k", 0, 0, k_ps)
                        if s == 4:
                            project("k", 0, 1, k_ps)
                        if s == 5:
                            pe.wait_ge(q_lo, 2 * (b + 1))
                            project("v", 1, 0, v_ps)
                        if s == 6:
                            project("v", 1, 1, v_ps)
                    if has(i, 1) and s == 9:
                        pe.wait_ge(s_max, NB * (i + 2))
                        if has(i, 2):
                            pe.wait_ge(k_lo, 2 * (i + 3))
                        elif isinstance(i, int) and i > 2:
                            pe.wait_ge(hT_done, i - 2)
                        for tt in range(2):
                            ins = pe.transpose(M[0][0:H, 0, tt * P:(tt + 1) * P], mx[:, tt, :], ident[:])
                        ins.then_inc(m_ps, 1)
                    if has(i, -2) and s == 10:
                        b = i - 2
                        pe.wait_ge(ln2_done, b + 1)
                        if has(i, 1):
                            pe.wait_ge(m_lo, i + 2)
                        elif isinstance(b, int) and b:
                            pe.wait_ge(hT_done, b)
                        for tt in range(2):
                            for kt in range(2):
                                ins = pe.transpose(M[0][:, kt, tt * P:(tt + 1) * P], hn2[:, tt, kt * P:(kt + 1) * P], ident[:])
                        ins.then_inc(hT_ps, 1)
                if has(i, -2):
                    b = i - 2
                    pe.wait_ge(hT_done, b + 1)
                    if has(i, 2):
                        pe.wait_ge(v_sum, i + 3)
                    elif isinstance(b, int) and b:
                        pe.wait_ge(rh_done, b)
                    for kt in range(2):
                        ins = pe.matmul(M[1][:, 0, :], rw1s[:, kt, :], hn2T[:, kt, :], start=(kt == 0), stop=(kt == 1))
                    ins.then_inc(rh_ps, 1)
            turns(pe, one)

        @block.scalar
        def _(act):
            act.wait_ge(c_in, 16 * 3)
            act.wait_ge(filled, 6)

            def exps(b, p, n):
                act.wait_ge(st_ps, NB * b + n + 1)
                if n == 0 and (not isinstance(b, int) or b >= 2):
                    act.wait_ge(o_ps, 4 * (b - 1))
                if n >= 3 or not isinstance(b, int) or b:
                    if n % 3 < 2:
                        act.wait_ge(pb_done, 8 * b + 2 * (n // 3) + n % 3 - 1)
                    else:
                        act.wait_ge(pc_done, 4 * b + n // 3)
                A.activation(pf[n % 3][:], TR[n % 2][:], ACT.Exp, bias=shift[:], scale=float(HD) ** -0.5).then_inc(exp_done, 1)

            def probs_hi(b, p, n):
                act.wait_ge(exp_done, NB * b + n + 1)
                A.activation(probs(p, 0, n), pf[n % 3][:].rearrange("p (a q) -> p a q", a=4 if n % 3 == 2 else 2),
                             ACT.Copy).then_inc(pa_done, 1)

            def parts_hi(b, m, bank, full, dst):
                act.wait_ge(full, b + 1)
                if not isinstance(b, int) or b:
                    act.wait_ge((q_written, k_written)[m], 32 * b)
                for ft in range(2):
                    A.activation(dst[0][:, ft, :], M[bank][:, ft, :], ACT.Identity,
                                 bias=bqk[:, m, ft:ft + 1]).then_inc(qk_hi, 1)

            def one(i, y):
                for s in range(12):
                    if has(i, 2) and s == 0:
                        act.wait_ge(xT_ps, i + 3)
                        A.activation(xT[0][:], M[0][:], ACT.Copy).then_inc(xT_hi, 1)
                    if has(i, 0):
                        for n in exps_of[s]:
                            exps(i, y % 2, n)
                            if n:
                                probs_hi(i, y % 2, n - 1)
                    if has(i, 2) and s == 2:
                        parts_hi(i + 2, 0, 1, q_ps, qf)
                    if has(i, 2) and s == 4:
                        parts_hi(i + 2, 1, 0, k_ps, kf)
                    if has(i, -2):
                        b = i - 2
                        if s == 8:
                            act.wait_ge(ln2_done, b + 1)
                            A.activation(lnA[:, tiles(b), :], hn2[:], ACT.Copy).then_inc(lnA_done, 1)
                        if s == 10:
                            act.wait_ge(hT_ps, b + 1)
                            A.activation(hn2T[:], M[0][:], ACT.Copy).then_inc(hT_done, 1)
                    if has(i, 0) and s == 8:
                        probs_hi(i, y % 2, NB - 1)
                    if has(i, 1) and s == 9:
                        act.wait_ge(m_ps, i + 2)
                        if has(i, 0):
                            act.wait_ge(m_in, 32 * (i + 1))
                        A.activation(mT[0][:], M[0][0:H, 0, :], ACT.Copy, scale=-1.0).then_inc(m_hi, 1)
                    if has(i, 2) and s in (9, 11):
                        act.wait_ge(v_rest if s == 11 else v_sum, i + 3)
                        A.activation(v_part(y, (s - 9) // 2), vf.rearrange("p t (h d) -> p t h d", d=HD),
                                     ACT.Copy).then_inc(v_mid if s == 11 else v_hi, 1)
                if has(i, -2):
                    b = i - 2
                    act.wait_ge(rest_done, b + 1)
                    A.activation(lnB[:, tiles(b), :], hn2[:], ACT.Copy, scale=2048.0).then_inc(lnB_done, 1)
                    act.wait_ge(rh_ps, b + 1)
                    if not isinstance(b, int) or b:
                        act.wait_ge(router_dma, 16 * (b + 2 if isinstance(b, int) and b > B - 3 else b + 1))
                    A.activation(rh_buf, M[1][:, 0, :], ACT.Copy).then_inc(rh_done, 1)
            turns(act, one)

        @block.vector
        def _(v):
            for p in range(4):
                V.memset(V1[p][:, :, :, 3 * HD:VW], 1.0).then_inc(filled, 1)
            V.memset(mv[:], 1.0).then_inc(filled, 1)
            V.memset(shift[:], math.log(2048.0)).then_inc(filled, 1)
            v.wait_ge(c_in, 16 * 3)
            v.wait_ge(filled, 6)
            O = [OP[u][:, 0:8 * VW].rearrange("p (h c) -> p h c", c=VW) for u in range(2)]
            xx, xh, yy, u = rs[:, 0], rs[:, 1], rs[:, 2], rs[:, 3]
            STEPS = 5 + 5 + 13 + 1 + 1

            def max_scores(b, n):
                v.wait_ge(s_ps, NB * b + n + 1)
                if n < 4:
                    V.tensor_reduce(mx[:, 0, 4 * n:4 * n + 4], SR[n % 2][:].rearrange("p (a k) -> p a k", a=4), AX.X,
                                    ALU.max).then_inc(s_max, 1)
                else:
                    j = n - 4
                    V.tensor_reduce(mx[:, 1, 2 * j:2 * j + 2], SR[n % 2][:].rearrange("p (a k) -> p a k", a=2), AX.X,
                                    ALU.max).then_inc(s_max, 1)

            def parts_lo(b, m, bank, src, done):
                v.wait_ge(qk_hi, 4 * b + 2 * m + 2)
                if not isinstance(b, int) or b:
                    v.wait_ge((q_written, k_written)[m], 32 * b)
                for ft in range(2):
                    V.scalar_tensor_tensor(src[1][:, ft, :], M[bank][:, ft, :], bqk[:, m, ft:ft + 1],
                                           src[0][:, ft, :].bitcast(F32), ALU.add, ALU.subtract).then_inc(done, 1)

            def outputs(b, u):
                v.wait_ge(o_ps, 4 * b + u + 1)
                if u or not isinstance(b, int) or b:
                    v.wait_ge(o_done, 4 * b + u)
                V.tensor_reduce(osum, O[u % 2][:, :, 0:3 * HD].rearrange("p h (x d) -> p h d x", d=HD), AX.X,
                                ALU.add).then_inc(o_left, 1)
                V.reciprocal(rden[:], O[u % 2][:, :, 3 * HD]).then_inc(o_left, 1)
                v.wait_ge(o_left, 2 * (4 * b + u + 1))
                V.tensor_tensor(on[:, u // 2, (u % 2) * P:(u % 2 + 1) * P].rearrange("p (h d) -> p h d", d=HD), osum,
                                rden[:].rearrange("p (h o) -> p h o", o=1).broadcast_to([P, H // 2, HD]),
                                ALU.mult).then_inc(o_done, 1)

            def newton(c, k):
                c.wait()
                if k == 0:
                    c.step(V.tensor_scalar(xx, mv[:, :, 1], EPS, None, ALU.add))
                elif k == 1:
                    c.step(V.tensor_scalar(xh, xx, -0.5, None, ALU.mult))
                    c.step(V.tensor_scalar(u.bitcast(I32), xx.bitcast(I32), 1, None, ALU.logical_shift_right))
                elif k == 2:
                    c.step(V.tensor_scalar(yy.bitcast(I32), u.bitcast(I32), -1.0, float(0x5F3759DF), ALU.mult, ALU.add))
                elif k % 3 == 0:
                    c.step(V.tensor_tensor(u, yy, yy, ALU.mult))
                elif k % 3 == 1:
                    c.step(V.tensor_tensor(u, u, xh, ALU.mult))
                else:
                    c.step(V.scalar_tensor_tensor(yy, u, 1.5, yy, ALU.add, ALU.mult))

            def normalise(c, b, k, dst, done):
                for tt in range(2):
                    ins = V.tensor_scalar(dst[:, tt, :], hacc[:, tiles(b), :][:, tt, :], mv[:, k + tt, 0:1], yy[:, k + tt:k + tt + 1],
                                          ALU.subtract, ALU.mult)
                    if tt == 0:
                        c.step(ins)
                    else:
                        ins.then_inc(done, 1)

            def one(i, y):
                c = Chain(v, chain, STEPS, i + 3)
                if isinstance(i, int) and i == 0:
                    v.wait_ge(h_last, 16)
                pad = lambda n: [c.step(V.memset(padding[:, c.n:c.n + 1], 0.0)) for _ in range(n)]
                for s in range(12):
                    if s == 1 and has(i, 2):
                        v.wait_ge(xT_hi, i + 3)
                        V.tensor_tensor(xT[1][:], M[0][:], xT[0][:].bitcast(F32), ALU.subtract).then_inc(xT_lo, 1)
                    if s == 3 and has(i, 2):
                        parts_lo(i + 2, 0, 1, qf, q_lo)
                    if s == 5 and has(i, 2):
                        parts_lo(i + 2, 1, 0, kf, k_lo)
                    if s == 7 and has(i, 2):
                        v.wait_ge(v_ps, i + 3)
                        if has(i, 1):
                            v.wait_ge(v_done, i + 2)
                        V.tensor_tensor(vf, M[1][:], bvb[:].rearrange("p (o n) -> p o n", o=1).broadcast_to([P, 2, D]),
                                        ALU.add).then_inc(v_sum, 1)
                    if has(i, 1):
                        if s == 1 and has(i, 0):
                            v.wait_ge(m_ps, i + 1)
                        for n in scores_of[s]:
                            max_scores(i + 1, n)
                    if s == 0:
                        if has(i, 2):
                            c.wait()
                            if has(i, 1):
                                v.wait_ge(xT_ps, i + 2)
                            normalise(c, i + 2, 2, hn1, ln1_done)
                        else:
                            pad(1)
                    if s == 0 and has(i, -2):
                        outputs(i - 2, 3)
                    if s in (4, 6, 7, 9) and has(i, 0):
                        g = (4, 6, 7, 9).index(s)
                        v.wait_ge(pa_done, NB * i + 3 * g + 3)
                        V.tensor_tensor(probs(y % 2, 1, 3 * g + 2), pf[2][:].rearrange("p (a q) -> p a q", a=4),
                                        probs(y % 2, 0, 3 * g + 2), ALU.subtract).then_inc(pc_done, 1)
                    if s in (2, 4, 8) and has(i, -1):
                        outputs(i - 1, (2, 4, 8).index(s))
                    if s == 0:
                        if has(i, -2):
                            v.wait_ge(o_done, 4 * (i - 1))
                            h_ = hacc[:, tiles(i - 2), :]
                            V.tensor_tensor(h_, h_, on[:], ALU.add).then_inc(h_done, 1)
                            v.wait_ge(h_done, i - 1)
                            c.step(V.memset(tick[:, 0:1], 0.0))
                            for tt in range(2):
                                c.step(V.bn_stats(st[:, tt, :], hacc[:, tiles(i - 2), :][:, tt, :]))
                        else:
                            pad(3)
                        if has(i, 3):
                            for tt in range(2):
                                c.step(V.bn_stats(st[:, 2 + tt, :], hacc[:, tiles(i + 3), :][:, tt, :]))
                        else:
                            pad(2)
                    if s == 1:
                        c.wait()
                        c.step(V.memset(tick[:, 1:2], 0.0))
                        for tt in range(4):
                            if has(i, -2 if tt < 2 else 3):
                                c.step(V.bn_aggr(mv[:, tt, :], st[:, tt, :]))
                            else:
                                pad(1)
                    if s == 2:
                        for k in range(4):
                            newton(c, k)
                    if s == 3:
                        for k in range(4, 6):
                            newton(c, k)
                    if s == 4:
                        for k in range(6, 9):
                            newton(c, k)
                    if s == 5:
                        for k in range(9, 12):
                            newton(c, k)
                    if s == 6:
                        c.wait()
                        if has(i, -2):
                            if not has(i, 2) and isinstance(i, int) and i - 2 > 0:
                                v.wait_ge(lnB_done, i - 2)
                            normalise(c, i - 2, 0, hn2, ln2_done)
                        else:
                            pad(1)
                    if s == 9 and has(i, 1):
                        v.wait_ge(m_hi, i + 2)
                        if has(i, 0):
                            v.wait_ge(m_in, 32 * (i + 1))
                        V.scalar_tensor_tensor(mT[1][:], M[0][0:H, 0, :], -1.0, mT[0][:].bitcast(F32), ALU.mult,
                                               ALU.subtract).then_inc(m_lo, 1)
                c.end()
            turns(v, one)


def top_tokens(nc, rh, rw2, posT, wT, iota, ident, dims):
    B, S, D, E, F, CAP = dims
    R = B * E // P
    IR = B // R
    with ExitStack() as ctx:
        sb = lambda n, s, d=F32: ctx.enter_context(nc.sbuf_tensor(n, s, d))
        sem = lambda n: ctx.enter_context(nc.semaphore(n))
        hid = sb("hid", [P, B * S])
        rw2s = sb("rw2s", [P, E])
        rw2p = sb("rw2_shifted", [P, IR, P])
        L = sb("L", [P, R, S])
        wk = sb("work", [P, R, S])
        top = sb("top8", [P, R, CAP])
        nm = sb("neg_max", [P, R])
        ex = sb("ex", [P, R, S])
        Z = sb("Z", [P, R])
        sel = sb("sel", [P, R, S])
        cum = sb("cum", [P, R, S])
        pos = sb("pos", [P, R, S])
        tot = sb("tot", [P, R])
        ones = sb("ones_row", [P, CAP])
        r1 = sb("w_rest", [P, 2, B * E])
        posP = ctx.enter_context(nc.psum_tensor("pos_ps", [P, 2, B * E], F32))
        wP = ctx.enter_context(nc.psum_tensor("w_ps", [P, 2, B * E], F32))
        LP = [ctx.enter_context(nc.psum_tensor(f"logit_ps{r}", [P, 512], F32)) for r in range(R)]
        rw2_in, rw2_done, silu_done, lg_ps = sem("rw2_in"), sem("rw2_done"), sem("silu_done"), sem("lg_ps")
        nm_done, ex_done, chain, pos_done, w_done, pos_ps, w_ps = (sem(n) for n in (
            "nm_done", "ex_done", "top_chain", "pos_done", "w_done", "pos_psd", "w_psd"))
        block = ctx.enter_context(nc.Block())
        V = nc.vector

        @block.sync
        def _(sp):
            sp.dma_start(rw2s[:], rw2).then_inc(rw2_in, 16)

        @block.scalar
        def _(act):
            for n in range(B // 2):
                nc.scalar.activation(hid[:, 512 * n:512 * (n + 1)], rh[:, 512 * n:512 * (n + 1)], ACT.Silu).then_inc(silu_done, 1)
            for r in range(R):
                act.wait_ge(nm_done, r + 1)
                nc.scalar.activation(ex[:, r], L[:, r], ACT.Exp, bias=nm[:, r:r + 1], accum_out=Z[:, r:r + 1]).then_inc(ex_done, 1)

        @block.tensor
        def _(pe):
            pe.wait_ge(rw2_done, 1 + IR)
            for b in range(B):
                pe.wait_ge(silu_done, b // 2 + 1)
                ins = pe.matmul(LP[b // IR][:, 0:S], rw2p[:, b % IR, :], hid[:, b * S:(b + 1) * S], start=(b % IR == 0),
                                stop=(b % IR == IR - 1))
                if b % IR == IR - 1:
                    ins.then_inc(lg_ps, 1)
            for done, src, dst, full in ((pos_done, pos, posP, pos_ps), (w_done, ex, wP, w_ps)):
                pe.wait_ge(done, R)
                for r in range(R):
                    for tt in range(2):
                        ins = pe.transpose(dst[:, tt, r * P:(r + 1) * P], src[:, r, tt * P:(tt + 1) * P], ident[:])
                ins.then_inc(full, 1)

        @block.vector
        def _(v):
            c = Chain(v, chain, 0, 0)
            c.step(V.memset(ones[:], 1.0))
            c.wait()
            c.step(V.tensor_tensor_scan(iota[:], ones[:], ones[:], 0.0, ALU.add, ALU.bypass))
            V.memset(rw2p[:], 0.0).then_inc(rw2_done, 1)
            v.wait_ge(rw2_in, 16)
            v.wait_ge(rw2_done, 1)
            for i in range(IR):
                V.tensor_copy(rw2p[:, i, i * E:(i + 1) * E], rw2s[:]).then_inc(rw2_done, 1)
            LAG = 2
            for n in range(CAP // 8 + LAG * (R - 1)):
                rounds = [(n - LAG * r, r) for r in range(R) if 0 <= n - LAG * r < CAP // 8]
                for k, r in rounds:
                    if k == 0:
                        v.wait_ge(lg_ps, r + 1)
                        c.step(V.tensor_copy(L[:, r], LP[r][:, 0:S]))
                    c.wait()
                    c.step(V.max(top[:, r, 8 * k:8 * k + 8], (wk if k else L)[:, r]))
                    if k == 0:
                        c.wait()
                        V.tensor_scalar(nm[:, r:r + 1], top[:, r, 0:1], -1.0, None, ALU.mult).then_inc(nm_done, 1)
                for k, r in rounds:
                    c.wait()
                    c.step(V.match_replace(wk[:, r], top[:, r, 8 * k:8 * k + 8], (wk if k else L)[:, r], BIG))
            c.wait()
            c.step(V.tensor_scalar(sel[:], wk[:], BIG, None, ALU.is_le))
            c.wait()
            for r in range(R):
                c.step(V.tensor_tensor_scan(cum[:, r], sel[:, r], sel[:, r], 0.0, ALU.add, ALU.bypass))
            c.wait()
            V.tensor_tensor(pos[:], cum[:], sel[:], ALU.mult).then_inc(pos_done, R)
            v.wait_ge(ex_done, R)
            c.step(V.reciprocal(Z[:], Z[:]))
            c.wait()
            for r in range(R):
                c.step(V.scalar_tensor_tensor(wk[:, r], ex[:, r], Z[:, r:r + 1], sel[:, r], ALU.mult, ALU.mult))
            c.wait()
            c.step(V.tensor_reduce(tot[:], wk[:], AX.X, ALU.add))
            c.wait()
            c.step(V.tensor_scalar(tot[:], tot[:], 1e-9, None, ALU.add))
            c.wait()
            c.step(V.reciprocal(tot[:], tot[:]))
            c.wait()
            for r in range(R):
                V.tensor_scalar(ex[:, r], wk[:, r], tot[:, r:r + 1], None, ALU.mult).then_inc(w_done, 1)
            v.wait_ge(pos_ps, 1)
            c.step(V.tensor_copy(posT[:], posP[:]))
            v.wait_ge(w_ps, 1)
            c.step(V.tensor_copy(wT[:, :, :, 0], wP[:]))
            c.wait()
            c.step(V.tensor_tensor(r1[:], wP[:], wT[:, :, :, 0], ALU.subtract))
            c.wait()
            c.step(V.tensor_copy(wT[:, :, :, 1], r1[:]))
            c.wait()
            c.step(V.tensor_tensor(r1[:], r1[:], wT[:, :, :, 1], ALU.subtract))
            c.wait()
            c.step(V.tensor_copy(wT[:, :, :, 2], r1[:]))
            c.wait()


def ffn(nc, ctx, w1, w2, w3, hacc, lnA, lnB, posT, wT, iota, ident16, out, dims):
    B, S, D, E, F, CAP = dims
    PR = E // 2
    FT = F // P
    HB = B // 2
    N = HB * CAP
    ST = N // P
    assert (FT, HB, N, CAP) == (4, 8, 512, 64)
    sb = lambda n, s, d=F32: ctx.enter_context(nc.sbuf_tensor(n, s, d))
    sem = lambda n: ctx.enter_context(nc.semaphore(n))
    ps = lambda n, s, d=F32: ctx.enter_context(nc.psum_tensor(n, s, d))
    raw = [sb(f"w_raw{i}", [P, 1024]) for i in range(2)]
    Wx = [[[sb(f"w{m + 1}_{x}{i}", [P, 1024], F32R) for x in ("hi", "lo")] for m in range(3)] for i in range(2)]
    OH = [sb(f"onehot{i}", [P, 2, B, 2, CAP], F16) for i in range(2)]
    ohT = [sb(f"onehotT{i}", [P, 2, S], F32R) for i in range(2)]
    xg = [[sb(f"xg_{x}{i}", [P, 2, N], F32R) for x in ("hi", "lo")] for i in range(2)]
    sg = [sb(f"silu_g{i}", [P, N]) for i in range(2)]
    hf = [sb(f"hidden{i}", [P, N]) for i in range(2)]
    hp = [sb(f"hidden_{x}", [P, FT, N], F32R) for x in ("hi", "lo")]
    Y = [sb(f"y_{x}", [P, B, D], F32R) for x in ("hi", "lo")]
    wpair = [sb(f"pair_weight{i}", [P, 2, B, 6], BF16) for i in range(2)]
    ws = [sb(f"slot_weight{i}", [P, 2, HB]) for i in range(2)]
    GP = [ps(f"gate_ps{i}", [P, N]) for i in range(2)]
    VP = [ps(f"value_ps{i}", [P, N]) for i in range(2)]
    YP = [ps(f"y_ps{i}", [P, 2, D]) for i in range(2)]
    XP = ps("gather_ps", [P, N])
    TP = ps("turn_ps", [P, 512])
    TP16 = TP[:, 0:256].bitcast(F16)

    zero = sb("zero_col", [P, 1])
    zeroed = sem("zeroed")
    raw_in = [sem(f"raw_in{i}") for i in range(2)]
    (wsplit, oh_done, ws_ps, ws_done, g_ps, v_ps, silu_done, hf_done, hh_done, hl_done, gath_ps, xh_done, xl_done,
     y_ps, y_hi, y_lo, comb_ps, comb_add, oht_ps, oht_done, out_done) = (sem(n) for n in (
         "wsplit", "oh_done", "slotw_ps", "slotw_done", "s_g_ps", "s_v_ps", "silu_g_done", "hf_done", "hh_done",
         "hl_done", "s_gath_ps", "xh_done", "xl_done", "s_y_ps", "y_hi_done", "y_lo_done", "comb_ps", "comb_add",
         "oht_ps", "oht_done", "out_done"))
    block = ctx.enter_context(nc.Block())
    T, A, V = nc.tensor, nc.scalar, nc.vector
    PASSES = ((0, 0), (0, 1), (1, 0))

    def pairs(eng, one):
        one(0, 0, True, False)
        with eng.Fori(1, PR - 2, 2) as pr:
            one(pr, 1, False, False)
            one(pr + 1, 0, False, False)
        one(PR - 1, 1, False, True)

    later = lambda n: not isinstance(n, int) or n > 0

    @block.sync
    def _(sp):
        def one(pr, par, first, last):
            for e2 in range(2):
                for m, w in enumerate((w1, w2, w3)):
                    n = 3 * e2 + m
                    e = 2 * pr + e2 if isinstance(pr, int) else sp.snap(2 * pr + e2)
                    src = w[e] if isinstance(pr, int) else w[bass.ds(e, 1)].rearrange("o a b -> (o a) b")
                    if not first or n >= 2:
                        sp.wait_ge(wsplit, 12 * pr + 2 * (n - 1))
                    sp.dma_start(raw[n % 2][:].rearrange("p (t c) -> p t c", c=src.shape[1]),
                                 src.rearrange("(t p) c -> p t c", p=P)).then_inc(raw_in[n % 2], 16)
        pairs(sp, one)
        for s in range(B // 2):
            sp.wait_ge(comb_add, 2 * HB * (PR - 1) + 2 * s + 2)
            sp.dma_start(out.rearrange("b (t p) d -> p (b t) d", p=P)[:, 4 * s:4 * s + 4, :],
                         hacc[:, 4 * s:4 * s + 4, :]).then_inc(out_done, 16)
        sp.wait_ge(out_done, 16 * (B // 2))

    @block.gpsimd
    def _(g):
        nc.gpsimd.memset(zero[:], 0.0).then_inc(zeroed, 1)
        g.wait_ge(zeroed, 1)

        def one(pr, par, first, last):
            for e2 in range(2):
                if not first:
                    g.wait_ge(y_ps, 2 * (4 * (pr - 1) + 2 * e2 + 2))
                for m in range(3):
                    n = 3 * e2 + m
                    g.wait_ge(raw_in[n % 2], 16 * (3 * pr + n // 2 + 1))
                    hi, lo = Wx[e2][m]
                    nc.gpsimd.tensor_tensor(hi[:], raw[n % 2][:], zero[:].broadcast_to([P, 1024]), ALU.add).then_inc(wsplit, 1)
                    g.wait_ge(wsplit, 12 * pr + 2 * n + 1)
                    nc.gpsimd.tensor_tensor(lo[:], raw[n % 2][:], hi[:].bitcast(F32), ALU.subtract).then_inc(wsplit, 1)
        pairs(g, one)

    @block.tensor
    def _(pe):
        def gather(Tn, par, e2, c, n):
            m, part = n // 2, n % 2
            if n:
                pe.wait_ge((xl_done, xh_done)[part], 2 * Tn + (n + 1) // 2)
            elif later(Tn):
                pe.wait_ge(xl_done, 2 * Tn)
            src = (lnA, lnB)[part]
            for b in range(HB):
                for tt in range(2):
                    ins = pe.matmul(XP[:, b * CAP:(b + 1) * CAP], src[:, 2 * (HB * c + b) + tt, m * P:(m + 1) * P],
                                    OH[par][:, tt, HB * c + b, e2, :], start=(tt == 0), stop=(tt == 1))
            ins.then_inc(gath_ps, 1)

        def slot_weights(pr, par):
            if later(pr - 1):
                pe.wait_ge(oht_done, 8 * (pr - 1))
            for b in range(B):
                for tt in range(2):
                    ins = pe.matmul(TP[:, 256 + 6 * b:256 + 6 * b + 6], OH[par][:, tt, b].rearrange("p e s -> p (e s)"),
                                    wpair[par][:, tt, b, :], start=(tt == 0), stop=(tt == 1))
            ins.then_inc(ws_ps, 1)

        def turn_onehot(pp, par, s):
            if s or later(pp):
                pe.wait_ge(oht_done, 8 * pp + s)
            if s == 0:
                pe.wait_ge(ws_done, 4 * PR if isinstance(pp, int) and pp == PR - 1 else 4 * (pp + 2))
            for x in range(2):
                for tt in range(2):
                    ins = pe.transpose(TP16[:, x * S + tt * P:x * S + (tt + 1) * P],
                                       OH[par][:, tt, 2 * s + x].rearrange("p e s -> p (e s)"), ident16[:])
            ins.then_inc(oht_ps, 1)

        def combine(pp, s):
            pe.wait_ge(oht_done, 8 * pp + s + 1)
            for x in range(2):
                if s % 4:
                    pe.wait_ge(comb_add, 2 * HB * pp + 2 * s - 1 + x)
                for tt in range(2):
                    for y in range(2):
                        ins = pe.matmul(YP[x][:, tt, :], ohT[s % 2][:, x, tt * P:(tt + 1) * P], Y[y][:, 2 * s + x, :],
                                        start=(y == 0), stop=(y == 1))
                ins.then_inc(comb_ps, 1)

        def combine_two(pr, par, e2, c, ft, U, first):
            if e2 or first:
                return
            s = 4 * c + ft
            if ft == 0:
                pe.wait_ge(y_lo, 8 * U)
            combine(pr - 1, s)
            if s + 1 < 8:
                turn_onehot(pr - 1, 1 - par, s + 1)

        def unit(pr, par, e2, c, first, last):
            U = 4 * pr + 2 * e2 + c
            pe.wait_ge(xh_done, 2 * (U + 1))
            pe.wait_ge(xl_done, 2 * (U + 1))
            for ft in range(FT):
                for m, bank, used, full in ((0, GP, silu_done, g_ps), (1, VP, hf_done, v_ps)):
                    if m == 1 and ft:
                        combine_two(pr, par, e2, c, ft, U, first)
                    if ft >= 2 or later(U):
                        pe.wait_ge(used, 4 * U + ft - 1)
                    if ft == 0 and c == 0:
                        pe.wait_ge(wsplit, 12 * pr + 6 * e2 + 2 * (m + 1))
                    n = 0
                    for kt in range(2):
                        for wi, xi in PASSES:
                            ins = pe.matmul(bank[ft % 2][:], Wx[e2][m][wi][:, kt * F + ft * P:kt * F + (ft + 1) * P],
                                            xg[c][xi][:, kt, :], start=(n == 0), stop=(n == 5))
                            n += 1
                    ins.then_inc(full, 1)
                if c == 0:
                    gather(U + 1, par, e2, 1, ft)
                elif e2 == 0:
                    gather(U + 1, par, 1, 0, ft)
                elif not last:
                    if ft == 0:
                        pe.wait_ge(oh_done, 3 * (pr + 2))
                    gather(U + 1, 1 - par, 0, 0, ft)
                    if ft == 1:
                        slot_weights(pr + 1, 1 - par)
                if ft == 0:
                    combine_two(pr, par, e2, c, 0, U, first)
            if e2 == 0 and not first:
                pe.wait_ge(comb_add, 2 * HB * (pr - 1) + 8 * (c + 1))
            elif later(U):
                pe.wait_ge(y_lo, 8 * U)
            if c == 0:
                pe.wait_ge(wsplit, 12 * pr + 6 * e2 + 6)
            for ft in range(FT):
                pe.wait_ge(hl_done, 4 * U + ft + 1)
                for st in range(ST):
                    for q, (hi_, wi) in enumerate(PASSES):
                        ins = pe.matmul(YP[st // 2][:, st % 2, :], hp[hi_][:, ft, st * P:(st + 1) * P],
                                        Wx[e2][2][wi][:, ft * D:(ft + 1) * D], start=(ft == 0 and st % 2 == 0 and q == 0),
                                        stop=(ft == FT - 1 and q == 2), skip_group_check=True)
                    if ft == FT - 1 and st % 2 == 1:
                        ins.then_inc(y_ps, 1)

        def one(pr, par, first, last):
            if first:
                pe.wait_ge(oh_done, 3)
                for n in range(4):
                    gather(0, 0, 0, 0, n)
                slot_weights(0, 0)
            for e2 in range(2):
                for c in range(2):
                    unit(pr, par, e2, c, first, last)
            turn_onehot(pr, par, 0)
        pairs(pe, one)
        for s in range(8):
            if s < 7:
                turn_onehot(PR - 1, 1, s + 1)
            if s == 0:
                pe.wait_ge(y_lo, 8 * 4 * PR)
            elif s == 4:
                pe.wait_ge(comb_add, 2 * HB * (PR - 1) + 8)
            combine(PR - 1, s)

    @block.scalar
    def _(act):
        def x_hi(Tn, c, m):
            act.wait_ge(gath_ps, 4 * Tn + 2 * m + 1)
            A.activation(xg[c][0][:, m, :], XP[:], ACT.Copy).then_inc(xh_done, 1)

        def turned(pp, s):
            act.wait_ge(oht_ps, 8 * pp + s + 1)
            A.activation(ohT[s % 2][:], TP16.rearrange("p (x t) -> p x t", x=2), ACT.Copy).then_inc(oht_done, 1)

        def hidden_hi(U, ft):
            act.wait_ge(hf_done, 4 * U + ft + 1)
            A.activation(hp[0][:, ft, :], hf[ft % 2][:], ACT.Copy).then_inc(hh_done, 1)

        def unit(pr, par, e2, c, first, last):
            U = 4 * pr + 2 * e2 + c
            for ft in range(FT):
                act.wait_ge(g_ps, 4 * U + ft + 1)
                if ft >= 2 or later(U):
                    act.wait_ge(hf_done, 4 * U + ft - 1)
                A.activation(sg[ft % 2][:], GP[ft % 2][:], ACT.Silu).then_inc(silu_done, 1)
                if ft:
                    hidden_hi(U, ft - 1)
                if ft % 2 == 0 and not (last and e2 and c):
                    x_hi(U + 1, 1 - c, ft // 2)
                if e2 == 0 and not first and 4 * c + ft + 1 < 8:
                    turned(pr - 1, 4 * c + ft + 1)
            hidden_hi(U, FT - 1)
            for st in range(ST):
                if st % 2 == 0:
                    act.wait_ge(y_ps, 2 * U + st // 2 + 1)
                if st == 0:
                    act.wait_ge(ws_done, 4 * (pr + 1))
                for b2 in range(2):
                    r, o = 64 * b2, 64 * e2
                    A.activation(Y[0][o:o + 64, HB * c + 2 * st + b2, :], YP[st // 2][r:r + 64, st % 2, :], ACT.Copy,
                                 scale=ws[par][r:r + 64, e2, (HB // 2) * c + st:(HB // 2) * c + st + 1]).then_inc(y_hi, 1)

        def one(pr, par, first, last):
            if first:
                for m in range(2):
                    x_hi(0, 0, m)
            for e2 in range(2):
                for c in range(2):
                    unit(pr, par, e2, c, first, last)
            turned(pr, 0)
        pairs(act, one)
        for s in range(1, 8):
            turned(PR - 1, s)

    @block.vector
    def _(v):
        def onehot(pr, par):
            w_ = wT[:].rearrange("p t (b e) x -> p t b (e x)", e=E)
            w_ = w_[:, :, :, 6 * pr:6 * pr + 6] if isinstance(pr, int) else w_[:, :, :, bass.ds(6 * pr, 6)]
            V.tensor_copy(wpair[par][:], w_).then_inc(oh_done, 1)
            for tt in range(2):
                p_ = posT[:, tt, :].rearrange("p (b e o) -> p b e o", e=E, o=1)
                p_ = p_[:, :, 2 * pr:2 * pr + 2] if isinstance(pr, int) else p_[:, :, bass.ds(2 * pr, 2)]
                V.tensor_tensor(OH[par][:, tt], iota[:].rearrange("p (b e s) -> p b e s", b=1, e=1).broadcast_to([P, B, 2, CAP]),
                                p_.broadcast_to([P, B, 2, CAP]), ALU.is_equal).then_inc(oh_done, 1)

        def slot_weights(pr, par):
            v.wait_ge(ws_ps, pr + 1)
            if later(pr - 1):
                v.wait_ge(y_hi, 32 * (pr - 1))
                v.wait_ge(y_lo, 32 * (pr - 1))
            for e2 in range(2):
                src = TP[64 * e2:64 * e2 + 64, 256:256 + 6 * B].rearrange("p (b two e x) -> p two e b x", two=2, e=2, x=3)
                for b2 in range(2):
                    V.tensor_reduce(ws[par][64 * b2:64 * b2 + 64, e2, :], src[:, b2, e2], AX.X, ALU.add).then_inc(ws_done, 1)

        def x_lo(Tn, c, m):
            v.wait_ge(gath_ps, 4 * Tn + 2 * m + 2)
            V.tensor_scalar(xg[c][1][:, m, :], XP[:], 1.0 / 2048, None, ALU.mult).then_inc(xl_done, 1)

        def hidden_lo(U, ft):
            v.wait_ge(hh_done, 4 * U + ft + 1)
            V.tensor_tensor(hp[1][:, ft, :], hf[ft % 2][:], hp[0][:, ft, :].bitcast(F32), ALU.subtract).then_inc(hl_done, 1)

        def add(pp, s):
            for x in range(2):
                b = 2 * s + x
                v.wait_ge(comb_ps, 2 * HB * pp + b + 1)
                V.tensor_tensor(hacc[:, 2 * b:2 * b + 2, :], YP[x][:], hacc[:, 2 * b:2 * b + 2, :], ALU.add).then_inc(comb_add, 1)

        def unit(pr, par, e2, c, first, last):
            U = 4 * pr + 2 * e2 + c
            for ft in range(FT):
                if ft and e2 == 0 and not first:
                    add(pr - 1, 4 * c + ft)
                v.wait_ge(silu_done, 4 * U + ft + 1)
                v.wait_ge(v_ps, 4 * U + ft + 1)
                if ft >= 2:
                    v.wait_ge(hh_done, 4 * U + ft - 1)
                if ft >= 2 or later(U):
                    v.wait_ge(hl_done, 4 * U + ft - 1)
                V.tensor_tensor(hf[ft % 2][:], sg[ft % 2][:], VP[ft % 2][:], ALU.mult).then_inc(hf_done, 1)
                if ft:
                    hidden_lo(U, ft - 1)
                if ft == 2 and e2 and c and not last:
                    slot_weights(pr + 1, 1 - par)
                if ft % 2 and not (last and e2 and c):
                    x_lo(U + 1, 1 - c, ft // 2)
                if ft == 0 and e2 == 0 and not first:
                    add(pr - 1, 4 * c)
            hidden_lo(U, FT - 1)
            if e2 == 1 and c == 0 and not last:
                onehot(pr + 1, 1 - par)
            for st in range(ST):
                for b2 in range(2):
                    r, o = 64 * b2, 64 * e2
                    b = HB * c + 2 * st + b2
                    if st % 2 == 0 and b2 == 0:
                        v.wait_ge(y_hi, 8 * U + 2 * st + 4)
                    V.scalar_tensor_tensor(Y[1][o:o + 64, b, :], YP[st // 2][r:r + 64, st % 2, :],
                                           ws[par][r:r + 64, e2, (HB // 2) * c + st:(HB // 2) * c + st + 1],
                                           Y[0][o:o + 64, b, :].bitcast(F32), ALU.mult, ALU.subtract).then_inc(y_lo, 1)

        def one(pr, par, first, last):
            if first:
                onehot(0, 0)
                for m in range(2):
                    x_lo(0, 0, m)
                slot_weights(0, 0)
            for e2 in range(2):
                for c in range(2):
                    unit(pr, par, e2, c, first, last)
        pairs(v, one)
        for s in range(8):
            add(PR - 1, s)


_INS = ["x", "L0_tok_Wa", "L0_tok_ba", "L0_tok_Wd1", "L0_tok_bd1", "L0_tok_Wd2", "L0_tok_bd2", "L0_tok_Wd3", "L0_tok_bd3",
        "L0_attn_Wq", "L0_attn_bq", "L0_attn_Wk", "L0_attn_bk", "L0_attn_Wv", "L0_attn_bv", "L0_ffn_router_w1",
        "L0_ffn_router_w2", "L0_ffn_w1", "L0_ffn_w2", "L0_ffn_w3"]


def kernel(**inputs):
    import numpy as _np
    import concourse.bacc as _bacc
    from concourse.bass_utils import run_bass_kernel_spmd as _run

    nc = _bacc.Bacc("TRN2", target_bir_lowering=False, num_devices=1, dynamic_dma_scratch_size=1024)
    arrays, args = {}, []
    for name in _INS:
        a = _np.ascontiguousarray(inputs[name])
        arrays[f"in_{name}"] = a
        args.append(nc.dram_tensor(f"in_{name}", a.shape, mybir.dt.from_np(a.dtype), kind="ExternalInput").ap())
    shape = inputs["x"].shape[:3]
    args.append(nc.dram_tensor("out_0", shape, F32, kind="ExternalOutput").ap())
    build_program(nc, *args)
    r = _run(nc, [arrays], core_ids=[0])
    return r.results[0]["out_0"]
```
